# Optimizing a Trainium2 kernel written in Bass

```python
import numpy as np
import jax
import jax.numpy as jnp

def _softmax(x, axis=-1):
    return jax.nn.softmax(x, axis=axis)

def _gelu(x):
    return jax.nn.gelu(x, approximate=True)

def _silu(x):
    return jax.nn.silu(x)

def _sigmoid(x):
    return jax.nn.sigmoid(x)

def _layernorm(x, axis=-1, eps=1e-05):
    m = jnp.mean(x, axis=axis, keepdims=True)
    v = jnp.var(x, axis=axis, keepdims=True)
    return (x - m) / jnp.sqrt(v + eps)

def _scatter_add(tgt, idx, src, axis=0):
    return tgt.at[idx].add(src)

def _segment_sum(src, seg, n):
    return jax.ops.segment_sum(src, seg, n)
kernel_name = 'mk_vit_tower_d1_tok_img256_r4_cbd37e'

def setup_inputs(seed: int=0):
    np.random.seed(seed)
    _w = jnp.asarray

    def _rec_inputs():
        import jax
        import jax.numpy as jnp
        _rk = jax.random.key(seed)
        x = -0.000125008 + 0.999885 * jax.random.normal(jax.random.fold_in(_rk, 1), (64, 64, 128, 128), jnp.float32)
        return x
    x = _rec_inputs()

    def _L0_tok_setup():
        import jax, jax.numpy as jnp
        import numpy as np
        D_MODEL = 64
        NHEAD = 8
        DS = 4
        OFFSET_SCALE = 4.0

        def bilinear_sample(fm, pts):
            B, C, H, W = fm.shape
            x = (pts[..., 0] + 1.0) * 0.5 * (W - 1)
            y = (pts[..., 1] + 1.0) * 0.5 * (H - 1)
            x0 = jnp.clip(jnp.floor(x), 0.0, W - 2)
            y0 = jnp.clip(jnp.floor(y), 0.0, H - 2)
            wx = jnp.clip(x - x0, 0.0, 1.0)
            wy = jnp.clip(y - y0, 0.0, 1.0)
            x0i = x0.astype(jnp.int32)
            y0i = y0.astype(jnp.int32)
            fm2 = fm.reshape(B, C, H * W)
            N, P = (pts.shape[1], pts.shape[2])

            def gather(yi, xi):
                idx = (yi * W + xi).reshape(B, N * P)
                g = jnp.take_along_axis(fm2, idx[:, None, :], axis=2)
                return g.reshape(B, C, N, P)
            v00 = gather(y0i, x0i)
            v01 = gather(y0i, x0i + 1)
            v10 = gather(y0i + 1, x0i)
            v11 = gather(y0i + 1, x0i + 1)
            wx_ = wx[:, None]
            wy_ = wy[:, None]
            out = v00 * (1 - wx_) * (1 - wy_) + v01 * wx_ * (1 - wy_) + v10 * (1 - wx_) * wy_ + v11 * wx_ * wy_
            return jnp.moveaxis(out, 1, -1)

        def layer_norm(x, g, b, eps=1e-05):
            mu = jnp.mean(x, axis=-1, keepdims=True)
            var = jnp.var(x, axis=-1, keepdims=True)
            return (x - mu) * jax.lax.rsqrt(var + eps) * g + b

        def reference_points(B, H, W):
            yc = jnp.linspace(-1.0, 1.0, H // DS)
            xc = jnp.linspace(-1.0, 1.0, W // DS)
            yg, xg = jnp.meshgrid(yc, xc, indexing='ij')
            ref = jnp.stack([xg.reshape(-1), yg.reshape(-1)], axis=-1)
            return jnp.broadcast_to(ref[None], (B,) + ref.shape)
        key = jax.random.key(seed)
        ks = jax.random.split(key, 6)
        B, C, H, W = (8, D_MODEL, 128, 128)
        s = 0.05
        return {'feature_map': jax.random.normal(ks[0], (B, C, H, W), jnp.float32), 'W_q': jax.random.normal(ks[1], (C, C), jnp.float32) * s, 'W_k': jax.random.normal(ks[2], (C, C), jnp.float32) * s, 'W_v': jax.random.normal(ks[3], (C, C), jnp.float32) * s, 'W_o1': jax.random.normal(ks[4], (C, C // DS), jnp.float32) * s, 'b_o1': jnp.zeros((C // DS,), jnp.float32), 'ln_g': jnp.ones((C // DS,), jnp.float32), 'ln_b': jnp.zeros((C // DS,), jnp.float32), 'W_o2': jax.random.normal(ks[5], (C // DS, NHEAD * 2), jnp.float32) * s, 'b_o2': jnp.zeros((NHEAD * 2,), jnp.float32)}
    _L0_tok_all = _L0_tok_setup()
    _L0_tok_in = {k: v for k, v in _L0_tok_all.items() if k in ('W_q', 'W_k', 'W_v', 'W_o1', 'b_o1', 'ln_g', 'ln_b', 'W_o2', 'b_o2')}
    del _L0_tok_all

    def _L0_attn_setup():
        import jax, jax.numpy as jnp
        import numpy as np
        EMB, HEADS, DEPTH, SEQ, BATCH = (64, 8, 4, 2048, 4)
        DH = EMB // HEADS
        FF = 4 * EMB
        EPS = 1e-05

        def _layernorm(x, g, b):
            mu = x.mean(-1, keepdims=True)
            var = ((x - mu) ** 2).mean(-1, keepdims=True)
            return (x - mu) * jax.lax.rsqrt(var + EPS) * g + b

        def _linear_attn(x, Wq, Wk, Wv, Wo, bo):
            b, n, dm = x.shape
            split = lambda t: t.reshape(b, n, HEADS, DH).transpose(0, 2, 1, 3)
            scale = DH ** (-0.25)
            q = jax.nn.softmax(split(x @ Wq) * scale, axis=-1)
            k = jax.nn.softmax(split(x @ Wk) * scale, axis=-2)
            v = split(x @ Wv)
            context = jnp.einsum('bhnd,bhne->bhde', k, v)
            out = jnp.einsum('bhnd,bhde->bhne', q, context)
            out = out.transpose(0, 2, 1, 3).reshape(b, n, dm)
            return out @ Wo + bo

        def _forward(x, Wq, Wk, Wv, Wo, bo, ln1_g, ln1_b, W1, b1, W2, b2, ln2_g, ln2_b):
            for i in range(DEPTH):
                h = _layernorm(x, ln1_g[i], ln1_b[i])
                x = x + _linear_attn(h, Wq[i], Wk[i], Wv[i], Wo[i], bo[i])
                h = _layernorm(x, ln2_g[i], ln2_b[i])
                x = x + (jax.nn.gelu(h @ W1[i] + b1[i], approximate=False) @ W2[i] + b2[i])
            return x
        key = jax.random.key(seed)
        ks = jax.random.split(key, 8)
        w = lambda k, shape: jax.random.normal(k, shape, dtype=jnp.float32) * 0.02
        D = DEPTH
        return {'x': jax.random.normal(ks[0], (BATCH, SEQ, EMB), dtype=jnp.float32), 'Wq': w(ks[1], (D, EMB, EMB)), 'Wk': w(ks[2], (D, EMB, EMB)), 'Wv': w(ks[3], (D, EMB, EMB)), 'Wo': w(ks[4], (D, EMB, EMB)), 'bo': jnp.zeros((D, EMB), jnp.float32), 'ln1_g': jnp.ones((D, EMB), jnp.float32), 'ln1_b': jnp.zeros((D, EMB), jnp.float32), 'W1': w(ks[5], (D, EMB, FF)), 'b1': jnp.zeros((D, FF), jnp.float32), 'W2': w(ks[6], (D, FF, EMB)), 'b2': jnp.zeros((D, EMB), jnp.float32), 'ln2_g': jnp.ones((D, EMB), jnp.float32), 'ln2_b': jnp.zeros((D, EMB), jnp.float32)}
    _L0_attn_all = _L0_attn_setup()
    _L0_attn_in = {k: v for k, v in _L0_attn_all.items() if k in ('Wq', 'Wk', 'Wv', 'Wo', 'bo', 'ln1_g', 'ln1_b', 'W1', 'b1', 'W2', 'b2', 'ln2_g', 'ln2_b')}
    del _L0_attn_all

    def _L0_ffn_setup():
        import jax, jax.numpy as jnp
        import numpy as np
        E, D, H, TOP_K = (6, 64, 64, 2)
        ROUTER_H = D // 2
        key = jax.random.key(seed)
        ks = jax.random.split(key, 12)
        s = 1.0 / np.sqrt(D)
        sh = 1.0 / np.sqrt(H)
        sr = 1.0 / np.sqrt(ROUTER_H)
        return {'features': jax.random.normal(ks[0], (8, 1024, D), dtype=jnp.float32), 'router_w1': jax.random.uniform(ks[1], (D, ROUTER_H), jnp.float32, -s, s), 'router_b1': jnp.zeros((ROUTER_H,), jnp.float32), 'router_w2': jax.random.uniform(ks[2], (ROUTER_H, E), jnp.float32, -sr, sr), 'router_b2': jnp.zeros((E,), jnp.float32), 'expert_w1': jax.random.uniform(ks[3], (E, D, H), jnp.float32, -s, s), 'expert_b1': jnp.zeros((E, H), jnp.float32), 'expert_w2': jax.random.uniform(ks[4], (E, H, H), jnp.float32, -sh, sh), 'expert_b2': jnp.zeros((E, H), jnp.float32), 'expert_w3': jax.random.uniform(ks[5], (E, H, D), jnp.float32, -sh, sh), 'expert_b3': jnp.zeros((E, D), jnp.float32)}
    _L0_ffn_all = _L0_ffn_setup()
    _L0_ffn_in = {k: v for k, v in _L0_ffn_all.items() if k in ('router_w1', 'router_b1', 'router_w2', 'router_b2', 'expert_w1', 'expert_b1', 'expert_w2', 'expert_b2', 'expert_w3', 'expert_b3')}
    del _L0_ffn_all
    return {'x': x, 'L0_tok_W_q': _L0_tok_in['W_q'], 'L0_tok_W_k': _L0_tok_in['W_k'], 'L0_tok_W_v': _L0_tok_in['W_v'], 'L0_tok_W_o1': _L0_tok_in['W_o1'], 'L0_tok_b_o1': _L0_tok_in['b_o1'], 'L0_tok_ln_g': _L0_tok_in['ln_g'], 'L0_tok_ln_b': _L0_tok_in['ln_b'], 'L0_tok_W_o2': _L0_tok_in['W_o2'], 'L0_tok_b_o2': _L0_tok_in['b_o2'], 'L0_attn_Wq': _L0_attn_in['Wq'], 'L0_attn_Wk': _L0_attn_in['Wk'], 'L0_attn_Wv': _L0_attn_in['Wv'], 'L0_attn_Wo': _L0_attn_in['Wo'], 'L0_attn_bo': _L0_attn_in['bo'], 'L0_attn_ln1_g': _L0_attn_in['ln1_g'], 'L0_attn_ln1_b': _L0_attn_in['ln1_b'], 'L0_attn_W1': _L0_attn_in['W1'], 'L0_attn_b1': _L0_attn_in['b1'], 'L0_attn_W2': _L0_attn_in['W2'], 'L0_attn_b2': _L0_attn_in['b2'], 'L0_attn_ln2_g': _L0_attn_in['ln2_g'], 'L0_attn_ln2_b': _L0_attn_in['ln2_b'], 'L0_ffn_router_w1': _L0_ffn_in['router_w1'], 'L0_ffn_router_b1': _L0_ffn_in['router_b1'], 'L0_ffn_router_w2': _L0_ffn_in['router_w2'], 'L0_ffn_router_b2': _L0_ffn_in['router_b2'], 'L0_ffn_expert_w1': _L0_ffn_in['expert_w1'], 'L0_ffn_expert_b1': _L0_ffn_in['expert_b1'], 'L0_ffn_expert_w2': _L0_ffn_in['expert_w2'], 'L0_ffn_expert_b2': _L0_ffn_in['expert_b2'], 'L0_ffn_expert_w3': _L0_ffn_in['expert_w3'], 'L0_ffn_expert_b3': _L0_ffn_in['expert_b3']}

def reference(x, L0_tok_W_q, L0_tok_W_k, L0_tok_W_v, L0_tok_W_o1, L0_tok_b_o1, L0_tok_ln_g, L0_tok_ln_b, L0_tok_W_o2, L0_tok_b_o2, L0_attn_Wq, L0_attn_Wk, L0_attn_Wv, L0_attn_Wo, L0_attn_bo, L0_attn_ln1_g, L0_attn_ln1_b, L0_attn_W1, L0_attn_b1, L0_attn_W2, L0_attn_b2, L0_attn_ln2_g, L0_attn_ln2_b, L0_ffn_router_w1, L0_ffn_router_b1, L0_ffn_router_w2, L0_ffn_router_b2, L0_ffn_expert_w1, L0_ffn_expert_b1, L0_ffn_expert_w2, L0_ffn_expert_b2, L0_ffn_expert_w3, L0_ffn_expert_b3):
    import jax
    import jax.numpy as jnp

    def _L0_tok_ref(feature_map, W_q, W_k, W_v, W_o1, b_o1, ln_g, ln_b, W_o2, b_o2):
        import jax, jax.numpy as jnp
        import numpy as np
        D_MODEL = 64
        NHEAD = 8
        DS = 4
        OFFSET_SCALE = 4.0

        def bilinear_sample(fm, pts):
            B, C, H, W = fm.shape
            x = (pts[..., 0] + 1.0) * 0.5 * (W - 1)
            y = (pts[..., 1] + 1.0) * 0.5 * (H - 1)
            x0 = jnp.clip(jnp.floor(x), 0.0, W - 2)
            y0 = jnp.clip(jnp.floor(y), 0.0, H - 2)
            wx = jnp.clip(x - x0, 0.0, 1.0)
            wy = jnp.clip(y - y0, 0.0, 1.0)
            x0i = x0.astype(jnp.int32)
            y0i = y0.astype(jnp.int32)
            fm2 = fm.reshape(B, C, H * W)
            N, P = (pts.shape[1], pts.shape[2])

            def gather(yi, xi):
                idx = (yi * W + xi).reshape(B, N * P)
                g = jnp.take_along_axis(fm2, idx[:, None, :], axis=2)
                return g.reshape(B, C, N, P)
            v00 = gather(y0i, x0i)
            v01 = gather(y0i, x0i + 1)
            v10 = gather(y0i + 1, x0i)
            v11 = gather(y0i + 1, x0i + 1)
            wx_ = wx[:, None]
            wy_ = wy[:, None]
            out = v00 * (1 - wx_) * (1 - wy_) + v01 * wx_ * (1 - wy_) + v10 * (1 - wx_) * wy_ + v11 * wx_ * wy_
            return jnp.moveaxis(out, 1, -1)

        def layer_norm(x, g, b, eps=1e-05):
            mu = jnp.mean(x, axis=-1, keepdims=True)
            var = jnp.var(x, axis=-1, keepdims=True)
            return (x - mu) * jax.lax.rsqrt(var + eps) * g + b

        def reference_points(B, H, W):
            yc = jnp.linspace(-1.0, 1.0, H // DS)
            xc = jnp.linspace(-1.0, 1.0, W // DS)
            yg, xg = jnp.meshgrid(yc, xc, indexing='ij')
            ref = jnp.stack([xg.reshape(-1), yg.reshape(-1)], axis=-1)
            return jnp.broadcast_to(ref[None], (B,) + ref.shape)
        B, C, H, W = feature_map.shape
        dh = C // NHEAD
        ref = reference_points(B, H, W)
        Nq = ref.shape[1]
        q_feat = bilinear_sample(feature_map, ref[:, :, None, :])[:, :, 0]
        queries = q_feat @ W_q.T
        h = jax.nn.gelu(layer_norm(q_feat @ W_o1 + b_o1, ln_g, ln_b))
        off = (h @ W_o2 + b_o2).reshape(B, Nq, NHEAD, 2) * OFFSET_SCALE
        scale = jnp.array([2.0 / (W - 1), 2.0 / (H - 1)], jnp.float32)
        sampling_points = ref[:, :, None, :] + off * scale
        sampled = bilinear_sample(feature_map, sampling_points)
        keys = jnp.einsum('bnpc,dc->bnpd', sampled, W_k)
        values = jnp.einsum('bnpc,dc->bnpd', sampled, W_v)
        q = queries.reshape(B, Nq, NHEAD, dh)
        k = keys.reshape(B, Nq, NHEAD, NHEAD, dh)
        v = values.reshape(B, Nq, NHEAD, NHEAD, dh)
        scores = jnp.einsum('bnhd,bnphd->bnhp', q, k) / jnp.sqrt(jnp.float32(dh))
        attn = jax.nn.softmax(scores, axis=-1)
        out = jnp.einsum('bnhp,bnphd->bnhd', attn, v).reshape(B, Nq, C)
        return out

    def _L0_attn_ref(x, Wq, Wk, Wv, Wo, bo, ln1_g, ln1_b, W1, b1, W2, b2, ln2_g, ln2_b):
        import jax, jax.numpy as jnp
        import numpy as np
        EMB, HEADS, DEPTH, SEQ, BATCH = (64, 8, 4, 2048, 4)
        DH = EMB // HEADS
        FF = 4 * EMB
        EPS = 1e-05

        def _layernorm(x, g, b):
            mu = x.mean(-1, keepdims=True)
            var = ((x - mu) ** 2).mean(-1, keepdims=True)
            return (x - mu) * jax.lax.rsqrt(var + EPS) * g + b

        def _linear_attn(x, Wq, Wk, Wv, Wo, bo):
            b, n, dm = x.shape
            split = lambda t: t.reshape(b, n, HEADS, DH).transpose(0, 2, 1, 3)
            scale = DH ** (-0.25)
            q = jax.nn.softmax(split(x @ Wq) * scale, axis=-1)
            k = jax.nn.softmax(split(x @ Wk) * scale, axis=-2)
            v = split(x @ Wv)
            context = jnp.einsum('bhnd,bhne->bhde', k, v)
            out = jnp.einsum('bhnd,bhde->bhne', q, context)
            out = out.transpose(0, 2, 1, 3).reshape(b, n, dm)
            return out @ Wo + bo

        def _forward(x, Wq, Wk, Wv, Wo, bo, ln1_g, ln1_b, W1, b1, W2, b2, ln2_g, ln2_b):
            for i in range(DEPTH):
                h = _layernorm(x, ln1_g[i], ln1_b[i])
                x = x + _linear_attn(h, Wq[i], Wk[i], Wv[i], Wo[i], bo[i])
                h = _layernorm(x, ln2_g[i], ln2_b[i])
                x = x + (jax.nn.gelu(h @ W1[i] + b1[i], approximate=False) @ W2[i] + b2[i])
            return x
        return _forward(x, Wq, Wk, Wv, Wo, bo, ln1_g, ln1_b, W1, b1, W2, b2, ln2_g, ln2_b)

    def _L0_ffn_ref(features, router_w1, router_b1, router_w2, router_b2, expert_w1, expert_b1, expert_w2, expert_b2, expert_w3, expert_b3):
        import jax, jax.numpy as jnp
        import numpy as np
        E, D, H, TOP_K = (6, 64, 64, 2)
        ROUTER_H = D // 2
        rh = jax.nn.relu(features @ router_w1 + router_b1)
        expert_logits = jax.nn.softmax(rh @ router_w2 + router_b2, axis=-1)
        top_w, top_i = jax.lax.top_k(expert_logits, TOP_K)
        routing_weights = jax.nn.softmax(top_w, axis=-1)
        h1 = jax.nn.relu(jnp.einsum('bsd,edh->bseh', features, expert_w1) + expert_b1)
        h2 = jax.nn.relu(jnp.einsum('bseh,ehf->bsef', h1, expert_w2) + expert_b2)
        expert_out = jnp.einsum('bsef,efo->bseo', h2, expert_w3) + expert_b3
        sel = jnp.take_along_axis(expert_out, top_i[:, :, :, None], axis=2)
        combined = jnp.sum(sel * routing_weights[..., None], axis=2)
        return combined
    h = _L0_tok_ref(x, L0_tok_W_q, L0_tok_W_k, L0_tok_W_v, L0_tok_W_o1, L0_tok_b_o1, L0_tok_ln_g, L0_tok_ln_b, L0_tok_W_o2, L0_tok_b_o2)
    h = h + _L0_attn_ref(_layernorm(h, axis=-1), L0_attn_Wq, L0_attn_Wk, L0_attn_Wv, L0_attn_Wo, L0_attn_bo, L0_attn_ln1_g, L0_attn_ln1_b, L0_attn_W1, L0_attn_b1, L0_attn_W2, L0_attn_b2, L0_attn_ln2_g, L0_attn_ln2_b)
    h = h + _L0_ffn_ref(_layernorm(h, axis=-1), L0_ffn_router_w1, L0_ffn_router_b1, L0_ffn_router_w2, L0_ffn_router_b2, L0_ffn_expert_w1, L0_ffn_expert_b1, L0_ffn_expert_w2, L0_ffn_expert_b2, L0_ffn_expert_w3, L0_ffn_expert_b3)
    return h

_drawn_inputs = setup_inputs


def setup_inputs(seed=0):
    import zlib

    import numpy as np

    out = dict(_drawn_inputs(seed))
    spreads = {'L0_tok_b_o1': (0.0, 0.1),
     'L0_tok_ln_g': (1.0, 0.2),
     'L0_tok_ln_b': (0.0, 0.1),
     'L0_tok_b_o2': (0.0, 0.1),
     'L0_attn_bo': (0.0, 0.1),
     'L0_attn_ln1_g': (1.0, 0.6),
     'L0_attn_ln1_b': (0.0, 0.8),
     'L0_attn_b1': (0.0, 0.1),
     'L0_attn_b2': (0.0, 0.1),
     'L0_attn_ln2_g': (1.0, 0.6),
     'L0_attn_ln2_b': (0.0, 0.8),
     'L0_ffn_router_b1': (0.0, 0.1),
     'L0_ffn_router_b2': (0.0, 0.1),
     'L0_ffn_expert_b1': (0.0, 0.8),
     'L0_ffn_expert_b2': (0.0, 0.341),
     'L0_ffn_expert_b3': (0.0, 0.1)}
    factors = {'L0_attn_Wq': 8.0, 'L0_attn_Wk': 8.0, 'L0_attn_Wv': 4.248, 'L0_attn_Wo': 5.181}
    for name, (base, spread) in spreads.items():
        noise = np.random.default_rng([zlib.crc32(name.encode()), seed]).standard_normal(out[name].shape)
        drawn = base * np.exp(spread * noise) if base else spread * noise
        out[name] = jnp.asarray(drawn.astype(out[name].dtype))
    for name, factor in factors.items():
        out[name] = (out[name] * factor).astype(out[name].dtype)
    return out
```

```python
import numpy as np
import concourse.bass as bass
from concourse import mybir
from contextlib import ExitStack

F32 = mybir.dt.float32
I32 = mybir.dt.int32
ALU = mybir.AluOpType
ACT = mybir.ActivationFunctionType
AX = mybir.AxisListType

C = 64
HW = 128
NPIX = HW * HW
GRID = 32
NQ = GRID * GRID
NH = 8
DH = C // NH
OH = 16
P = 128
TILES = NQ // P
GROUPS = 2 * TILES
CH = 16
NCH = HW // CH
RUNS = []
for q in range(GRID):
    px = min((HW - 1) * q // (GRID - 1), HW - 2)
    if RUNS and px == RUNS[-1][2] + 4 * RUNS[-1][1]:
        RUNS[-1][1] += 1
    else:
        RUNS.append([q, 1, px])
LN_EPS = 1e-5
GELU_2C = 2 * 0.7978845608028654
A_DVE = 52
B_DVE = GROUPS * 12


def wait_if(eng, sem, value):
    if not isinstance(value, int) or value > 0:
        eng.wait_ge(sem, value)


def hold(eng, sem, value, turns):
    if not isinstance(value, int) or value > 0:
        eng.wait_ge(sem, value)
        eng.sem_inc(turns, 1)


class Steps:

    def __init__(self, eng, sem, per_round, round_):
        self.eng, self.sem, self.base, self.n, self.per = eng, sem, round_ * per_round, 0, per_round

    def done(self, ins):
        ins.then_inc(self.sem, 1)
        self.n += 1

    def wait(self):
        self.eng.wait_ge(self.sem, self.base + self.n)

    def link(self, ins):
        self.done(ins)
        self.wait()

    def close(self):
        assert self.n == self.per, (self.n, self.per)


def tok_stage(nc, PAIRS, x, scr, hd, wqT, wkT, wvT, wo1, bo1, lng, lnb, wo2, bo2, c_ident, c_ref, c_wy, c_base):
    x_v = x.rearrange("b c h w -> (b c) (h w)")
    with ExitStack() as ctx:
        sb = lambda name, shape, dt=F32: ctx.enter_context(nc.sbuf_tensor(name, shape, dt))
        pb = lambda name, shape: ctx.enter_context(nc.psum_tensor(name, shape, F32))
        sem = lambda name: ctx.enter_context(nc.semaphore(name))

        X = sb("X", [P, HW, HW])
        T = sb("T", [P, 2, 2, CH + 1, C])
        V = sb("V", [P, GRID, HW])
        qf = sb("qf", [P, GRID, GRID])
        QO = sb("QO", [P, 2, TILES, 160])
        Z = sb("Z", [P, 256])
        Z2 = sb("Z2", [P, 256])
        Z3 = sb("Z3", [P, 256])
        st16 = sb("st16", [P, 2, GROUPS])
        rstd = sb("rstd", [P, GROUPS])
        HT = sb("HT", [P, 2, P])
        PI = sb("PI", [P, 256], I32)
        PF = sb("PF", [P, 256])
        FG = sb("FG", [P, 256, 2])
        W = sb("W", [P, 2, GROUPS * NH, 4])
        idx = sb("idx", [P, 2, GROUPS * NH], I32)
        idf = sb("idf", [P, GROUPS * NH])
        G = sb("G", [P, 2, NH, 4 * C])
        S = sb("S", [P, 2, NH * C])
        ST = sb("ST", [P, 4, P])
        PR = sb("PR", [P, NH * C])
        PV = sb("PV", [P, NH * C])
        sc = sb("sc", [P, 2, 64])
        ex = sb("ex", [P, 2, 64])
        mx = sb("mx", [P, NH])
        den = sb("den", [P, NH])
        rden = sb("rden", [P, NH])
        o8 = sb("o8", [P, C])
        HO = sb("HO", [P, 2, GROUPS, C])
        ident = sb("ident", [P, P])
        ref = sb("ref", [P, 256])
        wy = sb("wy", [P, GRID])
        base = sb("base", [P, GROUPS * NH])
        WQO = sb("WQO", [P, 160])
        WKV = sb("WKV", [P, 256])
        WO2 = sb("WO2", [P, P])
        bo1s = sb("bo1s", [P, 2, OH])
        lngs = sb("lngs", [P, OH])
        lnbs = sb("lnbs", [P, OH])
        bo2s = sb("bo2s", [P, 2 * NH])

        tp = [pb(f"tp{n}", [P, 4, P]) for n in range(2)]
        offp = pb("offp", [P, 512])
        stp = pb("stp", [P, 4, P])
        kvp = [pb(f"kvp{n}", [P, 2, 512]) for n in range(2)]

        weights_zeroed = sem("weights_zeroed")
        weights_loaded = sem("weights_loaded")
        x_loaded = [sem(f"x_loaded{k}") for k in range(NCH)]
        rows_interpolated = sem("rows_interpolated")
        rows_transposed = sem("rows_transposed")
        rows_copied = sem("rows_copied")
        scratch_stored = [sem(f"scratch_stored{n}") for n in range(2)]
        scratch_ready = sem("scratch_ready")
        qf_ready = sem("qf_ready")
        qo_projected = sem("qo_projected")
        qo_copied = sem("qo_copied")
        var_ready = sem("var_ready")
        ln_taken = sem("ln_taken")
        rstd_ready = sem("rstd_ready")
        gelu_arg_ready = sem("gelu_arg_ready")
        gelu_exp_ready = sem("gelu_exp_ready")
        hidden_ready = sem("hidden_ready")
        hidden_transposed = sem("hidden_transposed")
        hidden_copied = sem("hidden_copied")
        offsets_projected = sem("offsets_projected")
        points_ready = sem("points_ready")
        patches_gathered = [sem(f"patches_gathered{n}") for n in range(2)]
        patches_used = sem("patches_used")
        sampled_ready = sem("sampled_ready")
        sampled_transposed = sem("sampled_transposed")
        sampled_copied = sem("sampled_copied")
        kv_ready = sem("kv_ready")
        scores_ready = sem("scores_ready")
        probs_ready = sem("probs_ready")
        attended = sem("attended")
        h_stored = sem("h_stored")
        sp_turns = sem("sp_turns")
        pool_turns = sem("pool_turns")
        dve_a = sem("dve_a")
        dve_b = sem("dve_b")
        NW = 19

        block = ctx.enter_context(nc.Block())

        @block.sync
        def _(sp):
            sp.wait_ge(weights_zeroed, 3)
            last = []
            for m in range(2):
                r = slice(C * m, C * m + C)
                last.append(sp.dma_start(WQO[r, OH * m:OH * m + OH], wo1))
                last.append(sp.dma_start(WQO[r, 32 + C * m:32 + C * m + C], wqT))
                last.append(sp.dma_start(WKV[r, P * m:P * m + C], wkT))
                last.append(sp.dma_start(WKV[r, P * m + C:P * m + P], wvT))
                last.append(sp.dma_start(bo1s[:, m, :], bo1.partition_broadcast(P)))
            for g in range(8):
                last.append(sp.dma_start(WO2[OH * g:OH * g + OH, OH * g:OH * g + OH], wo2))
            for dst, src in ((lngs, lng), (lnbs, lnb), (bo2s, bo2)):
                last.append(sp.dma_start(dst[:, :], src.partition_broadcast(P)))
            for dst, src in ((ident, c_ident), (ref, c_ref), (wy, c_wy), (base, c_base)):
                last.append(sp.dma_start(dst[:, :], src))
            for d in last:
                d.then_inc(weights_loaded, 16)

            def load(i):
                hold(sp, rows_interpolated, i, sp_turns)
                hold(sp, rows_transposed, i * 4 * NCH, sp_turns)
                for k in range(NCH):
                    sp.dma_start(X[:, CH * k:CH * k + CH, :], x_v[bass.ts(i, P), CH * HW * k:CH * HW * (k + 1)]
                                 .rearrange("p (h w) -> p h w", w=HW)).then_inc(x_loaded[k], 16)

            def store(i, b2):
                hold(sp, patches_used, (i - 1) * GROUPS, sp_turns)
                for k in range(NCH):
                    b = k % 2
                    hold(sp, rows_copied, i * 4 * NCH + 4 * k + 4, sp_turns)
                    first = 1 if k == 0 else 0
                    n = CH - first
                    for m in range(2):
                        src = T[:, b, m, first:first + n, :]
                        src = bass.AP(src.tensor, src.offset, [src.ap[0], [C, n], [1, 2 * C]])
                        row = CH * k - 1 + first
                        at = scr[b2][(m * (HW - 1) + row) * HW:(m * (HW - 1) + row + n) * HW, :]
                        dst = at.rearrange("(h w) c -> w h c", w=HW)
                        sp.dma_start(dst, src).then_inc(scratch_stored[b], 16)
                for b in range(2):
                    sp.wait_ge(scratch_stored[b], (i + 1) * 2 * 16 * (NCH // 2))
                sp.sem_inc(scratch_ready, 1)

            def store_h(j, b):
                hold(sp, attended, (j + 1) * GROUPS, sp_turns)
                sp.dma_start(hd[bass.ts(j, P), :], HO[:, b, :, :].rearrange("p g c -> p (g c)")).then_inc(h_stored, 16)


            def body(i, b):
                load(i)
                store(i, b)
                if not (isinstance(i, int) and i == 0):
                    store_h(i - 1, 1 - b)
            for i in range(3):
                body(i, i % 2)
            with sp.Fori(1, PAIRS // 2 - 1) as s:
                body(s * 2 + 1, 1)
                body(s * 2 + 2, 0)
            body(PAIRS - 1, 1)
            store_h(PAIRS - 1, 1)
            sp.wait_ge(h_stored, PAIRS * 16)

        @block.gpsimd
        def _(pool):
            nc.gpsimd.memset(WQO[:, :], 0.0).then_inc(weights_zeroed, 1)
            nc.gpsimd.memset(WKV[:, :], 0.0).then_inc(weights_zeroed, 1)
            nc.gpsimd.memset(WO2[:, :], 0.0).then_inc(weights_zeroed, 1)

            def gather(j, b):
                hold(pool, points_ready, j + 1, pool_turns)
                hold(pool, scratch_ready, j + 1, pool_turns)
                for g in range(GROUPS):
                    hold(pool, patches_used, j * GROUPS + g - 1, pool_turns)
                    for p in range(NH):
                        pool.indirect_dma_start(
                            G[:, g % 2, p, :], None, scr[b],
                            bass.IndirectOffsetOnAxis(ap=idx[:, b, g * NH + p:g * NH + p + 1], axis=0),
                        ).then_inc(patches_gathered[g % 2], 16)
            for j in range(3):
                gather(j, j % 2)
            with pool.Fori(1, PAIRS // 2 - 1) as s:
                gather(s * 2 + 1, 1)
                gather(s * 2 + 2, 0)
            gather(PAIRS - 1, 1)

        @block.scalar
        def _(act):
            def copy_rows(i, k, q):
                b = k % 2
                if q == 0 and k == 0:
                    wait_if(act, scratch_stored[b], i * 2 * 16 * (NCH // 2))
                n = 4 * k + q
                act.wait_ge(rows_transposed, i * 4 * NCH + n + 1)
                src = tp[n % 2][:, :, :].rearrange("p r (m c) -> p m r c", m=2)
                if q < 3 or k == NCH - 1:
                    nc.scalar.copy(T[:, b, :, 1 + 4 * q:5 + 4 * q, :], src).then_inc(rows_copied, 1)
                else:
                    nc.scalar.copy(T[:, b, :, 1 + 4 * q:5 + 4 * q, :], src)
                    wait_if(act, scratch_stored[1 - b], i * 2 * 16 * (NCH // 2) + 32 * ((k + 1) // 2))
                    nc.scalar.copy(T[:, 1 - b, :, 0, :], src[:, :, 3, :]).then_inc(rows_copied, 1)

            def offsets_act(i, part):
                if part == 0:
                    act.wait_ge(var_ready, i + 1)
                    nc.scalar.activation(rstd[:, :], st16[:, 1, :], ACT.Ln).then_inc(ln_taken, 1)
                    act.wait_ge(ln_taken, i + 1)
                    nc.scalar.activation(rstd[:, :], rstd[:, :], ACT.Exp, scale=-0.5).then_inc(rstd_ready, 1)
                if part == 1:
                    act.wait_ge(gelu_arg_ready, i + 1)
                    nc.scalar.activation(Z3[:, :], Z3[:, :], ACT.Exp).then_inc(gelu_exp_ready, 1)
                if part == 2:
                    act.wait_ge(hidden_transposed, i + 1)
                    nc.scalar.copy(HT[:, :, :], offp[:, 0:256].rearrange("p (a b) -> p a b", a=2)).then_inc(hidden_copied, 1)

            def copy_sampled(j, g):
                act.wait_ge(sampled_transposed, j * GROUPS + g + 1)
                wait_if(act, kv_ready, j * GROUPS + g)
                nc.scalar.copy(ST[:, :, :], stp[:, :, :]).then_inc(sampled_copied, 1)

            def probs(j, g):
                act.wait_ge(scores_ready, j * GROUPS + g + 1)
                nc.scalar.activation(ex[:, g % 2, :], sc[:, g % 2, :], ACT.Exp, scale=float(DH) ** -0.5).then_inc(probs_ready, 1)

            def body(i, j):
                for g in range(GROUPS + 1):
                    if i is not None and g < GROUPS:
                        for q in range(2):
                            copy_rows(i, g // 2, 2 * (g % 2) + q)
                        if g in (10, 12, 14):
                            offsets_act(i, (g - 10) // 2)
                    if j is not None:
                        if g < GROUPS:
                            copy_sampled(j, g)
                        if g >= 1:
                            probs(j, g - 1)

            act.preload_act_table_set("natural_log_exp_and_others")
            body(0, None)
            body(1, 0)
            body(2, 1)
            with act.Fori(1, PAIRS // 2 - 1) as s:
                body(s * 2 + 1, s * 2)
                body(s * 2 + 2, s * 2 + 1)
            body(PAIRS - 1, PAIRS - 2)
            body(None, PAIRS - 1)

        @block.tensor
        def _(pe):
            pe.wait_ge(weights_loaded, 16 * (10 + 8 + 3 + 4))

            def transpose_rows(i, k, q):
                n = 4 * k + q
                if q == 0:
                    pe.wait_ge(x_loaded[k], (i + 1) * 16)
                wait_if(pe, rows_copied, i * 4 * NCH + n - 1)
                for r in range(4):
                    ins = nc.tensor.transpose(tp[n % 2][:, r, :], X[:, CH * k + 4 * q + r, :], ident[:, :])
                ins.then_inc(rows_transposed, 1)

            def offsets_pe(i, part):
                if part < 3:
                    if part == 0:
                        pe.wait_ge(qf_ready, i + 1)
                        wait_if(pe, dve_a, i * A_DVE)
                    else:
                        pe.wait_ge(qo_copied, i * 3 + part)
                    for t in range(3 * part, min(3 * part + 3, TILES)):
                        ins = nc.tensor.matmul(offp[:, 160 * (t % 3):160 * (t % 3) + 160],
                                               qf[:, 4 * t:4 * t + 4, :].rearrange("p a b -> p (a b)"),
                                               WQO[:, :], start=True, stop=True)
                    ins.then_inc(qo_projected, 1)
                if part == 3:
                    pe.wait_ge(hidden_ready, i + 1)
                    for a in range(2):
                        ins = nc.tensor.transpose(offp[:, P * a:P * a + P], Z[:, P * a:P * a + P], ident[:, :])
                    ins.then_inc(hidden_transposed, 1)
                if part == 4:
                    pe.wait_ge(hidden_copied, i + 1)
                    for a in range(2):
                        ins = nc.tensor.matmul(offp[:, P * a:P * a + P], HT[:, a, :], WO2[:, :], start=True, stop=True)
                    ins.then_inc(offsets_projected, 1)

            def transpose_sampled(j, g):
                pe.wait_ge(sampled_ready, j * GROUPS + g + 1)
                wait_if(pe, sampled_copied, j * GROUPS + g)
                for a in range(4):
                    ins = nc.tensor.transpose(stp[:, a, :], S[:, g % 2, P * a:P * a + P], ident[:, :])
                ins.then_inc(sampled_transposed, 1)

            def project_kv(j, g):
                pe.wait_ge(sampled_copied, j * GROUPS + g + 1)
                wait_if(pe, attended, j * GROUPS + g - 1)
                for a in range(4):
                    ins = nc.tensor.matmul(kvp[g % 2][:, a // 2, 256 * (a % 2):256 * (a % 2) + 256], ST[:, a, :],
                                           WKV[:, :], start=True, stop=True)
                ins.then_inc(kv_ready, 1)

            def body(i, j):
                for g in range(GROUPS + 1):
                    if i is not None and g < GROUPS:
                        for q in range(2):
                            transpose_rows(i, g // 2, 2 * (g % 2) + q)
                        if g in (6, 7, 8):
                            offsets_pe(i, g - 6)
                        if g in (14, 15):
                            offsets_pe(i, g - 11)
                    if j is not None:
                        if g >= 1:
                            project_kv(j, g - 1)
                        if g < GROUPS:
                            transpose_sampled(j, g)

            body(0, None)
            body(1, 0)
            body(2, 1)
            with pe.Fori(1, PAIRS // 2 - 1) as s:
                body(s * 2 + 1, s * 2)
                body(s * 2 + 2, s * 2 + 1)
            body(PAIRS - 1, PAIRS - 2)
            body(None, PAIRS - 1)

        @block.vector
        def _(dve):
            v = nc.vector
            dve.wait_ge(weights_loaded, 16 * (10 + 8 + 3 + 4))

            def rows(c, n):
                q0, cnt, p0 = RUNS[n]
                upper = X[:, p0:p0 + 4 * (cnt - 1) + 1:4, :]
                lower = X[:, p0 + 1:p0 + 4 * (cnt - 1) + 2:4, :]
                out = V[:, q0:q0 + cnt, :]
                c.link(v.tensor_tensor(out, lower, upper, ALU.subtract))
                c.link(v.tensor_tensor(out, out, wy[:, q0:q0 + cnt].unsqueeze(2).broadcast_to([P, cnt, HW]), ALU.mult))
                c.link(v.tensor_tensor(out, out, upper, ALU.add))

            def columns(c):
                for op in range(3):
                    for q0, cnt, p0 in RUNS:
                        left = V[:, :, p0:p0 + 4 * (cnt - 1) + 1:4]
                        right = V[:, :, p0 + 1:p0 + 4 * (cnt - 1) + 2:4]
                        out = qf[:, :, q0:q0 + cnt]
                        if op == 0:
                            c.done(v.tensor_tensor(out, right, left, ALU.subtract))
                        if op == 1:
                            c.done(v.tensor_tensor(out, out, wy[:, q0:q0 + cnt].unsqueeze(1).broadcast_to([P, GRID, cnt]), ALU.mult))
                        if op == 2:
                            c.done(v.tensor_tensor(out, out, left, ALU.add))
                    c.wait()

            g16 = lambda t: t[:, :].rearrange("p (g k) -> p g k", k=OH)
            over_groups = lambda t: t[:, :].unsqueeze(1).broadcast_to([P, GROUPS, OH])

            def offsets_dve(c, i, b, slot):
                if slot < 3:
                    if slot == 0:
                        for k in range(NCH):
                            dve.wait_ge(x_loaded[k], (i + 1) * 16)
                    rows(c, slot)
                    if slot == 2:
                        v.sem_inc(rows_interpolated, 1)
                if slot == 4:
                    columns(c)
                    v.sem_inc(qf_ready, 1)
                if slot in (7, 8, 9):
                    part = slot - 7
                    t0, n = 3 * part, min(3, TILES - 3 * part)
                    dve.wait_ge(qo_projected, i * 3 + part + 1)
                    c.done(v.tensor_copy(QO[:, b, t0:t0 + n, :], offp[:, 0:160 * n].rearrange("p (t n) -> p t n", n=160)))
                    c.wait()
                    v.sem_inc(qo_copied, 1)
                if slot == 9:
                    c.link(v.tensor_tensor(Z[:, :].rearrange("p (t n) -> p t n", n=32), QO[:, b, :, 0:32],
                                           bo1s[:, :, :].rearrange("p m k -> p (m k)").unsqueeze(1).broadcast_to([P, TILES, 32]), ALU.add))
                    c.link(v.tensor_reduce(st16[:, 0, :], g16(Z), AX.X, ALU.add))
                    c.link(v.scalar_tensor_tensor(g16(Z), st16[:, 0, :].unsqueeze(2).broadcast_to([P, GROUPS, OH]), -1.0 / OH,
                                                  g16(Z), ALU.mult, ALU.add))
                    c.link(v.tensor_tensor(Z2[:, :], Z[:, :], Z[:, :], ALU.mult))
                    c.link(v.tensor_reduce(st16[:, 1, :], g16(Z2), AX.X, ALU.add))
                    c.link(v.tensor_scalar(st16[:, 1, :], st16[:, 1, :], 1.0 / OH, LN_EPS, ALU.mult, ALU.add))
                    v.sem_inc(var_ready, 1)
                if slot == 11:
                    dve.wait_ge(rstd_ready, i + 1)
                    c.link(v.tensor_tensor(g16(Z), g16(Z), rstd[:, :].unsqueeze(2).broadcast_to([P, GROUPS, OH]), ALU.mult))
                    c.link(v.tensor_tensor(g16(Z), g16(Z), over_groups(lngs), ALU.mult))
                    c.link(v.tensor_tensor(g16(Z), g16(Z), over_groups(lnbs), ALU.add))
                    c.link(v.tensor_tensor(Z2[:, :], Z[:, :], Z[:, :], ALU.mult))
                    c.link(v.tensor_scalar(Z2[:, :], Z2[:, :], 0.044715 * GELU_2C, GELU_2C, ALU.mult, ALU.add))
                    c.link(v.tensor_tensor(Z3[:, :], Z2[:, :], Z[:, :], ALU.mult))
                    c.link(v.tensor_scalar(Z3[:, :], Z3[:, :], 80.0, None, ALU.min))
                    v.sem_inc(gelu_arg_ready, 1)
                if slot == 13:
                    dve.wait_ge(gelu_exp_ready, i + 1)
                    c.link(v.tensor_scalar(Z3[:, :], Z3[:, :], 1.0, None, ALU.add))
                    c.link(v.reciprocal(Z3[:, :], Z3[:, :]))
                    c.link(v.tensor_scalar(Z3[:, :], Z3[:, :], -1.0, 1.0, ALU.mult, ALU.add))
                    c.link(v.tensor_tensor(Z[:, :], Z[:, :], Z3[:, :], ALU.mult))
                    v.sem_inc(hidden_ready, 1)
                if slot == 16:
                    dve.wait_ge(offsets_projected, i + 1)
                    c.link(v.tensor_tensor(g16(Z), offp[:, 0:256].rearrange("p (g k) -> p g k", k=OH), over_groups(bo2s), ALU.add))
                    c.link(v.scalar_tensor_tensor(Z[:, :], Z[:, :], 4.0, ref[:, :], ALU.mult, ALU.add))
                    c.link(v.tensor_scalar(Z[:, :], Z[:, :], 0.0, float(HW - 1), ALU.max, ALU.min))
                    c.link(v.tensor_copy(PI[:, :], Z[:, :]))
                    c.link(v.tensor_copy(PF[:, :], PI[:, :]))
                    c.link(v.tensor_tensor(Z2[:, :], PF[:, :], Z[:, :], ALU.is_gt))
                    c.link(v.tensor_tensor(PF[:, :], PF[:, :], Z2[:, :], ALU.subtract))
                    c.link(v.tensor_scalar(PF[:, :], PF[:, :], float(HW - 2), None, ALU.min))
                    c.link(v.tensor_tensor(FG[:, :, 1], Z[:, :], PF[:, :], ALU.subtract))
                    c.link(v.tensor_scalar(FG[:, :, 0], FG[:, :, 1], -1.0, 1.0, ALU.mult, ALU.add))
                    fg = FG[:, :, :].rearrange("p (n a) w -> p n a w", a=2)
                    c.done(v.tensor_tensor(W[:, b, :, :].rearrange("p n (x y) -> p n x y", x=2),
                                           fg[:, :, 0, :].unsqueeze(3).broadcast_to([P, GROUPS * NH, 2, 2]),
                                           fg[:, :, 1, :].unsqueeze(2).broadcast_to([P, GROUPS * NH, 2, 2]), ALU.mult))
                    pf = PF[:, :].rearrange("p (n a) -> p n a", a=2)
                    c.link(v.scalar_tensor_tensor(idf[:, :], pf[:, :, 1], float(HW), pf[:, :, 0], ALU.mult, ALU.add))
                    c.link(v.tensor_tensor(idf[:, :], idf[:, :], base[:, :], ALU.add))
                    c.done(v.tensor_copy(idx[:, b, :], idf[:, :]))
                    c.wait()
                    v.sem_inc(points_ready, 1)

            def sample(c, j, b, g):
                dve.wait_ge(patches_gathered[g % 2], (j * (GROUPS // 2) + g // 2 + 1) * NH * 16)
                n = g % 2
                patches = G[:, n, :, :].rearrange("p k (x c) -> p (k x) c", c=C)
                w = W[:, b, g * NH:g * NH + NH, :].rearrange("p k x -> p (k x)").unsqueeze(2).broadcast_to([P, 4 * NH, C])
                c.link(v.tensor_tensor(patches, patches, w, ALU.mult))
                c.link(v.tensor_tensor(G[:, n, :, 0:2 * C], G[:, n, :, 0:2 * C], G[:, n, :, 2 * C:4 * C], ALU.add))
                wait_if(dve, sampled_transposed, j * GROUPS + g - 1)
                c.link(v.tensor_tensor(S[:, n, :].rearrange("p (k c) -> p k c", c=C), G[:, n, :, 0:C], G[:, n, :, C:2 * C], ALU.add))
                v.sem_inc(patches_used, 1)
                v.sem_inc(sampled_ready, 1)

            def scores(c, j, b, g):
                t, m, n = g // 2, g % 2, g % 2
                dve.wait_ge(kv_ready, j * GROUPS + g + 1)
                k_part = kvp[n][:, :, :].rearrange("p a (k n) -> p (a k) n", n=2 * C)[:, :, 0:C]
                q = QO[:, b, t, 32 + C * m:32 + C * m + C].unsqueeze(1).broadcast_to([P, NH, C])
                c.link(v.tensor_tensor(PR[:, :].rearrange("p (k c) -> p k c", c=C), k_part, q, ALU.mult))
                c.link(v.tensor_reduce(sc[:, n, :], PR[:, :].rearrange("p (s d) -> p s d", d=DH), AX.X, ALU.add))
                c.link(v.tensor_reduce(mx[:, :], sc[:, n, :].rearrange("p (k h) -> p h k", h=NH), AX.X, ALU.max))
                s3 = sc[:, n, :].rearrange("p (k h) -> p k h", h=NH)
                c.link(v.tensor_tensor(s3, s3, mx[:, :].unsqueeze(1).broadcast_to([P, NH, NH]), ALU.subtract))
                v.sem_inc(scores_ready, 1)

            def attend(c, j, b, g):
                n = g % 2
                dve.wait_ge(probs_ready, j * GROUPS + g + 1)
                e3 = ex[:, n, :].rearrange("p (k h) -> p k h", h=NH)
                c.done(v.tensor_reduce(den[:, :], e3.rearrange("p k h -> p h k"), AX.X, ALU.add))
                v_part = kvp[n][:, :, :].rearrange("p a (k n) -> p (a k) n", n=2 * C)[:, :, C:2 * C].rearrange("p k (h d) -> p k h d", d=DH)
                c.link(v.tensor_tensor(PV[:, :].rearrange("p (k h d) -> p k h d", h=NH, d=DH), v_part,
                                       e3.unsqueeze(3).broadcast_to([P, NH, NH, DH]), ALU.mult))
                c.done(v.reciprocal(rden[:, :], den[:, :]))
                c.link(v.tensor_reduce(o8[:, :], PV[:, :].rearrange("p (k c) -> p c k", c=C), AX.X, ALU.add))
                if g == 0:
                    wait_if(dve, h_stored, (j - 1) * 16)
                c.link(v.tensor_tensor(HO[:, b, g, :].rearrange("p (h d) -> p h d", d=DH), o8[:, :].rearrange("p (h d) -> p h d", d=DH),
                                       rden[:, :].unsqueeze(2).broadcast_to([P, NH, DH]), ALU.mult))
                v.sem_inc(attended, 1)

            def body(i, j, b):
                ca = None if i is None else Steps(dve, dve_a, A_DVE, i)
                cb = None if j is None else Steps(dve, dve_b, B_DVE, j)
                for g in range(GROUPS + 2):
                    if j is not None and g < GROUPS:
                        sample(cb, j, 1 - b, g)
                    if i is not None and g <= GROUPS:
                        offsets_dve(ca, i, b, g)
                    if j is not None:
                        if 1 <= g <= GROUPS:
                            scores(cb, j, 1 - b, g - 1)
                        if g >= 2:
                            attend(cb, j, 1 - b, g - 2)
                if ca:
                    ca.close()
                if cb:
                    cb.close()

            body(0, None, 0)
            body(1, 0, 1)
            body(2, 1, 0)
            with dve.Fori(1, PAIRS // 2 - 1) as s:
                body(s * 2 + 1, s * 2, 1)
                body(s * 2 + 2, s * 2 + 1, 0)
            body(PAIRS - 1, PAIRS - 2, 1)
            body(None, PAIRS - 1, 0)


LAYERS = 4
FF = 4 * C
RH = C // 2
EXP = 6
HALF = NQ // 2
QK_SCALE = float(DH) ** -0.25


def ln_steps(tag, pe, act, dve):
    pe += [f"{tag}.center{h}" for h in range(2)] + [f"{tag}.var{h}" for h in range(2)]
    act += [f"{tag}.square{h}" for h in range(2)] + [f"{tag}.rstd{h}" for h in range(2)]
    dve += [f"{tag}.norm{h}" for h in range(2)]


def tower_steps():
    pe, act, dve, pool = [], [], [], []
    both = lambda name: [f"{name}{h}" for h in range(2)]
    pe += both("h_transposed")
    act += both("h_copied")
    ln_steps("in", pe, act, dve)
    for l in range(LAYERS):
        ln_steps(f"a{l}", pe, act, dve)
        pool += both(f"a{l}.shift")
        pe += [f"{l}.{n}" for n in ("k0", "k1", "q0", "q1", "v0", "v1", "kT0", "kT1", "qT0", "qT1", "context", "out_weights", "out0", "out1")]
        act += [f"{l}.{n}" for n in ("k_exp0", "k_exp1", "q_exp0", "q_exp1", "v_copied0", "v_copied1", "kT_copied0", "kT_copied1", "qT_copied0", "qT_copied1")]
        dve += [f"{l}.{n}" for n in ("k_max", "q_shifted0", "q_shifted1", "q_ready0", "q_ready1", "context_ready", "out_weights_ready", "added0", "added1")]
        ln_steps(f"f{l}", pe, act, dve)
        pool += both(f"f{l}.shift")
        pe += [f"{l}.up{c}{h}" for c in range(4) for h in range(2)] + both(f"{l}.down")
        act += [f"{l}.gelu{c}{h}" for c in range(4) for h in range(2)]
        dve += both(f"{l}.ff_added")
    pool += both("residual")
    ln_steps("m", pe, act, dve)
    pe += both("router_hidden") + ["logits", "weights_transposed"]
    act += both("router_relu") + ["expert_exp", "second_exp", "weights_copied"]
    dve += ["logits_shifted", "top_ready", "weights_ready"]
    for e in range(EXP):
        pe += both(f"e{e}.first") + both(f"e{e}.second") + both(f"e{e}.weight")
        act += both(f"e{e}.first_relu") + both(f"e{e}.second_relu")
        dve += both(f"e{e}.weighted")
    pe += both("final")
    act += both("final_copied")
    return {"pe": pe, "act": act, "dve": dve, "pool": pool}


STEPS = tower_steps()
AT = {engine: {name: n + 1 for n, name in enumerate(names)} for engine, names in STEPS.items()}
DVE_OWN = LAYERS * 11 + 21


class Signals:

    def __init__(self, engine, eng, sems, round_):
        self.engine, self.eng, self.sems, self.n, self.round = engine, eng, sems, 0, round_

    def mark(self, ins, name):
        assert STEPS[self.engine][self.n] == name, (STEPS[self.engine][self.n], name)
        ins.then_inc(self.sems[self.engine], 1)
        self.n += 1

    def wait(self, engine, name):
        self.eng.wait_ge(self.sems[engine], self.round * len(STEPS[engine]) + AT[engine][name])

    def wait_last_round(self, engine):
        wait_if(self.eng, self.sems[engine], self.round * len(STEPS[engine]))

    def close(self):
        assert self.n == len(STEPS[self.engine])


def tower_stage(nc, PAIRS, hd, out, w):
    ROUNDS = PAIRS // 2
    out_v = out.rearrange("(i m) (t p) c -> i p t m c", m=2, p=P)
    with ExitStack() as ctx:
        sb = lambda name, shape, dt=F32: ctx.enter_context(nc.sbuf_tensor(name, shape, dt))
        pb = lambda name, shape: ctx.enter_context(nc.psum_tensor(name, shape, F32))
        sem = lambda name: ctx.enter_context(nc.semaphore(name))
        two = lambda name, shape: [sb(f"{name}{s}", shape) for s in range(2)]

        ident = sb("ident_t", [P, P])
        center = sb("center", [P, P])
        mean = sb("mean", [P, P])
        hmask = sb("hmask", [P, P])
        rank = sb("rank", [P, EXP])
        eps = sb("eps", [P, 1])
        Wq = sb("Wq", [P, LAYERS, P])
        Wk = sb("Wk", [P, LAYERS, P])
        Wv = sb("Wv", [P, LAYERS, P])
        Wo = sb("Wo", [P, LAYERS, P])
        W1 = sb("W1", [P, LAYERS, FF])
        W2 = sb("W2", [P, LAYERS, 2, C])
        cols = sb("cols", [P, 6, LAYERS])
        b1c = sb("b1c", [P, LAYERS, 2])
        Rw1 = sb("Rw1", [P, 2 * RH])
        rb1 = sb("rb1", [2 * RH, 1])
        Rw2 = sb("Rw2", [2 * RH, 2 * EXP])
        rb2 = sb("rb2", [P, EXP])
        E1w = sb("E1w", [P, EXP, P])
        E2w = sb("E2w", [P, EXP, P])
        E3w = sb("E3w", [P, EXP, P])
        eb1 = sb("eb1", [P, EXP])
        eb2 = sb("eb2", [P, EXP])
        eb3 = sb("eb3", [2 * EXP, P])
        spread = sb("spread", [2 * EXP, EXP, P])

        HTOK = two("HTOK", [P, TILES, P])
        HH = two("HH", [P, NQ])
        X = two("XT", [P, NQ])
        SQ = two("SQ", [P, NQ])
        R = two("R", [P, NQ])
        HN = two("HN", [P, NQ])
        QE = two("QE", [P, TILES, P])
        QT = two("QT", [P, NQ])
        KE = two("KE", [P, NQ])
        KT = two("KT", [P, TILES, P])
        VT = two("VT", [P, TILES, P])
        BIG = two("BIG", [P, EXP, NQ])
        OT = two("OT", [P, TILES, P])
        CT = two("CT", [P, P])
        MM = two("MM", [P, P])
        kmax = two("kmax", [P, 4])
        kden = two("kden", [P, 4])
        qmax = two("qmax", [P, P])
        LG = two("LG", [P, TILES * 2 * EXP])
        L2 = two("L2", [P, TILES * 2 * EXP])
        L3 = two("L3", [P, TILES * 2 * EXP])
        S1 = two("S1", [P, TILES * 2 * EXP])
        t16 = two("t16", [P, 8, GROUPS])
        WF = two("WF", [2 * EXP, NQ])
        U = [[pb(f"U{s}{n}", [P, 2, HALF]) for n in range(2)] for s in range(2)]

        zeroed = sem("zeroed")
        w_loaded = sem("w_loaded")
        h_loaded = [sem(f"h_loaded{s}") for s in range(2)]
        out_stored = [sem(f"out_stored{s}") for s in range(2)]
        done = [{e: sem(f"{e}_done{s}") for e in ("pe", "act", "dve", "pool")} for s in range(2)]
        own = [sem(f"dve_own{s}") for s in range(2)]
        sp_turns = sem("sp_turns_t")
        rstd_log = [sem(f"rstd_log{s}") for s in range(2)]

        block = ctx.enter_context(nc.Block())
        half = lambda t, h: t[:, HALF * h:HALF * h + HALF]
        tiles = lambda t, h: t[:, 4 * h:4 * h + 4, :]
        flat = lambda t: t.rearrange("p a b -> p (a b)")
        streams = range(2)
        N_ZERO = 9

        @block.gpsimd
        def _(pool):
            for t in (Wq, Wk, Wv, Wo, Rw1, Rw2, E1w, E2w, E3w):
                nc.gpsimd.memset(t[:], 0.0).then_inc(zeroed, 1)
            nc.gpsimd.memset(eb3[:], 0.0).then_inc(zeroed, 1)
            nc.gpsimd.memset(eps[:, :], LN_EPS).then_inc(zeroed, 1)

            def round_(r):
                sg = [Signals("pool", pool, done[s], r) for s in streams]

                def shift(s, tag, col):
                    for h in range(2):
                        sg[s].wait("dve", f"{tag}.norm{h}")
                        sg[s].mark(nc.gpsimd.tensor_tensor(half(HN[s], h), half(HN[s], h),
                                                         cols[:, col, l:l + 1].broadcast_to([P, HALF]), ALU.add), f"{tag}.shift{h}")
                for l in range(LAYERS):
                    for s in streams:
                        shift(s, f"a{l}", 1)
                    for s in streams:
                        shift(s, f"f{l}", 4)
                for s in streams:
                    for h in range(2):
                        sg[s].wait("dve", f"{LAYERS - 1}.ff_added{h}")
                        sg[s].mark(nc.gpsimd.tensor_tensor(half(HH[s], h), half(HH[s], h), half(X[s], h), ALU.add), f"residual{h}")
                for s in streams:
                    sg[s].close()
            pool.wait_ge(w_loaded, w["count"] * 16)
            round_(0)
            with pool.Fori(1, ROUNDS) as r:
                round_(r)

        @block.sync
        def _(sp):
            def load_h(r, s):
                sp.dma_start(flat(HTOK[s][:, :, :]), hd[bass.ts(r * 2 + s, P), :]).then_inc(h_loaded[s], 16)

            for s in streams:
                load_h(0, s)
            sp.wait_ge(zeroed, 11)
            n = 0

            def put(dst, src):
                nonlocal n
                sp.dma_start(dst, src).then_inc(w_loaded, 16)
                n += 1
            for m in range(2):
                r = slice(C * m, C * m + C)
                for dst, src in ((Wq, w["L0_attn_Wq"]), (Wk, w["L0_attn_Wk"]), (Wv, w["L0_attn_Wv"]), (Wo, w["L0_attn_Wo"])):
                    put(dst[r, :, r], src.rearrange("l i o -> i l o"))
                put(W1[r, :, :], w["L0_attn_W1"].rearrange("l i o -> i l o"))
                for c, name in enumerate(("ln1_g", "ln1_b", "bo", "ln2_g", "ln2_b", "b2")):
                    for l in range(LAYERS):
                        put(cols[r, c, l:l + 1], w[f"L0_attn_{name}"][l, :].unsqueeze(1))
                put(Rw1[r, RH * m:RH * m + RH], w["L0_ffn_router_w1"])
                put(Rw2[RH * m:RH * m + RH, EXP * m:EXP * m + EXP], w["L0_ffn_router_w2"])
                put(rb1[RH * m:RH * m + RH, :], w["L0_ffn_router_b1"].unsqueeze(1))
                for dst, src in ((E1w, w["L0_ffn_expert_w1"]), (E2w, w["L0_ffn_expert_w2"]), (E3w, w["L0_ffn_expert_w3"])):
                    put(dst[r, :, r], src.rearrange("l i o -> i l o"))
                for e in range(EXP):
                    put(eb1[r, e:e + 1], w["L0_ffn_expert_b1"][e, :].unsqueeze(1))
                    put(eb2[r, e:e + 1], w["L0_ffn_expert_b2"][e, :].unsqueeze(1))
                put(eb3[EXP * m:EXP * m + EXP, r], w["L0_ffn_expert_b3"])
            for f in range(2):
                put(W2[:, :, f, :], w["L0_attn_W2"][:, P * f:P * f + P, :].rearrange("l i o -> i l o"))
                for l in range(LAYERS):
                    put(b1c[:, l, f:f + 1], w["L0_attn_b1"][l, P * f:P * f + P].unsqueeze(1))
            put(rb2[:, :], w["L0_ffn_router_b2"].partition_broadcast(P))
            for dst, name in ((ident, "c_ident"), (center, "c_center"), (mean, "c_mean"), (hmask, "c_hmask"), (rank, "c_rank")):
                put(dst[:, :], w[name])
            put(spread[:, :, :], w["c_spread"])
            assert n == w["count"], n

            def store_out(r, s):
                for h in range(2):
                    hold(sp, done[s]["act"], r * len(STEPS["act"]) + AT["act"][f"final_copied{h}"], sp_turns)
                for m in range(2):
                    sp.dma_start(out_v[r * 2 + s, :, :, m, :] if isinstance(r, int) else
                                 out_v[bass.ds(r * 2 + s, 1), :, :, m, :].rearrange("a p t c -> (a p) t c"),
                                 OT[s][:, :, C * m:C * m + C]).then_inc(out_stored[s], 16)

            with sp.Fori(0, ROUNDS - 1) as r:
                for s in streams:
                    hold(sp, done[s]["pe"], r * len(STEPS["pe"]) + AT["pe"]["h_transposed1"], sp_turns)
                    load_h(r + 1, s)
                for s in streams:
                    store_out(r, s)
            for s in streams:
                store_out(ROUNDS - 1, s)
            for s in streams:
                sp.wait_ge(out_stored[s], ROUNDS * 32)

        @block.scalar
        def _(act):
            sc = nc.scalar
            act.wait_ge(w_loaded, w["count"] * 16)

            def round_(r):
                sg = [Signals("act", act, done[s], r) for s in streams]
                logs = [0, 0]
                per = 2 * (2 * LAYERS + 2)

                def squares(s, tag):
                    for h in range(2):
                        sg[s].wait("pe", f"{tag}.center{h}")
                        sg[s].mark(sc.activation(half(SQ[s], h), U[s][0][:, h, :], ACT.Square), f"{tag}.square{h}")

                def rstds(s, tag):
                    for h in range(2):
                        sg[s].wait("pe", f"{tag}.var{h}")
                        logs[s] += 1
                        sc.activation(half(R[s], h), U[s][1][:, h, :], ACT.Ln, bias=eps[:, 0:1]).then_inc(rstd_log[s], 1)
                        act.wait_ge(rstd_log[s], r * per + logs[s])
                        sg[s].mark(sc.activation(half(R[s], h), half(R[s], h), ACT.Exp, scale=-0.5), f"{tag}.rstd{h}")

                def norm(tag):
                    for s in streams:
                        squares(s, tag)
                    for s in streams:
                        rstds(s, tag)

                for s in streams:
                    for h in range(2):
                        sg[s].wait("pe", f"h_transposed{h}")
                        sg[s].mark(sc.copy(half(HH[s], h), U[s][0][:, h, :]), f"h_copied{h}")
                norm("in")
                for l in range(LAYERS):
                    norm(f"a{l}")
                    for s in streams:
                        sg[s].wait("dve", f"{l}.k_max")
                        for h in range(2):
                            sg[s].mark(sc.activation(half(KE[s], h), U[s][1][:, h, :], ACT.Exp, bias=kmax[s][:, 3:4], scale=QK_SCALE,
                                                     accum_out=kden[s][:, h:h + 1]), f"{l}.k_exp{h}")
                        for h in range(2):
                            sg[s].wait("dve", f"{l}.q_shifted{h}")
                            sg[s].mark(sc.activation(tiles(QE[s], h), tiles(QE[s], h), ACT.Exp, scale=QK_SCALE), f"{l}.q_exp{h}")
                    for s in streams:
                        for what, dst, u in (("v", VT, 1), ("kT", KT, 0)):
                            for h in range(2):
                                sg[s].wait("pe", f"{l}.{what}{h}")
                                sg[s].mark(sc.copy(flat(tiles(dst[s], h)), U[s][u][:, h, :]), f"{l}.{what}_copied{h}")
                    for s in streams:
                        for h in range(2):
                            sg[s].wait("pe", f"{l}.qT{h}")
                            sg[s].mark(sc.copy(half(QT[s], h), U[s][1][:, h, :]), f"{l}.qT_copied{h}")
                    norm(f"f{l}")
                    for cc in range(2):
                        for s in streams:
                            for c in (2 * cc, 2 * cc + 1):
                                for h in range(2):
                                    sg[s].wait("pe", f"{l}.up{c}{h}")
                                    sg[s].mark(sc.activation(half(BIG[s][:, c, :], h), U[s][c % 2][:, h, :], ACT.Gelu,
                                                             bias=b1c[:, l, c % 2:c % 2 + 1]), f"{l}.gelu{c}{h}")
                    act.preload_act_table_set("natural_log_exp_and_others")
                norm("m")
                for s in streams:
                    for h in range(2):
                        sg[s].wait("pe", f"router_hidden{h}")
                        sg[s].mark(sc.activation(QT[s][0:2 * RH, HALF * h:HALF * h + HALF], U[s][1][0:2 * RH, h, :], ACT.Relu, bias=rb1[:, 0:1]), f"router_relu{h}")
                for s in streams:
                    sg[s].wait("dve", "logits_shifted")
                    sg[s].mark(sc.activation(LG[s][:, :], LG[s][:, :], ACT.Exp), "expert_exp")
                for s in streams:
                    sg[s].wait("dve", "top_ready")
                    sg[s].mark(sc.activation(t16[s][:, 4, :], t16[s][:, 3, :], ACT.Exp), "second_exp")
                for s in streams:
                    sg[s].wait("pe", "weights_transposed")
                    sg[s].mark(sc.copy(WF[s][:, :].rearrange("p (a b) -> p a b", a=2), U[s][0][0:2 * EXP, :, :]), "weights_copied")
                for e in range(EXP):
                    for s in streams:
                        for h in range(2):
                            sg[s].wait("pe", f"e{e}.first{h}")
                            sg[s].mark(sc.activation(half(SQ[s], h), U[s][0][:, h, :], ACT.Relu, bias=eb1[:, e:e + 1]), f"e{e}.first_relu{h}")
                    for s in streams:
                        for h in range(2):
                            sg[s].wait("pe", f"e{e}.second{h}")
                            sg[s].mark(sc.activation(half(BIG[s][:, e, :], h), U[s][1][:, h, :], ACT.Relu, bias=eb2[:, e:e + 1]), f"e{e}.second_relu{h}")
                for s in streams:
                    wait_if(act, out_stored[s], r * 32)
                    for h in range(2):
                        sg[s].wait("pe", f"final{h}")
                        sg[s].mark(sc.copy(flat(tiles(OT[s], h)), U[s][0][:, h, :]), f"final_copied{h}")
                    sg[s].close()
                assert logs[0] == per

            act.preload_act_table_set("natural_log_exp_and_others")
            round_(0)
            with act.Fori(1, ROUNDS) as r:
                round_(r)

        @block.tensor
        def _(pe):
            mmul = lambda o, a, b, start=True, stop=True: nc.tensor.matmul(o, a, b, start=start, stop=stop)
            pe.wait_ge(w_loaded, w["count"] * 16)

            def round_(r):
                sg = [Signals("pe", pe, done[s], r) for s in streams]

                def norm(tag, src, ready):
                    for s in streams:
                        for h in range(2):
                            sg[s].wait(*ready(h))
                            sg[s].mark(mmul(U[s][0][:, h, :], center[:, :], half(src[s], h)), f"{tag}.center{h}")
                    for s in streams:
                        for h in range(2):
                            sg[s].wait("act", f"{tag}.square{h}")
                            sg[s].mark(mmul(U[s][1][:, h, :], mean[:, :], half(SQ[s], h)), f"{tag}.var{h}")

                for s in streams:
                    pe.wait_ge(h_loaded[s], (r + 1) * 16)
                    sg[s].wait_last_round("act")
                    for h in range(2):
                        for t in range(4):
                            ins = nc.tensor.transpose(U[s][0][:, h, P * t:P * t + P], HTOK[s][:, 4 * h + t, :], ident[:, :])
                        sg[s].mark(ins, f"h_transposed{h}")
                norm("in", HH, lambda h: ("act", f"h_copied{h}"))
                for l in range(LAYERS):
                    norm(f"a{l}", X, lambda h: ("dve", f"in.norm{h}" if l == 0 else f"{l - 1}.ff_added{h}"))
                    for s in streams:
                        for h in range(2):
                            sg[s].wait("pool", f"a{l}.shift{h}")
                            sg[s].mark(mmul(U[s][1][:, h, :], Wk[:, l, :], half(HN[s], h)), f"{l}.k{h}")
                        for h in range(2):
                            for t in range(4):
                                ins = mmul(U[s][0][:, h, P * t:P * t + P], HN[s][:, P * (4 * h + t):P * (4 * h + t) + P], Wq[:, l, :])
                            sg[s].mark(ins, f"{l}.q{h}")
                    for s in streams:
                        for h in range(2):
                            sg[s].wait("act", f"{l}.k_exp{h}")
                            for t in range(4):
                                ins = mmul(U[s][1][:, h, P * t:P * t + P], HN[s][:, P * (4 * h + t):P * (4 * h + t) + P], Wv[:, l, :])
                            sg[s].mark(ins, f"{l}.v{h}")
                        for h in range(2):
                            sg[s].wait("dve", f"{l}.q_shifted{h}")
                            for t in range(4):
                                ins = nc.tensor.transpose(U[s][0][:, h, P * t:P * t + P], KE[s][:, P * (4 * h + t):P * (4 * h + t) + P], ident[:, :])
                            sg[s].mark(ins, f"{l}.kT{h}")
                    for s in streams:
                        for h in range(2):
                            sg[s].wait("act", f"{l}.v_copied{h}")
                            sg[s].wait("dve", f"{l}.q_ready{h}")
                            for t in range(4):
                                ins = nc.tensor.transpose(U[s][1][:, h, P * t:P * t + P], QE[s][:, 4 * h + t, :], ident[:, :])
                            sg[s].mark(ins, f"{l}.qT{h}")
                        sg[s].wait("act", f"{l}.kT_copied1")
                        for t in range(TILES):
                            ins = mmul(U[s][0][:, 0, 0:P], VT[s][:, t, :], KT[s][:, t, :], start=t == 0, stop=t == TILES - 1)
                        sg[s].mark(ins, f"{l}.context")
                    for s in streams:
                        sg[s].wait("dve", f"{l}.context_ready")
                        sg[s].mark(mmul(U[s][0][:, 1, 0:P], CT[s][:, :], Wo[:, l, :]), f"{l}.out_weights")
                    for s in streams:
                        sg[s].wait("dve", f"{l}.out_weights_ready")
                        for h in range(2):
                            sg[s].wait("act", f"{l}.qT_copied{h}")
                            sg[s].mark(mmul(U[s][1][:, h, :], MM[s][:, :], half(QT[s], h)), f"{l}.out{h}")
                    norm(f"f{l}", X, lambda h: ("dve", f"{l}.added{h}"))
                    for cc in range(2):
                        for s in streams:
                            for c in (2 * cc, 2 * cc + 1):
                                m, f = c // 2, c % 2
                                for h in range(2):
                                    if cc == 0:
                                        sg[s].wait("pool", f"f{l}.shift{h}")
                                    else:
                                        sg[s].wait("act", f"{l}.gelu{c - 2}{h}")
                                    sg[s].mark(mmul(U[s][f][:, h, :], W1[C * m:C * m + C, l, P * f:P * f + P],
                                                    HN[s][C * m:C * m + C, HALF * h:HALF * h + HALF]), f"{l}.up{c}{h}")
                    for s in streams:
                        for h in range(2):
                            sg[s].wait("act", f"{l}.gelu3{h}")
                            for m in range(2):
                                for f in range(2):
                                    ins = mmul(U[s][0][C * m:C * m + C, h, :], W2[:, l, f, :], half(BIG[s][:, 2 * m + f, :], h), start=f == 0, stop=f == 1)
                            sg[s].mark(ins, f"{l}.down{h}")
                norm("m", HH, lambda h: ("pool", f"residual{h}"))
                for s in streams:
                    for h in range(2):
                        sg[s].wait("dve", f"m.norm{h}")
                        sg[s].mark(mmul(U[s][1][0:2 * RH, h, :], Rw1[:, :], half(HN[s], h)), f"router_hidden{h}")
                for s in streams:
                    sg[s].wait("act", "router_relu1")
                    for t in range(TILES):
                        ins = mmul(U[s][0][:, 0, 2 * EXP * t:2 * EXP * t + 2 * EXP], QT[s][0:2 * RH, P * t:P * t + P], Rw2[:, :])
                    sg[s].mark(ins, "logits")
                for s in streams:
                    sg[s].wait("dve", "weights_ready")
                    for t in range(TILES):
                        ins = nc.tensor.transpose(U[s][0][0:2 * EXP, t // 4, P * (t % 4):P * (t % 4) + P], L3[s][:, 2 * EXP * t:2 * EXP * t + 2 * EXP], ident[:, :])
                    sg[s].mark(ins, "weights_transposed")
                for e in range(EXP):
                    for s in streams:
                        for h in range(2):
                            if e == 0:
                                sg[s].wait("act", "weights_copied")
                            else:
                                sg[s].wait("dve", f"e{e - 1}.weighted{h}")
                            sg[s].mark(mmul(U[s][0][:, h, :], E1w[:, e, :], half(HN[s], h)), f"e{e}.first{h}")
                    for s in streams:
                        for h in range(2):
                            sg[s].wait("act", f"e{e}.first_relu{h}")
                            sg[s].mark(mmul(U[s][1][:, h, :], E2w[:, e, :], half(SQ[s], h)), f"e{e}.second{h}")
                        for h in range(2):
                            sg[s].mark(mmul(U[s][0][:, h, :], spread[:, e, :], half(WF[s], h)), f"e{e}.weight{h}")
                for s in streams:
                    for h in range(2):
                        for hh in range(2):
                            sg[s].wait("dve", f"e{EXP - 1}.weighted{hh}")
                        for t in range(4):
                            tok = slice(P * (4 * h + t), P * (4 * h + t) + P)
                            o = U[s][0][:, h, P * t:P * t + P]
                            mmul(o, HH[s][:, tok], ident[:, :], True, False)
                            for e in range(EXP):
                                mmul(o, BIG[s][:, e, tok], E3w[:, e, :], False, False)
                            ins = mmul(o, WF[s][:, tok], eb3[:, :], False, True)
                        sg[s].mark(ins, f"final{h}")
                    sg[s].close()

            round_(0)
            with pe.Fori(1, ROUNDS) as r:
                round_(r)

        @block.vector
        def _(dve):
            v = nc.vector
            dve.wait_ge(w_loaded, w["count"] * 16)

            def round_(r):
                sg = [Signals("dve", dve, done[s], r) for s in streams]
                cs = [Steps(dve, own[s], DVE_OWN, r) for s in streams]

                def norm(tag, dst, gain=None):
                    for s in streams:
                        for h in range(2):
                            sg[s].wait("act", f"{tag}.rstd{h}")
                            if gain is None:
                                ins = v.tensor_tensor(half(dst[s], h), U[s][0][:, h, :], half(R[s], h), ALU.mult)
                            else:
                                ins = v.scalar_tensor_tensor(half(dst[s], h), U[s][0][:, h, :], gain, half(R[s], h), ALU.mult, ALU.mult)
                            sg[s].mark(ins, f"{tag}.norm{h}")

                norm("in", X)
                for l in range(LAYERS):
                    norm(f"a{l}", HN, cols[:, 0, l:l + 1])
                    for s in streams:
                        c = cs[s]
                        for h in range(2):
                            sg[s].wait("pe", f"{l}.k{h}")
                            c.done(v.tensor_reduce(kmax[s][:, h:h + 1], U[s][1][:, h, :], AX.X, ALU.max))
                        c.wait()
                        c.link(v.tensor_reduce(kmax[s][:, 2:3], kmax[s][:, 0:2], AX.X, ALU.max))
                        sg[s].mark(v.tensor_scalar(kmax[s][:, 3:4], kmax[s][:, 2:3], -QK_SCALE, None, ALU.mult), f"{l}.k_max")
                        heads = lambda t, h: t.rearrange("p (g d) -> p g d", d=DH)
                        for h in range(2):
                            sg[s].wait("pe", f"{l}.q{h}")
                            qm = qmax[s][:, C * h:C * h + C]
                            u = U[s][0][:, h, :].rearrange("p (g d) -> p g d", d=DH)
                            c.link(v.tensor_reduce(qm, u, AX.X, ALU.max))
                            sg[s].mark(v.tensor_tensor(flat(tiles(QE[s], h)).rearrange("p (g d) -> p g d", d=DH), u,
                                                       qm.unsqueeze(2).broadcast_to([P, C, DH]), ALU.subtract), f"{l}.q_shifted{h}")
                    for s in streams:
                        c = cs[s]
                        for h in range(2):
                            sg[s].wait("act", f"{l}.q_exp{h}")
                            qm = qmax[s][:, C * h:C * h + C]
                            q = flat(tiles(QE[s], h)).rearrange("p (g d) -> p g d", d=DH)
                            c.link(v.tensor_reduce(qm, q, AX.X, ALU.add))
                            c.link(v.reciprocal(qm, qm))
                            sg[s].mark(v.tensor_tensor(q, q, qm.unsqueeze(2).broadcast_to([P, C, DH]), ALU.mult), f"{l}.q_ready{h}")
                    for s in streams:
                        sg[s].wait("pe", f"{l}.context")
                        sg[s].mark(v.tensor_tensor(CT[s][:, :], U[s][0][:, 0, 0:P], hmask[:, :], ALU.mult), f"{l}.context_ready")
                    for s in streams:
                        c = cs[s]
                        c.link(v.tensor_tensor(kden[s][:, 2:3], kden[s][:, 0:1], kden[s][:, 1:2], ALU.add))
                        c.link(v.reciprocal(kden[s][:, 3:4], kden[s][:, 2:3]))
                        sg[s].wait("pe", f"{l}.out_weights")
                        sg[s].mark(v.tensor_scalar(MM[s][:, :], U[s][0][:, 1, 0:P], kden[s][:, 3:4], None, ALU.mult), f"{l}.out_weights_ready")
                    for s in streams:
                        for h in range(2):
                            sg[s].wait("pe", f"{l}.out{h}")
                            sg[s].mark(v.scalar_tensor_tensor(half(X[s], h), U[s][1][:, h, :], cols[:, 2, l:l + 1], half(X[s], h), ALU.add, ALU.add), f"{l}.added{h}")
                    norm(f"f{l}", HN, cols[:, 3, l:l + 1])
                    for s in streams:
                        for h in range(2):
                            sg[s].wait("pe", f"{l}.down{h}")
                            sg[s].mark(v.scalar_tensor_tensor(half(X[s], h), U[s][0][:, h, :], cols[:, 5, l:l + 1], half(X[s], h), ALU.add, ALU.add), f"{l}.ff_added{h}")
                norm("m", HN)
                g6 = lambda t: t[:, :].rearrange("p (g e) -> p g e", e=EXP)
                bc = lambda t: t.unsqueeze(2).broadcast_to([P, GROUPS, EXP])
                row = lambda t: t[:, :].unsqueeze(1).broadcast_to([P, GROUPS, EXP])
                for s in streams:
                    c, t = cs[s], t16[s]
                    sg[s].wait("pe", "logits")
                    c.link(v.tensor_tensor(g6(LG[s]), U[s][0][:, 0, 0:GROUPS * EXP].rearrange("p (g e) -> p g e", e=EXP), row(rb2), ALU.add))
                    c.link(v.tensor_reduce(t[:, 0, :], g6(LG[s]), AX.X, ALU.max))
                    sg[s].mark(v.tensor_tensor(g6(LG[s]), g6(LG[s]), bc(t[:, 0, :]), ALU.subtract), "logits_shifted")
                for s in streams:
                    c, t = cs[s], t16[s]
                    sg[s].wait("act", "expert_exp")
                    c.link(v.tensor_reduce(t[:, 0, :], g6(LG[s]), AX.X, ALU.add))
                    c.link(v.reciprocal(t[:, 0, :], t[:, 0, :]))
                    c.link(v.tensor_tensor(g6(LG[s]), g6(LG[s]), bc(t[:, 0, :]), ALU.mult))
                    for k, (src, sel) in enumerate(((LG[s], S1[s]), (L2[s], L3[s]))):
                        if k == 1:
                            c.link(v.scalar_tensor_tensor(L2[s][:, :], S1[s][:, :], -2.0, LG[s][:, :], ALU.mult, ALU.add))
                        c.link(v.tensor_reduce(t[:, 1 + k, :], g6(src), AX.X, ALU.max))
                        c.link(v.tensor_tensor(g6(sel), g6(src), bc(t[:, 1 + k, :]), ALU.is_equal))
                        c.link(v.tensor_tensor(g6(sel), g6(sel), row(rank), ALU.mult))
                        c.link(v.tensor_reduce(t[:, 5, :], g6(sel), AX.X, ALU.max))
                        c.link(v.tensor_tensor(g6(sel), g6(sel), bc(t[:, 5, :]), ALU.is_equal))
                    sg[s].mark(v.tensor_tensor(t[:, 3, :], t[:, 2, :], t[:, 1, :], ALU.subtract), "top_ready")
                for s in streams:
                    c, t = cs[s], t16[s]
                    sg[s].wait("act", "second_exp")
                    c.link(v.tensor_scalar(t[:, 6, :], t[:, 4, :], 1.0, None, ALU.add))
                    c.link(v.reciprocal(t[:, 6, :], t[:, 6, :]))
                    c.link(v.tensor_tensor(t[:, 7, :], t[:, 4, :], t[:, 6, :], ALU.mult))
                    c.link(v.tensor_tensor(g6(S1[s]), g6(S1[s]), bc(t[:, 6, :]), ALU.mult))
                    c.link(v.tensor_tensor(g6(L3[s]), g6(L3[s]), bc(t[:, 7, :]), ALU.mult))
                    sg[s].mark(v.tensor_tensor(L3[s][:, :], L3[s][:, :], S1[s][:, :], ALU.add), "weights_ready")
                for e in range(EXP):
                    for s in streams:
                        for h in range(2):
                            sg[s].wait("act", f"e{e}.second_relu{h}")
                            sg[s].wait("pe", f"e{e}.weight{h}")
                            b = half(BIG[s][:, e, :], h)
                            sg[s].mark(v.tensor_tensor(b, b, U[s][0][:, h, :], ALU.mult), f"e{e}.weighted{h}")
                for s in streams:
                    sg[s].close()
                    cs[s].close()

            round_(0)
            with dve.Fori(1, ROUNDS) as r:
                round_(r)


def build(nc, a, out):
    PAIRS = a["x"].shape[0] // 2
    scr = [nc.dram_tensor(f"scratch{n}", (2 * (HW - 1) * HW, 2 * C), F32).ap() for n in range(2)]
    hd = nc.dram_tensor("h_scratch", (PAIRS * P, GROUPS * C), F32).ap()
    tok_stage(nc, PAIRS, a["x"], scr, hd, a["wqT"], a["wkT"], a["wvT"], a["L0_tok_W_o1"], a["L0_tok_b_o1"],
              a["L0_tok_ln_g"], a["L0_tok_ln_b"], a["L0_tok_W_o2"], a["L0_tok_b_o2"],
              a["c_ident"], a["c_ref"], a["c_wy"], a["c_base"])
    tower_stage(nc, PAIRS, hd, out, dict(a, count=113))


def kernel(**inputs):
    import numpy as _np
    import concourse.bacc as _bacc
    from concourse import mybir as _mybir
    from concourse.bass_utils import run_bass_kernel_spmd as _run

    nb = inputs["x"].shape[0]
    lin = _np.linspace(-1.0, 1.0, GRID, dtype=_np.float32)
    px = (lin + _np.float32(1)) * _np.float32(0.5) * _np.float32(HW - 1)
    tok = _np.arange(NQ)
    xy = _np.stack([px[tok % GRID], px[tok // GRID]], -1).reshape(TILES, P, 2).transpose(1, 0, 2)
    left = _np.minimum(_np.floor(px), HW - 2)
    same = lambda n: _np.equal.outer(_np.arange(P) // n, _np.arange(P) // n).astype(_np.float32)
    spread = _np.zeros((2 * EXP, EXP, P), _np.float32)
    for m in range(2):
        for e in range(EXP):
            spread[EXP * m + e, e, C * m:C * m + C] = 1
    constants = {
        "c_ident": _np.eye(P, dtype=_np.float32),
        "c_ref": _np.broadcast_to(xy[:, :, None, None, :], (P, TILES, 2, NH, 2)).reshape(P, 256),
        "c_wy": _np.broadcast_to((px - left)[None], (P, GRID)),
        "c_base": _np.broadcast_to(_np.array([0, (HW - 1) * HW], _np.float32)[None, None, :, None], (P, TILES, 2, NH)).reshape(P, 128),
        "c_center": _np.eye(P, dtype=_np.float32) - same(C) / C,
        "c_mean": same(C) / C,
        "c_hmask": same(DH),
        "c_rank": _np.broadcast_to(_np.arange(8, 8 - EXP, -1, dtype=_np.float32)[None], (P, EXP)),
        "c_spread": spread,
    }
    skip = ("L0_tok_W_q", "L0_tok_W_k", "L0_tok_W_v")
    arrays = {k: _np.asarray(v) for k, v in inputs.items() if k not in skip}
    arrays |= {"wqT": _np.asarray(inputs["L0_tok_W_q"]).T, "wkT": _np.asarray(inputs["L0_tok_W_k"]).T, "wvT": _np.asarray(inputs["L0_tok_W_v"]).T}
    arrays |= {k: v.astype(_np.float32) for k, v in constants.items()}
    arrays = {k: _np.ascontiguousarray(v) for k, v in arrays.items()}
    nc = _bacc.Bacc("TRN2", target_bir_lowering=False, num_devices=1)
    a = {k: nc.dram_tensor(f"in_{k}", v.shape, _mybir.dt.from_np(v.dtype), kind="ExternalInput").ap() for k, v in arrays.items()}
    out = nc.dram_tensor("out_0", (nb, NQ, C), F32, kind="ExternalOutput").ap()
    build(nc, a, out)
    r = _run(nc, [{f"in_{k}": v for k, v in arrays.items()}], core_ids=[0])
    return r.results[0]["out_0"]
```

```python
import numpy as np
import concourse.bass as bass
from concourse import mybir
from contextlib import ExitStack

F32 = mybir.dt.float32
I32 = mybir.dt.int32
ALU = mybir.AluOpType
ACT = mybir.ActivationFunctionType
AX = mybir.AxisListType

C = 64
HW = 128
NPIX = HW * HW
GRID = 32
NQ = GRID * GRID
NH = 8
DH = C // NH
OH = 16
P = 128
TILES = NQ // P
GROUPS = 2 * TILES
CH = 16
NCH = HW // CH
RUNS = []
ROWS = []
for q in range(GRID):
    px = min((HW - 1) * q // (GRID - 1), HW - 2)
    if RUNS and px == RUNS[-1][2] + 4 * RUNS[-1][1]:
        RUNS[-1][1] += 1
    else:
        RUNS.append([q, 1, px])
for q in range(GRID):
    px = min((HW - 1) * q // (GRID - 1), HW - 2)
    assert px % CH < CH - 1, "a query's two rows lie in one chunk"
    if ROWS and ROWS[-1][0] == px // CH and px % CH == ROWS[-1][3] + 4 * ROWS[-1][2]:
        ROWS[-1][2] += 1
    else:
        ROWS.append([px // CH, q, 1, px % CH])
LN_EPS = 1e-5
GELU_2C = 2 * 0.7978845608028654
LAYERS = 4
FF = 4 * C
RH = C // 2
EXP = 6
HALF = NQ // 2
QK_SCALE = float(DH) ** -0.25
A_POOL = 3 * len(ROWS) + 3 * len(RUNS)
A_DVE = 28
B_DVE = GROUPS * 12
T_DVE = LAYERS * 11 + 21
SLOTS = GROUPS + 2
OFFSETS_PE = [(9, 1), (10, 1), (11, 1), (14, 1), (15, 1)]
OFFSETS_ACT = [(12, 0), (13, 0), (14, 2)]
TOWER_FIRST_DVE = [(2, 0), (1, 2)]
WEIGHT_LOADS = 10 + 8 + 3 + 3 + 113


def wait_if(eng, sem, value):
    if not isinstance(value, int) or value > 0:
        eng.wait_ge(sem, value)


def hold(eng, sem, value, turns):
    if not isinstance(value, int) or value > 0:
        eng.wait_ge(sem, value)
        eng.sem_inc(turns, 1)


class Steps:

    def __init__(self, eng, sem, per_round, round_):
        self.eng, self.sem, self.base, self.n, self.per = eng, sem, round_ * per_round, 0, per_round

    def done(self, ins):
        ins.then_inc(self.sem, 1)
        self.n += 1

    def wait(self):
        self.eng.wait_ge(self.sem, self.base + self.n)

    def link(self, ins):
        self.done(ins)
        self.wait()

    def close(self):
        assert self.n == self.per, (self.n, self.per)


def ln_steps(tag, pe, act, dve, shifted=False):
    pe += [f"{tag}.center{h}" for h in range(2)] + [f"{tag}.var{h}" for h in range(2)]
    act += [f"{tag}.square{h}" for h in range(2)] + [f"{tag}.rstd{h}" for h in range(2)]
    for h in range(2):
        dve += [f"{tag}.norm{h}"] + ([f"{tag}.shift{h}"] if shifted else [])


def tower_steps():
    pe, act, dve = [], [], []
    both = lambda name: [f"{name}{h}" for h in range(2)]
    pe += both("h_transposed")
    act += both("h_copied")
    ln_steps("in", pe, act, dve)
    for l in range(LAYERS):
        ln_steps(f"a{l}", pe, act, dve, True)
        pe += [f"{l}.{n}" for n in ("k0", "k1", "q0", "q1", "v0", "v1", "kT0", "kT1", "context", "qT0", "qT1", "out_weights", "out0", "out1")]
        act += [f"{l}.{n}" for n in ("k_exp0", "k_exp1", "q_exp0", "q_exp1", "v_copied0", "v_copied1", "kT_copied0", "kT_copied1", "qT_copied0", "qT_copied1")]
        dve += [f"{l}.{n}" for n in ("k_max", "q_shifted0", "q_shifted1", "q_ready0", "q_ready1", "context_ready", "out_weights_ready", "added0", "added1")]
        ln_steps(f"f{l}", pe, act, dve, True)
        pe += [f"{l}.up{2 * f + m}{h}" for f in range(2) for h in range(2) for m in range(2)] + both(f"{l}.down")
        act += [f"{l}.gelu{2 * f + m}{h}" for f in range(2) for h in range(2) for m in range(2)]
        dve += both(f"{l}.ff_added")
    dve += both("residual")
    ln_steps("m", pe, act, dve)
    pe += both("router_hidden") + ["logits"]
    act += both("router_relu") + ["expert_exp"]
    dve += ["logits_shifted", "top_ready", "weights_ready"]
    for e in range(EXP):
        pe += both(f"e{e}.first") + (["weights_transposed"] if e == 2 else []) + both(f"e{e}.second")
        act += both(f"e{e}.first_relu") + (["weights_copied"] if e == 2 else []) + both(f"e{e}.second_relu")
        if e == 1:
            act += ["second_exp"]
        if e >= 2:
            pe += both(f"e{e - 2}.weight")
    for e in (EXP - 2, EXP - 1):
        pe += both(f"e{e}.weight")
    for e in range(EXP):
        dve += both(f"e{e}.weighted")
    pe += both("final")
    act += both("final_copied")
    return {"pe": pe, "act": act, "dve": dve}


STEPS = tower_steps()
AT = {engine: {name: n + 1 for n, name in enumerate(names)} for engine, names in STEPS.items()}


class Signals:

    def __init__(self, engine, eng, sems, round_):
        self.engine, self.eng, self.sems, self.n, self.round = engine, eng, sems, 0, round_

    def mark(self, ins, name):
        assert STEPS[self.engine][self.n] == name, (STEPS[self.engine][self.n], name)
        ins.then_inc(self.sems[self.engine], 1)
        self.n += 1

    def wait(self, engine, name):
        self.eng.wait_ge(self.sems[engine], self.round * len(STEPS[engine]) + AT[engine][name])

    def wait_last_round(self, engine):
        self.eng.wait_ge(self.sems[engine], self.round * len(STEPS[engine]))

    def close(self):
        assert self.n == len(STEPS[self.engine])


def program(nc, PAIRS, x, out, w):
    x_v = x.rearrange("b c h w -> (b c) (h w)")
    out_v = out.rearrange("(i m) (t p) c -> i p t m c", m=2, p=P)
    scr = [nc.dram_tensor(f"scratch{n}", (2 * (HW - 1) * HW, 2 * C), F32).ap() for n in range(2)]
    with ExitStack() as ctx:
        sb = lambda name, shape, dt=F32: ctx.enter_context(nc.sbuf_tensor(name, shape, dt))
        pb = lambda name, shape: ctx.enter_context(nc.psum_tensor(name, shape, F32))
        sem = lambda name: ctx.enter_context(nc.semaphore(name))

        ident = sb("ident", [P, P])
        ref = sb("ref", [P, 256])
        wy = sb("wy", [P, GRID])
        base = sb("base", [P, GROUPS * NH])
        WQO = sb("WQO", [P, 160])
        WKV = sb("WKV", [P, 2, P])
        WO2 = sb("WO2", [P, P])
        bo1s = sb("bo1s", [P, 2, OH])
        lngs = sb("lngs", [P, OH])
        lnbs = sb("lnbs", [P, OH])
        bo2s = sb("bo2s", [P, 2 * NH])
        center = sb("center", [P, P])
        mean = sb("mean", [P, P])
        hmask = sb("hmask", [P, P])
        rank = sb("rank", [P, EXP])
        eps = sb("eps", [P, 1])
        Wq = sb("Wq", [P, LAYERS, P])
        Wk = sb("Wk", [P, LAYERS, P])
        Wv = sb("Wv", [P, LAYERS, P])
        Wo = sb("Wo", [P, LAYERS, P])
        W1 = sb("W1", [P, LAYERS, FF])
        W2 = sb("W2", [P, LAYERS, 2, C])
        cols = sb("cols", [P, 6, LAYERS])
        b1c = sb("b1c", [P, LAYERS, 2])
        Rw1 = sb("Rw1", [P, 2 * RH])
        rb1 = sb("rb1", [2 * RH, 1])
        Rw2 = sb("Rw2", [2 * RH, 2 * EXP])
        rb2 = sb("rb2", [P, EXP])
        E1w = sb("E1w", [P, EXP, P])
        E2w = sb("E2w", [P, EXP, P])
        E3w = sb("E3w", [P, EXP, P])
        eb1 = sb("eb1", [P, EXP])
        eb2 = sb("eb2", [P, EXP])
        eb3 = sb("eb3", [2 * EXP, P])
        spread = sb("spread", [2 * EXP, EXP, P])

        X = sb("X", [P, 2, CH, HW])
        T = sb("T", [P, 2, 2, CH + 1, C])
        V = sb("V", [P, GRID, HW])
        qf = sb("qf", [P, GRID, GRID])
        QO = sb("QO", [P, 2, TILES, 160])
        Z = sb("Z", [P, 256])
        Z2 = sb("Z2", [P, 256])
        Z3 = sb("Z3", [P, 256])
        st16 = sb("st16", [P, 2, GROUPS])
        rstd = sb("rstd", [P, GROUPS])
        HT = sb("HT", [P, 2, P])
        PI = sb("PI", [P, 256], I32)
        PF = sb("PF", [P, 256])
        FG = sb("FG", [P, 256, 2])
        W = sb("W", [P, 2, GROUPS * NH, 4])
        idx = sb("idx", [P, 2, GROUPS * NH], I32)
        idf = sb("idf", [P, GROUPS * NH])
        G = sb("G", [P, 2, NH, 4 * C])
        S = sb("S", [P, 2, NH * C])
        ST = sb("ST", [P, 4, P])
        PR = sb("PR", [P, NH * C])
        PV = sb("PV", [P, NH * C])
        sc = sb("sc", [P, 2, 64])
        ex = sb("ex", [P, 2, 64])
        mx = sb("mx", [P, NH])
        den = sb("den", [P, NH])
        rden = sb("rden", [P, NH])
        o8 = sb("o8", [P, C])
        HO = sb("HO", [P, GROUPS, C])
        HH = sb("HH", [P, NQ])
        XT = sb("XT", [P, NQ])
        SQ = sb("SQ", [P, NQ])
        R = sb("R", [P, NQ])
        HN = sb("HN", [P, NQ])
        ARENA = sb("ARENA", [P, EXP, NQ])
        tok_major = lambda n: ARENA[:, n, :].rearrange("p (t n) -> p t n", n=P)
        QE, KE, QT, KT, VT = tok_major(0), ARENA[:, 1, :], ARENA[:, 2, :], tok_major(3), tok_major(4)
        BIG = ARENA
        OT = sb("OT", [P, TILES, P])
        CT = sb("CT", [P, P])
        MM = sb("MM", [P, P])
        kmax = sb("kmax", [P, 4])
        kden = sb("kden", [P, 4])
        qmax = sb("qmax", [P, P])
        LG = sb("LG", [P, GROUPS * EXP])
        L2 = sb("L2", [P, GROUPS * EXP])
        L3 = sb("L3", [P, GROUPS * EXP])
        S1 = sb("S1", [P, GROUPS * EXP])
        t16 = sb("t16", [P, 8, GROUPS])
        WF = sb("WF", [2 * EXP, NQ])

        rowp = pb("rowp", [P, 4, P])
        stp = pb("stp", [P, 4, P])
        offp = stp[:, :, :].rearrange("p a b -> p (a b)")
        keyp = pb("keyp", [P, NH, C])
        valp = pb("valp", [P, NH, C])
        U = [pb(f"U{n}", [P, 2, HALF]) for n in range(2)]

        zeroed = sem("zeroed")
        w_loaded = sem("w_loaded")
        x_loaded = [sem(f"x_loaded{n}") for n in range(2)]
        rows_interpolated = sem("rows_interpolated")
        rows_transposed = sem("rows_transposed")
        rows_copied = sem("rows_copied")
        scratch_stored = [sem(f"scratch_stored{n}") for n in range(2)]
        scratch_ready = sem("scratch_ready")
        qf_ready = sem("qf_ready")
        qo_projected = sem("qo_projected")
        qo_copied = sem("qo_copied")
        var_ready = sem("var_ready")
        small_act = sem("small_act")
        gelu_arg_ready = sem("gelu_arg_ready")
        hidden_ready = sem("hidden_ready")
        hidden_transposed = sem("hidden_transposed")
        hidden_copied = sem("hidden_copied")
        offsets_projected = sem("offsets_projected")
        offsets_taken = sem("offsets_taken")
        points_ready = sem("points_ready")
        patches_gathered = [sem(f"patches_gathered{n}") for n in range(2)]
        patches_used = sem("patches_used")
        sampled_ready = sem("sampled_ready")
        sampled_transposed = sem("sampled_transposed")
        sampled_copied = sem("sampled_copied")
        keys_ready = sem("keys_ready")
        values_ready = sem("values_ready")
        keys_used = sem("keys_used")
        scores_ready = sem("scores_ready")
        probs_ready = sem("probs_ready")
        attended = sem("attended")
        out_stored = sem("out_stored")
        sp_turns = sem("sp_turns")
        pool_turns = sem("pool_turns")
        pool_a = sem("pool_a")
        dve_a = sem("dve_a")
        dve_b = sem("dve_b")
        dve_t = sem("dve_t")
        rstd_log = sem("rstd_log")
        done = {e: sem(f"tower_{e}") for e in ("pe", "act", "dve")}
        SMALL_ACT = 5

        block = ctx.enter_context(nc.Block())
        half = lambda t, h: t[:, HALF * h:HALF * h + HALF]
        tiles = lambda t, h: t[:, 4 * h:4 * h + 4, :]
        flat = lambda t: t.rearrange("p a b -> p (a b)")

        def run(eng, body):
            body(0, 0, None, None)
            body(1, 1, 0, None)
            body(2, 0, 1, 0)
            with eng.Fori(1, PAIRS // 2 - 1) as s:
                body(s * 2 + 1, 1, s * 2, s * 2 - 1)
                body(s * 2 + 2, 0, s * 2 + 1, s * 2)
            body(PAIRS - 1, 1, PAIRS - 2, PAIRS - 3)
            body(None, 0, PAIRS - 1, PAIRS - 2)
            body(None, 1, None, PAIRS - 1)

        def slots(stages, tower, tower_first=()):
            for g in range(SLOTS):
                for micro in range(4):
                    first = (g % 3, micro) in tower_first and g <= 3 * LAYERS
                    if tower is not None and first:
                        next(tower, None)
                    if stages is not None:
                        stages(g, micro)
                    if tower is not None and not first:
                        next(tower, None)

        @block.sync
        def _(sp):
            sp.wait_ge(zeroed, 14)
            n = 0

            def put(dst, src):
                nonlocal n
                sp.dma_start(dst, src).then_inc(w_loaded, 16)
                n += 1
            for m in range(2):
                r = slice(C * m, C * m + C)
                put(WQO[r, OH * m:OH * m + OH], w["L0_tok_W_o1"])
                put(WQO[r, 32 + C * m:32 + C * m + C], w["wqT"])
                put(WKV[r, 0, r], w["wkT"])
                put(WKV[r, 1, r], w["wvT"])
                put(bo1s[:, m, :], w["L0_tok_b_o1"].partition_broadcast(P))
            for g in range(P // OH):
                put(WO2[OH * g:OH * g + OH, OH * g:OH * g + OH], w["L0_tok_W_o2"])
            for dst, name in ((lngs, "ln_g"), (lnbs, "ln_b"), (bo2s, "b_o2")):
                put(dst[:, :], w[f"L0_tok_{name}"].partition_broadcast(P))
            for m in range(2):
                r = slice(C * m, C * m + C)
                for dst, src in ((Wq, w["L0_attn_Wq"]), (Wk, w["L0_attn_Wk"]), (Wv, w["L0_attn_Wv"]), (Wo, w["L0_attn_Wo"])):
                    put(dst[r, :, r], src.rearrange("l i o -> i l o"))
                put(W1[r, :, :], w["L0_attn_W1"].rearrange("l i o -> i l o"))
                for c, name in enumerate(("ln1_g", "ln1_b", "bo", "ln2_g", "ln2_b", "b2")):
                    for l in range(LAYERS):
                        put(cols[r, c, l:l + 1], w[f"L0_attn_{name}"][l, :].unsqueeze(1))
                put(Rw1[r, RH * m:RH * m + RH], w["L0_ffn_router_w1"])
                put(Rw2[RH * m:RH * m + RH, EXP * m:EXP * m + EXP], w["L0_ffn_router_w2"])
                put(rb1[RH * m:RH * m + RH, :], w["L0_ffn_router_b1"].unsqueeze(1))
                for dst, src in ((E1w, w["L0_ffn_expert_w1"]), (E2w, w["L0_ffn_expert_w2"]), (E3w, w["L0_ffn_expert_w3"])):
                    put(dst[r, :, r], src.rearrange("l i o -> i l o"))
                for e in range(EXP):
                    put(eb1[r, e:e + 1], w["L0_ffn_expert_b1"][e, :].unsqueeze(1))
                    put(eb2[r, e:e + 1], w["L0_ffn_expert_b2"][e, :].unsqueeze(1))
                put(eb3[EXP * m:EXP * m + EXP, r], w["L0_ffn_expert_b3"])
            for f in range(2):
                put(W2[:, :, f, :], w["L0_attn_W2"][:, P * f:P * f + P, :].rearrange("l i o -> i l o"))
                for l in range(LAYERS):
                    put(b1c[:, l, f:f + 1], w["L0_attn_b1"][l, P * f:P * f + P].unsqueeze(1))
            put(rb2[:, :], w["L0_ffn_router_b2"].partition_broadcast(P))
            for dst, name in ((ident, "c_ident"), (ref, "c_ref"), (wy, "c_wy"), (base, "c_base"), (center, "c_center"),
                              (mean, "c_mean"), (hmask, "c_hmask"), (rank, "c_rank")):
                put(dst[:, :], w[name])
            put(spread[:, :, :], w["c_spread"])
            assert n == WEIGHT_LOADS, n

            def load(i, k):
                hold(sp, rows_transposed, (i * NCH + k - 1) * 4, sp_turns)
                hold(sp, rows_interpolated, i * NCH + k - 1, sp_turns)
                sp.dma_start(X[:, k % 2, :, :], x_v[bass.ts(i, P), CH * HW * k:CH * HW * (k + 1)]
                             .rearrange("p (h w) -> p h w", w=HW)).then_inc(x_loaded[k % 2], 16)

            def store(i, b, k):
                hold(sp, rows_copied, i * 4 * NCH + 4 * k + 4, sp_turns)
                first = 1 if k == 0 else 0
                n = CH - first
                for m in range(2):
                    src = T[:, k % 2, m, first:first + n, :]
                    src = bass.AP(src.tensor, src.offset, [src.ap[0], [C, n], [1, 2 * C]])
                    row = m * (HW - 1) + CH * k - 1 + first
                    sp.dma_start(scr[b][row * HW:(row + n) * HW, :].rearrange("(h w) c -> w h c", w=HW), src)\
                        .then_inc(scratch_stored[k % 2], 16)

            def store_out(t):
                for h in range(2):
                    hold(sp, done["act"], t * len(STEPS["act"]) + AT["act"][f"final_copied{h}"], sp_turns)
                for m in range(2):
                    dst = out_v[t, :, :, m, :] if isinstance(t, int) else \
                        out_v[bass.ds(t, 1), :, :, m, :].rearrange("a p t c -> (a p) t c")
                    sp.dma_start(dst, OT[:, :, C * m:C * m + C]).then_inc(out_stored, 16)

            def body(i, b, j, t):
                if i is not None:
                    hold(sp, patches_used, (i - 1) * GROUPS, sp_turns)
                    for k in range(NCH):
                        store(i, b, k)
                        if k < NCH - 2:
                            load(i, k + 2)
                        elif not (isinstance(i, int) and i == PAIRS - 1):
                            load(i + 1, k + 2 - NCH)
                    for n in range(2):
                        hold(sp, scratch_stored[n], (i + 1) * 2 * 16 * (NCH // 2), sp_turns)
                    sp.sem_inc(scratch_ready, 1)
                if t is not None:
                    store_out(t)
            load(0, 0)
            load(0, 1)
            run(sp, body)
            sp.wait_ge(out_stored, PAIRS * 32)

        @block.gpsimd
        def _(pool):
            for t in (WQO, WKV, WO2, Wq, Wk, Wv, Wo, Rw1, Rw2, E1w, E2w, E3w, eb3):
                nc.gpsimd.memset(t[:], 0.0).then_inc(zeroed, 1)
            nc.gpsimd.memset(eps[:, :], LN_EPS).then_inc(zeroed, 1)

            g = nc.gpsimd
            pool.wait_ge(w_loaded, WEIGHT_LOADS * 16)

            def rows(c, i, k):
                hold(pool, x_loaded[k % 2], (i * (NCH // 2) + k // 2 + 1) * 16, pool_turns)
                runs = [r for r in ROWS if r[0] == k]
                for op in range(3):
                    for _, q0, cnt, r0 in runs:
                        upper = X[:, k % 2, r0:r0 + 4 * (cnt - 1) + 1:4, :]
                        lower = X[:, k % 2, r0 + 1:r0 + 4 * (cnt - 1) + 2:4, :]
                        o = V[:, q0:q0 + cnt, :]
                        if op == 0:
                            c.done(g.tensor_tensor(o, lower, upper, ALU.subtract))
                        if op == 1:
                            c.done(g.tensor_tensor(o, o, wy[:, q0:q0 + cnt].unsqueeze(2).broadcast_to([P, cnt, HW]), ALU.mult))
                        if op == 2:
                            c.done(g.tensor_tensor(o, o, upper, ALU.add))
                    c.wait()
                g.sem_inc(rows_interpolated, 1)

            def columns(c):
                for op in range(3):
                    for q0, cnt, p0 in RUNS:
                        left = V[:, :, p0:p0 + 4 * (cnt - 1) + 1:4]
                        right = V[:, :, p0 + 1:p0 + 4 * (cnt - 1) + 2:4]
                        o = qf[:, :, q0:q0 + cnt]
                        if op == 0:
                            c.done(g.tensor_tensor(o, right, left, ALU.subtract))
                        if op == 1:
                            c.done(g.tensor_tensor(o, o, wy[:, q0:q0 + cnt].unsqueeze(1).broadcast_to([P, GRID, cnt]), ALU.mult))
                        if op == 2:
                            c.done(g.tensor_tensor(o, o, left, ALU.add))
                    c.wait()
                g.sem_inc(qf_ready, 1)

            def gather(j, b, n):
                hold(pool, patches_used, j * GROUPS + n - 1, pool_turns)
                for p in range(NH):
                    pool.indirect_dma_start(
                        G[:, n % 2, p, :], None, scr[1 - b],
                        bass.IndirectOffsetOnAxis(ap=idx[:, 1 - b, n * NH + p:n * NH + p + 1], axis=0),
                    ).then_inc(patches_gathered[n % 2], 16)

            def body(i, b, j, t):
                c = None if i is None else Steps(pool, pool_a, A_POOL, i)
                if j is not None:
                    hold(pool, points_ready, j + 1, pool_turns)
                    hold(pool, scratch_ready, j + 1, pool_turns)
                for n in range(GROUPS):
                    if j is not None:
                        gather(j, b, n)
                    if i is not None and n < NCH:
                        rows(c, i, n)
                    if i is not None and n == NCH:
                        columns(c)
                if c:
                    c.close()
            run(pool, body)

        @block.scalar
        def _(act):
            sa = nc.scalar
            act.wait_ge(zeroed, 14)
            act.wait_ge(w_loaded, WEIGHT_LOADS * 16)

            def copy_rows(i, n):
                k, q = n // 4, n % 4
                b = k % 2
                if n == 0:
                    wait_if(act, scratch_stored[b], i * 2 * 16 * (NCH // 2))
                act.wait_ge(rows_transposed, i * 4 * NCH + n + 1)
                src = rowp[:, :, :].rearrange("p r (m c) -> p m r c", m=2)
                if q < 3 or k == NCH - 1:
                    sa.copy(T[:, b, :, 1 + 4 * q:5 + 4 * q, :], src).then_inc(rows_copied, 1)
                else:
                    sa.copy(T[:, b, :, 1 + 4 * q:5 + 4 * q, :], src)
                    wait_if(act, scratch_stored[1 - b], i * 2 * 16 * (NCH // 2) + 32 * ((k + 1) // 2))
                    sa.copy(T[:, 1 - b, :, 0, :], src[:, :, 3, :]).then_inc(rows_copied, 1)

            def offsets(i, part):
                if part == 0:
                    act.wait_ge(var_ready, i + 1)
                    sa.activation(rstd[:, :], st16[:, 1, :], ACT.Ln).then_inc(small_act, 1)
                    act.wait_ge(small_act, i * SMALL_ACT + 1)
                    sa.activation(rstd[:, :], rstd[:, :], ACT.Exp, scale=-0.5).then_inc(small_act, 1)
                if part == 1:
                    act.wait_ge(gelu_arg_ready, i + 1)
                    sa.activation(Z3[:, :], Z3[:, :], ACT.Exp).then_inc(small_act, 1)
                    act.wait_ge(small_act, i * SMALL_ACT + 3)
                    sa.activation(Z3[:, :], Z3[:, :], ACT.Ln, bias=1.0).then_inc(small_act, 1)
                    act.wait_ge(small_act, i * SMALL_ACT + 4)
                    sa.activation(Z3[:, :], Z3[:, :], ACT.Exp, scale=-1.0).then_inc(small_act, 1)
                if part == 2:
                    act.wait_ge(hidden_transposed, i + 1)
                    sa.copy(HT[:, :, :], offp[:, 0:256].rearrange("p (a b) -> p a b", a=2)).then_inc(hidden_copied, 1)

            def copy_qo(i, b, part):
                t0, n = 3 * part, min(3, TILES - 3 * part)
                act.wait_ge(qo_projected, i * 3 + part + 1)
                if part == 0:
                    wait_if(act, scores_ready, (i - 1) * GROUPS)
                sa.copy(QO[:, b, t0:t0 + n, :], offp[:, 0:160 * n].rearrange("p (t n) -> p t n", n=160)).then_inc(qo_copied, 1)

            def copy_sampled(j, g):
                act.wait_ge(sampled_transposed, j * GROUPS + g + 1)
                wait_if(act, values_ready, j * GROUPS + g)
                sa.copy(ST[:, :, :], stp[:, :, :]).then_inc(sampled_copied, 1)

            def probs(j, g):
                act.wait_ge(scores_ready, j * GROUPS + g + 1)
                sa.activation(ex[:, g % 2, :], sc[:, g % 2, :], ACT.Exp, scale=float(DH) ** -0.5).then_inc(probs_ready, 1)

            def tower(t):
                sg = Signals("act", act, done, t)
                logs = 0
                per = 2 * (2 * LAYERS + 2)

                def norm(tag):
                    nonlocal logs
                    for h in range(2):
                        sg.wait("pe", f"{tag}.center{h}")
                        sg.mark(sa.activation(half(SQ, h), U[0][:, h, :], ACT.Square), f"{tag}.square{h}")
                    yield
                    for h in range(2):
                        sg.wait("pe", f"{tag}.var{h}")
                        logs += 1
                        sa.activation(half(R, h), U[1][:, h, :], ACT.Ln, bias=eps[:, 0:1]).then_inc(rstd_log, 1)
                        act.wait_ge(rstd_log, t * per + logs)
                        sg.mark(sa.activation(half(R, h), half(R, h), ACT.Exp, scale=-0.5), f"{tag}.rstd{h}")
                    yield

                for h in range(2):
                    sg.wait("pe", f"h_transposed{h}")
                    sg.mark(sa.copy(half(HH, h), U[0][:, h, :]), f"h_copied{h}")
                yield
                yield from norm("in")
                for l in range(LAYERS):
                    yield from norm(f"a{l}")
                    sg.wait("dve", f"{l}.k_max")
                    for h in range(2):
                        sg.mark(sa.activation(half(KE, h), U[1][:, h, :], ACT.Exp, bias=kmax[:, 3:4], scale=QK_SCALE,
                                              accum_out=kden[:, h:h + 1]), f"{l}.k_exp{h}")
                    for h in range(2):
                        sg.wait("dve", f"{l}.q_shifted{h}")
                        sg.mark(sa.activation(tiles(QE, h), tiles(QE, h), ACT.Exp, scale=QK_SCALE), f"{l}.q_exp{h}")
                    yield
                    for what, dst, u in (("v", VT, 1), ("kT", KT, 0)):
                        for h in range(2):
                            sg.wait("pe", f"{l}.{what}{h}")
                            sg.mark(sa.copy(flat(tiles(dst, h)), U[u][:, h, :]), f"{l}.{what}_copied{h}")
                    yield
                    for h in range(2):
                        sg.wait("pe", f"{l}.qT{h}")
                        sg.mark(sa.copy(half(QT, h), U[1][:, h, :]), f"{l}.qT_copied{h}")
                    yield
                    yield
                    yield
                    yield from norm(f"f{l}")
                    for f in range(2):
                        for h in range(2):
                            for m in range(2):
                                c = 2 * f + m
                                sg.wait("pe", f"{l}.up{c}{h}")
                                sg.mark(sa.activation(half(BIG[:, c, :], h), U[m][:, h, :], ACT.Gelu, bias=b1c[:, l, f:f + 1]), f"{l}.gelu{c}{h}")
                        if f == 1:
                            act.preload_act_table_set("natural_log_exp_and_others")
                        yield
                    yield
                yield from norm("m")
                for h in range(2):
                    sg.wait("pe", f"router_hidden{h}")
                    sg.mark(sa.activation(QT[0:2 * RH, HALF * h:HALF * h + HALF], U[1][0:2 * RH, h, :], ACT.Relu, bias=rb1[:, 0:1]), f"router_relu{h}")
                yield
                sg.wait("dve", "logits_shifted")
                sg.mark(sa.activation(LG[:, :], LG[:, :], ACT.Exp), "expert_exp")
                yield
                for e in range(EXP):
                    for h in range(2):
                        sg.wait("pe", f"e{e}.first{h}")
                        sg.mark(sa.activation(half(SQ, h), U[0][:, h, :], ACT.Relu, bias=eb1[:, e:e + 1]), f"e{e}.first_relu{h}")
                    yield
                    if e == 2:
                        sg.wait("pe", "weights_transposed")
                        sg.mark(sa.copy(WF[:, :].rearrange("p (a b) -> p a b", a=2), U[1][0:2 * EXP, :, :]), "weights_copied")
                        yield
                    for h in range(2):
                        sg.wait("pe", f"e{e}.second{h}")
                        sg.mark(sa.activation(half(BIG[:, e, :], h), U[1][:, h, :], ACT.Relu, bias=eb2[:, e:e + 1]), f"e{e}.second_relu{h}")
                    if e == 1:
                        sg.wait("dve", "top_ready")
                        sg.mark(sa.activation(t16[:, 4, :], t16[:, 3, :], ACT.Exp), "second_exp")
                    yield
                yield
                wait_if(act, out_stored, t * 32)
                for h in range(2):
                    sg.wait("pe", f"final{h}")
                    sg.mark(sa.copy(flat(tiles(OT, h)), U[0][:, h, :]), f"final_copied{h}")
                sg.close()
                assert logs == per
                yield

            def body(i, b, j, t):
                def stages(g, micro):
                    n = 4 * g + micro
                    if i is not None:
                        if n < 4 * NCH:
                            copy_rows(i, n)
                        for part in range(3):
                            if (g, micro) == (OFFSETS_PE[part][0], 2):
                                copy_qo(i, b, part)
                        if (g, micro) in OFFSETS_ACT:
                            offsets(i, OFFSETS_ACT.index((g, micro)))
                    if j is not None:
                        if micro == 3 and 1 <= g <= GROUPS:
                            probs(j, g - 1)
                        if micro == 3 and g < GROUPS:
                            copy_sampled(j, g)
                slots(stages, None if t is None else tower(t))
            act.preload_act_table_set("natural_log_exp_and_others")
            run(act, body)

        @block.tensor
        def _(pe):
            mmul = lambda o, a, b, start=True, stop=True: nc.tensor.matmul(o, a, b, start=start, stop=stop)
            pe.wait_ge(w_loaded, WEIGHT_LOADS * 16)

            def transpose_rows(i, n):
                k, q = n // 4, n % 4
                if q == 0:
                    pe.wait_ge(x_loaded[k % 2], (i * (NCH // 2) + k // 2 + 1) * 16)
                wait_if(pe, rows_copied, i * 4 * NCH + n)
                for r in range(4):
                    ins = nc.tensor.transpose(rowp[:, r, :], X[:, k % 2, 4 * q + r, :], ident[:, :])
                ins.then_inc(rows_transposed, 1)

            def offsets(i, j, part):
                if j is not None and part < 3:
                    pe.wait_ge(sampled_copied, j * GROUPS + OFFSETS_PE[part][0])
                if part == 0:
                    pe.wait_ge(qf_ready, i + 1)
                if part in (1, 2):
                    pe.wait_ge(qo_copied, i * 3 + part)
                if part < 3:
                    for t in range(3 * part, min(3 * part + 3, TILES)):
                        ins = mmul(offp[:, 160 * (t % 3):160 * (t % 3) + 160], flat(qf[:, 4 * t:4 * t + 4, :]), WQO[:, :])
                    ins.then_inc(qo_projected, 1)
                if part == 3:
                    if j is not None:
                        pe.wait_ge(sampled_copied, j * GROUPS + OFFSETS_PE[part][0])
                    pe.wait_ge(hidden_ready, i + 1)
                    for a in range(2):
                        ins = nc.tensor.transpose(offp[:, P * a:P * a + P], Z[:, P * a:P * a + P], ident[:, :])
                    ins.then_inc(hidden_transposed, 1)
                if part == 4:
                    if j is not None:
                        pe.wait_ge(sampled_copied, j * GROUPS + OFFSETS_PE[part][0])
                    pe.wait_ge(hidden_copied, i + 1)
                    for a in range(2):
                        ins = mmul(offp[:, P * a:P * a + P], HT[:, a, :], WO2[:, :])
                    ins.then_inc(offsets_projected, 1)

            def transpose_sampled(i, j, g):
                pe.wait_ge(sampled_ready, j * GROUPS + g + 1)
                wait_if(pe, sampled_copied, j * GROUPS + g)
                if i is not None and (g, 1) in OFFSETS_PE:
                    part = OFFSETS_PE.index((g, 1))
                    if part < 3:
                        pe.wait_ge(qo_copied, i * 3 + part + 1)
                    elif part == 3:
                        pe.wait_ge(hidden_copied, i + 1)
                    else:
                        pe.wait_ge(offsets_taken, i + 1)
                for a in range(4):
                    ins = nc.tensor.transpose(stp[:, a, :], S[:, g % 2, P * a:P * a + P], ident[:, :])
                ins.then_inc(sampled_transposed, 1)

            def project(j, g, which, bank, free, ready):
                pe.wait_ge(sampled_copied, j * GROUPS + g + 1)
                wait_if(pe, free, j * GROUPS + g)
                for a in range(4):
                    ins = mmul(bank[:, 2 * a:2 * a + 2, :].rearrange("p k c -> p (k c)"), ST[:, a, :], WKV[:, which, :])
                ins.then_inc(ready, 1)

            def tower(t):
                sg = Signals("pe", pe, done, t)

                def norm(tag, src, ready):
                    for h in range(2):
                        sg.wait(*ready(h))
                        sg.mark(mmul(U[0][:, h, :], center[:, :], half(src, h)), f"{tag}.center{h}")
                    yield
                    for h in range(2):
                        sg.wait("act", f"{tag}.square{h}")
                        sg.mark(mmul(U[1][:, h, :], mean[:, :], half(SQ, h)), f"{tag}.var{h}")
                    yield

                pe.wait_ge(attended, (t + 1) * GROUPS)
                wait_if(pe, done["act"], t * len(STEPS["act"]))
                for h in range(2):
                    for a in range(4):
                        n = 2 * (4 * h + a)
                        ins = nc.tensor.transpose(U[0][:, h, P * a:P * a + P], flat(HO[:, n:n + 2, :]), ident[:, :])
                    sg.mark(ins, f"h_transposed{h}")
                yield
                yield from norm("in", HH, lambda h: ("act", f"h_copied{h}"))
                for l in range(LAYERS):
                    yield from norm(f"a{l}", XT, lambda h: ("dve", f"in.norm{h}" if l == 0 else f"{l - 1}.ff_added{h}"))
                    for h in range(2):
                        sg.wait("dve", f"a{l}.shift{h}")
                        sg.mark(mmul(U[1][:, h, :], Wk[:, l, :], half(HN, h)), f"{l}.k{h}")
                    for h in range(2):
                        for a in range(4):
                            ins = mmul(U[0][:, h, P * a:P * a + P], HN[:, P * (4 * h + a):P * (4 * h + a) + P], Wq[:, l, :])
                        sg.mark(ins, f"{l}.q{h}")
                    yield
                    for h in range(2):
                        sg.wait("act", f"{l}.k_exp{h}")
                        for a in range(4):
                            ins = mmul(U[1][:, h, P * a:P * a + P], HN[:, P * (4 * h + a):P * (4 * h + a) + P], Wv[:, l, :])
                        sg.mark(ins, f"{l}.v{h}")
                    for h in range(2):
                        sg.wait("dve", f"{l}.q_shifted{h}")
                        for a in range(4):
                            ins = nc.tensor.transpose(U[0][:, h, P * a:P * a + P], KE[:, P * (4 * h + a):P * (4 * h + a) + P], ident[:, :])
                        sg.mark(ins, f"{l}.kT{h}")
                    yield
                    for a in range(TILES):
                        if a % 4 == 0:
                            sg.wait("act", f"{l}.kT_copied{a // 4}")
                        ins = mmul(U[0][:, 0, 0:P], VT[:, a, :], KT[:, a, :], start=a == 0, stop=a == TILES - 1)
                    sg.mark(ins, f"{l}.context")
                    for h in range(2):
                        sg.wait("dve", f"{l}.q_ready{h}")
                        for a in range(4):
                            ins = nc.tensor.transpose(U[1][:, h, P * a:P * a + P], QE[:, 4 * h + a, :], ident[:, :])
                        sg.mark(ins, f"{l}.qT{h}")
                    yield
                    sg.wait("dve", f"{l}.context_ready")
                    sg.mark(mmul(U[0][:, 1, 0:P], CT[:, :], Wo[:, l, :]), f"{l}.out_weights")
                    yield
                    sg.wait("dve", f"{l}.out_weights_ready")
                    for h in range(2):
                        sg.wait("act", f"{l}.qT_copied{h}")
                        sg.mark(mmul(U[1][:, h, :], MM[:, :], half(QT, h)), f"{l}.out{h}")
                    yield
                    yield from norm(f"f{l}", XT, lambda h: ("dve", f"{l}.added{h}"))
                    for f in range(2):
                        for h in range(2):
                            for m in range(2):
                                c = 2 * f + m
                                if f == 0:
                                    sg.wait("dve", f"f{l}.shift{h}")
                                else:
                                    sg.wait("act", f"{l}.gelu{m}{h}")
                                sg.mark(mmul(U[m][:, h, :], W1[C * m:C * m + C, l, P * f:P * f + P],
                                             HN[C * m:C * m + C, HALF * h:HALF * h + HALF]), f"{l}.up{c}{h}")
                        yield
                    for h in range(2):
                        sg.wait("act", f"{l}.gelu3{h}")
                        for f in range(2):
                            for m in range(2):
                                ins = mmul(U[0][C * m:C * m + C, h, :], W2[:, l, f, :], half(BIG[:, 2 * f + m, :], h), start=f == 0, stop=f == 1)
                        sg.mark(ins, f"{l}.down{h}")
                    yield
                yield from norm("m", HH, lambda h: ("dve", f"residual{h}"))
                for h in range(2):
                    sg.wait("dve", f"m.norm{h}")
                    sg.mark(mmul(U[1][0:2 * RH, h, :], Rw1[:, :], half(HN, h)), f"router_hidden{h}")
                yield
                sg.wait("act", "router_relu1")
                for a in range(TILES):
                    ins = mmul(U[0][:, 0, 2 * EXP * a:2 * EXP * a + 2 * EXP], QT[0:2 * RH, P * a:P * a + P], Rw2[:, :])
                sg.mark(ins, "logits")
                yield

                def weight(e, u):
                    for h in range(2):
                        sg.mark(mmul(U[u][:, h, :], spread[:, e, :], half(WF, h)), f"e{e}.weight{h}")

                for e in range(EXP):
                    for h in range(2):
                        if e == 0:
                            sg.wait("dve", "logits_shifted")
                        if e >= 3:
                            sg.wait("dve", f"e{e - 3}.weighted{h}")
                        sg.mark(mmul(U[0][:, h, :], E1w[:, e, :], half(HN, h)), f"e{e}.first{h}")
                    yield
                    if e == 2:
                        sg.wait("dve", "weights_ready")
                        sg.wait("act", "e1.second_relu1")
                        for a in range(TILES):
                            ins = nc.tensor.transpose(U[1][0:2 * EXP, a // 4, P * (a % 4):P * (a % 4) + P], L3[:, 2 * EXP * a:2 * EXP * a + 2 * EXP], ident[:, :])
                        sg.mark(ins, "weights_transposed")
                        yield
                        sg.wait("act", "weights_copied")
                    for h in range(2):
                        sg.wait("act", f"e{e}.first_relu{h}")
                        sg.mark(mmul(U[1][:, h, :], E2w[:, e, :], half(SQ, h)), f"e{e}.second{h}")
                    if e >= 2:
                        weight(e - 2, 0)
                    yield
                sg.wait("act", f"e{EXP - 1}.second_relu1")
                weight(EXP - 2, 1)
                sg.wait("dve", f"e{EXP - 3}.weighted1")
                weight(EXP - 1, 0)
                yield
                for h in range(2):
                    sg.wait("dve", f"e{EXP - 1}.weighted{h}")
                    for a in range(4):
                        tok = slice(P * (4 * h + a), P * (4 * h + a) + P)
                        o = U[0][:, h, P * a:P * a + P]
                        mmul(o, HH[:, tok], ident[:, :], True, False)
                        for e in range(EXP):
                            mmul(o, BIG[:, e, tok], E3w[:, e, :], False, False)
                        ins = mmul(o, WF[:, tok], eb3[:, :], False, True)
                    sg.mark(ins, f"final{h}")
                sg.close()
                yield

            def body(i, b, j, t):
                def stages(g, micro):
                    if i is not None:
                        if 4 * g + micro < 4 * NCH:
                            transpose_rows(i, 4 * g + micro)
                        if (g, micro) in OFFSETS_PE:
                            offsets(i, j, OFFSETS_PE.index((g, micro)))
                    if j is not None:
                        if micro == 1 and 1 <= g <= GROUPS:
                            project(j, g - 1, 0, keyp, keys_used, keys_ready)
                        if micro == 2 and 1 <= g <= GROUPS:
                            project(j, g - 1, 1, valp, attended, values_ready)
                        if micro == 3 and g < GROUPS:
                            transpose_sampled(i, j, g)
                slots(stages, None if t is None else tower(t))
            run(pe, body)

        @block.vector
        def _(dve):
            v = nc.vector
            dve.wait_ge(w_loaded, WEIGHT_LOADS * 16)
            g16 = lambda t: t[:, :].rearrange("p (g k) -> p g k", k=OH)
            over_groups = lambda t: t[:, :].unsqueeze(1).broadcast_to([P, GROUPS, OH])

            def hidden_norm(c, i, b):
                dve.wait_ge(qo_copied, i * 3 + 3)
                c.link(v.tensor_tensor(Z[:, :].rearrange("p (t n) -> p t n", n=32), QO[:, b, :, 0:32],
                                       flat(bo1s[:, :, :]).unsqueeze(1).broadcast_to([P, TILES, 32]), ALU.add))
                c.link(v.tensor_reduce(st16[:, 0, :], g16(Z), AX.X, ALU.add))
                c.link(v.scalar_tensor_tensor(g16(Z), st16[:, 0, :].unsqueeze(2).broadcast_to([P, GROUPS, OH]), -1.0 / OH,
                                              g16(Z), ALU.mult, ALU.add))
                c.link(v.tensor_tensor(Z2[:, :], Z[:, :], Z[:, :], ALU.mult))
                c.link(v.tensor_reduce(st16[:, 1, :], g16(Z2), AX.X, ALU.add))
                c.link(v.tensor_scalar(st16[:, 1, :], st16[:, 1, :], 1.0 / OH, LN_EPS, ALU.mult, ALU.add))
                v.sem_inc(var_ready, 1)

            def gelu_argument(c, i):
                dve.wait_ge(small_act, i * SMALL_ACT + 2)
                c.link(v.tensor_tensor(g16(Z), g16(Z), rstd[:, :].unsqueeze(2).broadcast_to([P, GROUPS, OH]), ALU.mult))
                c.link(v.tensor_tensor(g16(Z), g16(Z), over_groups(lngs), ALU.mult))
                c.link(v.tensor_tensor(g16(Z), g16(Z), over_groups(lnbs), ALU.add))
                c.link(v.tensor_tensor(Z2[:, :], Z[:, :], Z[:, :], ALU.mult))
                c.link(v.tensor_scalar(Z2[:, :], Z2[:, :], 0.044715 * GELU_2C, GELU_2C, ALU.mult, ALU.add))
                c.link(v.tensor_tensor(Z3[:, :], Z2[:, :], Z[:, :], ALU.mult))
                c.link(v.tensor_scalar(Z3[:, :], Z3[:, :], 40.0, None, ALU.min))
                v.sem_inc(gelu_arg_ready, 1)

            def gelu(c, i):
                dve.wait_ge(small_act, i * SMALL_ACT + 5)
                c.link(v.tensor_scalar(Z3[:, :], Z3[:, :], -1.0, 1.0, ALU.mult, ALU.add))
                c.link(v.tensor_tensor(Z[:, :], Z[:, :], Z3[:, :], ALU.mult))
                v.sem_inc(hidden_ready, 1)

            def points(c, i, b):
                dve.wait_ge(offsets_projected, i + 1)
                c.link(v.tensor_tensor(g16(Z), offp[:, 0:256].rearrange("p (g k) -> p g k", k=OH), over_groups(bo2s), ALU.add))
                v.sem_inc(offsets_taken, 1)
                c.link(v.scalar_tensor_tensor(Z[:, :], Z[:, :], 4.0, ref[:, :], ALU.mult, ALU.add))
                c.link(v.tensor_scalar(Z[:, :], Z[:, :], 0.0, float(HW - 1), ALU.max, ALU.min))
                c.link(v.tensor_copy(PI[:, :], Z[:, :]))
                c.link(v.tensor_copy(PF[:, :], PI[:, :]))
                c.link(v.tensor_tensor(Z2[:, :], PF[:, :], Z[:, :], ALU.is_gt))
                c.link(v.tensor_tensor(PF[:, :], PF[:, :], Z2[:, :], ALU.subtract))
                c.link(v.tensor_scalar(PF[:, :], PF[:, :], float(HW - 2), None, ALU.min))
                pf = PF[:, :].rearrange("p (n a) -> p n a", a=2)
                c.done(v.scalar_tensor_tensor(idf[:, :], pf[:, :, 1], float(HW), pf[:, :, 0], ALU.mult, ALU.add))
                c.link(v.tensor_tensor(FG[:, :, 1], Z[:, :], PF[:, :], ALU.subtract))
                c.done(v.tensor_tensor(idx[:, b, :], idf[:, :], base[:, :], ALU.add))
                c.link(v.tensor_scalar(FG[:, :, 0], FG[:, :, 1], -1.0, 1.0, ALU.mult, ALU.add))
                v.sem_inc(points_ready, 1)
                fg = FG[:, :, :].rearrange("p (n a) w -> p n a w", a=2)
                c.link(v.tensor_tensor(W[:, b, :, :].rearrange("p n (x y) -> p n x y", x=2),
                                       fg[:, :, 0, :].unsqueeze(3).broadcast_to([P, GROUPS * NH, 2, 2]),
                                       fg[:, :, 1, :].unsqueeze(2).broadcast_to([P, GROUPS * NH, 2, 2]), ALU.mult))

            def weigh(c, j, b, g):
                dve.wait_ge(patches_gathered[g % 2], (j * (GROUPS // 2) + g // 2 + 1) * NH * 16)
                patches = G[:, g % 2, :, :].rearrange("p k (x c) -> p (k x) c", c=C)
                wgt = W[:, b, g * NH:g * NH + NH, :].rearrange("p k x -> p (k x)").unsqueeze(2).broadcast_to([P, 4 * NH, C])
                c.done(v.tensor_tensor(patches, patches, wgt, ALU.mult))

            def sample(c, j, g):
                n = g % 2
                c.wait()
                c.link(v.tensor_tensor(G[:, n, :, 0:2 * C], G[:, n, :, 0:2 * C], G[:, n, :, 2 * C:4 * C], ALU.add))
                wait_if(dve, sampled_transposed, j * GROUPS + g - 1)
                c.link(v.tensor_tensor(S[:, n, :].rearrange("p (k c) -> p k c", c=C), G[:, n, :, 0:C], G[:, n, :, C:2 * C], ALU.add))
                v.sem_inc(patches_used, 1)
                v.sem_inc(sampled_ready, 1)

            def scores(c, j, b, g):
                t, m, n = g // 2, g % 2, g % 2
                dve.wait_ge(keys_ready, j * GROUPS + g + 1)
                q = QO[:, b, t, 32 + C * m:32 + C * m + C].unsqueeze(1).broadcast_to([P, NH, C])
                c.link(v.tensor_tensor(PR[:, :].rearrange("p (k c) -> p k c", c=C), keyp[:, :, :], q, ALU.mult))
                v.sem_inc(keys_used, 1)
                c.link(v.tensor_reduce(sc[:, n, :], PR[:, :].rearrange("p (s d) -> p s d", d=DH), AX.X, ALU.add))
                c.link(v.tensor_reduce(mx[:, :], sc[:, n, :].rearrange("p (k h) -> p h k", h=NH), AX.X, ALU.max))
                s3 = sc[:, n, :].rearrange("p (k h) -> p k h", h=NH)
                c.link(v.tensor_tensor(s3, s3, mx[:, :].unsqueeze(1).broadcast_to([P, NH, NH]), ALU.subtract))
                v.sem_inc(scores_ready, 1)

            def attend(c, j, g):
                n = g % 2
                dve.wait_ge(probs_ready, j * GROUPS + g + 1)
                dve.wait_ge(values_ready, j * GROUPS + g + 1)
                e3 = ex[:, n, :].rearrange("p (k h) -> p k h", h=NH)
                c.done(v.tensor_reduce(den[:, :], e3.rearrange("p k h -> p h k"), AX.X, ALU.add))
                c.link(v.tensor_tensor(PV[:, :].rearrange("p (k h d) -> p k h d", h=NH, d=DH),
                                       valp[:, :, :].rearrange("p k (h d) -> p k h d", d=DH),
                                       e3.unsqueeze(3).broadcast_to([P, NH, NH, DH]), ALU.mult))
                c.done(v.reciprocal(rden[:, :], den[:, :]))
                c.link(v.tensor_reduce(o8[:, :], PV[:, :].rearrange("p (k c) -> p c k", c=C), AX.X, ALU.add))
                if g == 0:
                    wait_if(dve, done["pe"], (j - 1) * len(STEPS["pe"]) + 2 if not (isinstance(j, int) and j == 0) else 0)
                c.link(v.tensor_tensor(HO[:, g, :].rearrange("p (h d) -> p h d", d=DH), o8[:, :].rearrange("p (h d) -> p h d", d=DH),
                                       rden[:, :].unsqueeze(2).broadcast_to([P, NH, DH]), ALU.mult))
                v.sem_inc(attended, 1)

            def tower(t):
                sg = Signals("dve", dve, done, t)
                c = Steps(dve, dve_t, T_DVE, t)

                def norm(tag, dst, gain=None, bias=None):
                    yield
                    for h in range(2):
                        sg.wait("act", f"{tag}.rstd{h}")
                        if gain is None:
                            ins = v.tensor_tensor(half(dst, h), U[0][:, h, :], half(R, h), ALU.mult)
                        else:
                            ins = v.scalar_tensor_tensor(half(dst, h), U[0][:, h, :], gain, half(R, h), ALU.mult, ALU.mult)
                        sg.mark(ins, f"{tag}.norm{h}")
                        if bias is not None:
                            sg.wait("dve", f"{tag}.norm{h}")
                            sg.mark(v.tensor_scalar(half(dst, h), half(dst, h), bias, None, ALU.add), f"{tag}.shift{h}")
                    yield

                yield
                yield from norm("in", XT)
                for l in range(LAYERS):
                    yield from norm(f"a{l}", HN, cols[:, 0, l:l + 1], cols[:, 1, l:l + 1])
                    for h in range(2):
                        sg.wait("pe", f"{l}.k{h}")
                        c.done(v.tensor_reduce(kmax[:, h:h + 1], U[1][:, h, :], AX.X, ALU.max))
                    c.wait()
                    c.link(v.tensor_reduce(kmax[:, 2:3], kmax[:, 0:2], AX.X, ALU.max))
                    sg.mark(v.tensor_scalar(kmax[:, 3:4], kmax[:, 2:3], -QK_SCALE, None, ALU.mult), f"{l}.k_max")
                    for h in range(2):
                        sg.wait("pe", f"{l}.q{h}")
                        qm = qmax[:, C * h:C * h + C]
                        u = U[0][:, h, :].rearrange("p (g d) -> p g d", d=DH)
                        c.link(v.tensor_reduce(qm, u, AX.X, ALU.max))
                        sg.mark(v.tensor_tensor(flat(tiles(QE, h)).rearrange("p (g d) -> p g d", d=DH), u,
                                                qm.unsqueeze(2).broadcast_to([P, C, DH]), ALU.subtract), f"{l}.q_shifted{h}")
                    yield
                    for h in range(2):
                        sg.wait("act", f"{l}.q_exp{h}")
                        qm = qmax[:, C * h:C * h + C]
                        q = flat(tiles(QE, h)).rearrange("p (g d) -> p g d", d=DH)
                        c.link(v.tensor_reduce(qm, q, AX.X, ALU.add))
                        c.link(v.reciprocal(qm, qm))
                        sg.mark(v.tensor_tensor(q, q, qm.unsqueeze(2).broadcast_to([P, C, DH]), ALU.mult), f"{l}.q_ready{h}")
                    yield
                    sg.wait("pe", f"{l}.context")
                    sg.mark(v.tensor_tensor(CT[:, :], U[0][:, 0, 0:P], hmask[:, :], ALU.mult), f"{l}.context_ready")
                    yield
                    c.link(v.tensor_tensor(kden[:, 2:3], kden[:, 0:1], kden[:, 1:2], ALU.add))
                    c.link(v.reciprocal(kden[:, 3:4], kden[:, 2:3]))
                    sg.wait("pe", f"{l}.out_weights")
                    sg.mark(v.tensor_scalar(MM[:, :], U[0][:, 1, 0:P], kden[:, 3:4], None, ALU.mult), f"{l}.out_weights_ready")
                    yield
                    for h in range(2):
                        sg.wait("pe", f"{l}.out{h}")
                        sg.mark(v.scalar_tensor_tensor(half(XT, h), U[1][:, h, :], cols[:, 2, l:l + 1], half(XT, h), ALU.add, ALU.add), f"{l}.added{h}")
                    yield
                    yield from norm(f"f{l}", HN, cols[:, 3, l:l + 1], cols[:, 4, l:l + 1])
                    yield
                    yield
                    for h in range(2):
                        sg.wait("pe", f"{l}.down{h}")
                        sg.mark(v.scalar_tensor_tensor(half(XT, h), U[0][:, h, :], cols[:, 5, l:l + 1], half(XT, h), ALU.add, ALU.add), f"{l}.ff_added{h}")
                    if l == LAYERS - 1:
                        for h in range(2):
                            sg.wait("dve", f"{l}.ff_added{h}")
                            sg.mark(v.tensor_tensor(half(HH, h), half(HH, h), half(XT, h), ALU.add), f"residual{h}")
                    yield
                yield from norm("m", HN)
                yield
                g6 = lambda t: t[:, :].rearrange("p (g e) -> p g e", e=EXP)
                bc = lambda t: t.unsqueeze(2).broadcast_to([P, GROUPS, EXP])
                row = lambda t: t[:, :].unsqueeze(1).broadcast_to([P, GROUPS, EXP])
                s16 = lambda n: t16[:, n, :]
                sg.wait("pe", "logits")
                c.link(v.tensor_tensor(g6(LG), U[0][:, 0, 0:GROUPS * EXP].rearrange("p (g e) -> p g e", e=EXP), row(rb2), ALU.add))
                c.link(v.tensor_reduce(s16(0), g6(LG), AX.X, ALU.max))
                sg.mark(v.tensor_tensor(g6(LG), g6(LG), bc(s16(0)), ALU.subtract), "logits_shifted")
                yield
                sg.wait("act", "expert_exp")
                c.link(v.tensor_reduce(s16(0), g6(LG), AX.X, ALU.add))
                c.link(v.reciprocal(s16(0), s16(0)))
                c.link(v.tensor_tensor(g6(LG), g6(LG), bc(s16(0)), ALU.mult))
                for k, (src, sel) in enumerate(((LG, S1), (L2, L3))):
                    if k == 1:
                        yield
                        c.link(v.scalar_tensor_tensor(L2[:, :], S1[:, :], -2.0, LG[:, :], ALU.mult, ALU.add))
                    c.link(v.tensor_reduce(s16(1 + k), g6(src), AX.X, ALU.max))
                    c.link(v.tensor_tensor(g6(sel), g6(src), bc(s16(1 + k)), ALU.is_equal))
                    c.link(v.tensor_tensor(g6(sel), g6(sel), row(rank), ALU.mult))
                    c.link(v.tensor_reduce(s16(5), g6(sel), AX.X, ALU.max))
                    c.link(v.tensor_tensor(g6(sel), g6(sel), bc(s16(5)), ALU.is_equal))
                sg.mark(v.tensor_tensor(s16(3), s16(2), s16(1), ALU.subtract), "top_ready")
                yield
                yield
                sg.wait("act", "second_exp")
                c.link(v.tensor_scalar(s16(6), s16(4), 1.0, None, ALU.add))
                c.link(v.reciprocal(s16(6), s16(6)))
                c.link(v.tensor_tensor(s16(7), s16(4), s16(6), ALU.mult))
                c.link(v.tensor_tensor(g6(S1), g6(S1), bc(s16(6)), ALU.mult))
                c.link(v.tensor_tensor(g6(L3), g6(L3), bc(s16(7)), ALU.mult))
                sg.mark(v.tensor_tensor(L3[:, :], L3[:, :], S1[:, :], ALU.add), "weights_ready")
                yield

                def weighted(e, u):
                    for h in range(2):
                        sg.wait("act", f"e{e}.second_relu{h}")
                        sg.wait("pe", f"e{e}.weight{h}")
                        o = half(BIG[:, e, :], h)
                        sg.mark(v.tensor_tensor(o, o, U[u][:, h, :], ALU.mult), f"e{e}.weighted{h}")

                yield
                for e in range(2, EXP):
                    yield
                    weighted(e - 2, 0)
                    yield
                weighted(EXP - 2, 1)
                weighted(EXP - 1, 0)
                yield
                sg.close()
                c.close()
                yield

            def body(i, b, j, t):
                ca = None if i is None else Steps(dve, dve_a, A_DVE, i)
                cb = None if j is None else Steps(dve, dve_b, B_DVE, j)

                def stages(g, micro):
                    if j is not None:
                        if micro == 0 and g >= 2:
                            attend(cb, j, g - 2)
                        if micro == 0 and g < GROUPS:
                            weigh(cb, j, 1 - b, g)
                        if micro == 1 and g < GROUPS:
                            sample(cb, j, g)
                        if micro == 2 and 1 <= g <= GROUPS:
                            scores(cb, j, 1 - b, g - 1)
                    if i is not None:
                        if (g, micro) == (11, 3):
                            hidden_norm(ca, i, b)
                        if (g, micro) == (12, 2):
                            gelu_argument(ca, i)
                        if (g, micro) == (13, 1):
                            gelu(ca, i)
                        if (g, micro) == (15, 2):
                            points(ca, i, b)
                slots(stages, None if t is None else tower(t), TOWER_FIRST_DVE)
                if ca:
                    ca.close()
                if cb:
                    cb.close()
            run(dve, body)


def kernel(**inputs):
    import numpy as _np
    import concourse.bacc as _bacc
    from concourse import mybir as _mybir
    from concourse.bass_utils import run_bass_kernel_spmd as _run

    nb = inputs["x"].shape[0]
    lin = _np.linspace(-1.0, 1.0, GRID, dtype=_np.float32)
    px = (lin + _np.float32(1)) * _np.float32(0.5) * _np.float32(HW - 1)
    tok = _np.arange(NQ)
    xy = _np.stack([px[tok % GRID], px[tok // GRID]], -1).reshape(TILES, P, 2).transpose(1, 0, 2)
    left = _np.minimum(_np.floor(px), HW - 2)
    same = lambda n: _np.equal.outer(_np.arange(P) // n, _np.arange(P) // n).astype(_np.float32)
    spread = _np.zeros((2 * EXP, EXP, P), _np.float32)
    for m in range(2):
        for e in range(EXP):
            spread[EXP * m + e, e, C * m:C * m + C] = 1
    constants = {
        "c_ident": _np.eye(P, dtype=_np.float32),
        "c_ref": _np.broadcast_to(xy[:, :, None, None, :], (P, TILES, 2, NH, 2)).reshape(P, 256),
        "c_wy": _np.broadcast_to((px - left)[None], (P, GRID)),
        "c_base": _np.broadcast_to(_np.array([0, (HW - 1) * HW], _np.float32)[None, None, :, None], (P, TILES, 2, NH)).reshape(P, 128),
        "c_center": _np.eye(P, dtype=_np.float32) - same(C) / C,
        "c_mean": same(C) / C,
        "c_hmask": same(DH),
        "c_rank": _np.broadcast_to(_np.arange(8, 8 - EXP, -1, dtype=_np.float32)[None], (P, EXP)),
        "c_spread": spread,
    }
    skip = ("L0_tok_W_q", "L0_tok_W_k", "L0_tok_W_v")
    arrays = {k: _np.asarray(v) for k, v in inputs.items() if k not in skip}
    arrays |= {"wqT": _np.asarray(inputs["L0_tok_W_q"]).T, "wkT": _np.asarray(inputs["L0_tok_W_k"]).T, "wvT": _np.asarray(inputs["L0_tok_W_v"]).T}
    arrays |= {k: v.astype(_np.float32) for k, v in constants.items()}
    arrays = {k: _np.ascontiguousarray(v) for k, v in arrays.items()}
    nc = _bacc.Bacc("TRN2", target_bir_lowering=False, num_devices=1)
    a = {k: nc.dram_tensor(f"in_{k}", v.shape, _mybir.dt.from_np(v.dtype), kind="ExternalInput").ap() for k, v in arrays.items()}
    out = nc.dram_tensor("out_0", (nb, NQ, C), F32, kind="ExternalOutput").ap()
    program(nc, nb // 2, a["x"], out, a)
    r = _run(nc, [{f"in_{k}": v for k, v in arrays.items()}], core_ids=[0])
    return r.results[0]["out_0"]
```

```python
import numpy as np
import concourse.bass as bass
from concourse import mybir
from contextlib import ExitStack

F32 = mybir.dt.float32
I32 = mybir.dt.int32
BF16 = mybir.dt.bfloat16
ALU = mybir.AluOpType
ACT = mybir.ActivationFunctionType
AX = mybir.AxisListType

C = 64
HW = 128
NPIX = HW * HW
GRID = 32
NQ = GRID * GRID
NH = 8
DH = C // NH
OH = 16
P = 128
TILES = NQ // P
GROUPS = 2 * TILES
CH = 16
NCH = HW // CH
RUNS = []
ROWS = []
for q in range(GRID):
    px = min((HW - 1) * q // (GRID - 1), HW - 2)
    if RUNS and px == RUNS[-1][2] + 4 * RUNS[-1][1]:
        RUNS[-1][1] += 1
    else:
        RUNS.append([q, 1, px])
for q in range(GRID):
    px = min((HW - 1) * q // (GRID - 1), HW - 2)
    assert px % CH < CH - 1, "a query's two rows lie in one chunk"
    if ROWS and ROWS[-1][0] == px // CH and px % CH == ROWS[-1][3] + 4 * ROWS[-1][2]:
        ROWS[-1][2] += 1
    else:
        ROWS.append([px // CH, q, 1, px % CH])
LN_EPS = 1e-5
GELU_2C = 2 * 0.7978845608028654
LAYERS = 4
FF = 4 * C
RH = C // 2
EXP = 6
HALF = NQ // 2
SPLIT = 3 * 2 * EXP
QK_SCALE = float(DH) ** -0.25
A_POOL = 3 * len(ROWS) + 3 * len(RUNS) + 17
A_DVE = 15
B_DVE = GROUPS * 12
T_DVE = LAYERS * 11 + 28
SLOTS = GROUPS + 2
OFFSETS_PE = [(9, 0), (9, 2), (10, 0), (14, 1), (14, 3)]
OFFSETS_ACT = [(12, 2), (13, 2), (14, 2), (15, 0)]
QO_COPIES = [(9, 1), (9, 3), (10, 1)]
PARTS_DVE = {
    "project": {(0, 0): ["weigh0"], (1, 0): ["attend2"], (3, 0): ["sample0"]},
    "mix": {(0, 1): ["scores2"], (1, 1): ["attend2"], (3, 0): ["scores1"], (3, 1): ["weigh0", "sample0"]},
    "feed": {(0, 0): ["weigh0"], (1, 0): ["attend2", "sample0"], (2, 1): ["scores1"]},
    "route": {(0, 0): ["attend2"], (1, 1): ["scores1"]},
    "decide": {(0, 1): ["attend2"], (1, 1): ["weigh0"], (2, 1): ["sample0"], (3, 1): ["scores1"]},
    "tail": {(0, 0): ["weigh0"], (0, 1): ["attend2"], (1, 1): ["sample0"]},
    "last": {(0, 1): ["scores2"], (1, 0): ["attend2"], (2, 0): ["scores1"], (3, 0): ["attend1"]},
    "other": {(0, 0): ["weigh0"], (0, 1): ["attend2"], (1, 1): ["sample0"], (3, 1): ["scores1"]},
}
VALUES_PE = {("project", 1): 2, ("project", 3): 1, ("feed", 0): 2}
VALUES_PE |= {(k, 3): 1 for k in ("other", "route", "decide", "tail")} | {("last", 2): 1}
FIRST_POINTS = 4
WEIGHT_LOADS = 68


def kind(g):
    if 1 <= g <= 3 * LAYERS:
        return ("feed", "project", "mix")[g % 3]
    return {3 * LAYERS + 1: "route", 3 * LAYERS + 2: "decide", SLOTS - 2: "tail", SLOTS - 1: "last"}.get(g, "other")


def tile_of(slot):
    n = slot if slot <= 3 * LAYERS else slot - 1
    return n if slot != 3 * LAYERS + 1 and 0 <= n < GROUPS else None


def wait_if(eng, sem, value):
    if not isinstance(value, int) or value > 0:
        eng.wait_ge(sem, value)


def hold(eng, sem, value, turns):
    if not isinstance(value, int) or value > 0:
        eng.wait_ge(sem, value)
        eng.sem_inc(turns, 1)


class Steps:

    def __init__(self, eng, sem, per_round, round_, turns=None):
        self.eng, self.sem, self.base, self.n, self.per, self.turns = eng, sem, round_ * per_round, 0, per_round, turns

    def done(self, ins):
        ins.then_inc(self.sem, 1)
        self.n += 1

    def wait(self):
        if self.turns is None:
            self.eng.wait_ge(self.sem, self.base + self.n)
        else:
            hold(self.eng, self.sem, self.base + self.n, self.turns)

    def link(self, ins):
        self.done(ins)
        self.wait()

    def close(self):
        assert self.n == self.per, (self.n, self.per)


def ln_steps(tag, pe, act, dve, shifted=False):
    pe += [f"{tag}.center{h}" for h in range(2)] + [f"{tag}.var{h}" for h in range(2)]
    act += [f"{tag}.square{h}" for h in range(2)] + [f"{tag}.rstd{h}" for h in range(2)]
    for h in range(2):
        dve += [f"{tag}.norm{h}"] + ([f"{tag}.shift{h}"] if shifted else [])


def tower_steps():
    pe, act, dve = [], [], []
    both = lambda name: [f"{name}{h}" for h in range(2)]
    pe += both("h_transposed")
    act += both("h_copied")
    ln_steps("in", pe, act, dve)
    for l in range(LAYERS):
        ln_steps(f"a{l}", pe, act, dve, True)
        pe += [f"{l}.{n}" for n in ("k0", "k1", "q0", "q1", "v0", "v1", "kT0", "kT1", "context", "qT0", "qT1", "out_weights", "out0", "out1")]
        act += [f"{l}.{n}" for n in ("k_exp0", "k_exp1", "q_exp0", "q_exp1", "v_copied0", "v_copied1", "kT_copied0", "kT_copied1", "qT_copied0", "qT_copied1")]
        dve += [f"{l}.{n}" for n in ("k_max", "q_shifted0", "q_shifted1", "q_ready0", "q_ready1", "context_ready", "out_weights_ready", "added0", "added1")]
        ln_steps(f"f{l}", pe, act, dve)
        pe += [f"{l}.up{2 * f + m}{h}" for f in range(2) for h in range(2) for m in range(2)] + both(f"{l}.down")
        act += [f"{l}.gelu{2 * f + m}{h}" for f in range(2) for h in range(2) for m in range(2)]
        dve += both(f"{l}.ff_added") if l < LAYERS - 1 else both("skipped_over") + both("residual")
    ln_steps("m", pe, act, dve)
    pe += both("router_hidden") + ["logits"]
    act += both("router_relu") + ["expert_exp"]
    dve += ["logits_shifted", "top_ready", "weights_ready"]
    for e in range(EXP):
        pe += both(f"e{e}.first") + (["weights_transposed"] if e == 2 else []) + both(f"e{e}.second")
        act += both(f"e{e}.first_relu") + (["weights_copied", "weights_kept"] if e == 2 else []) + both(f"e{e}.second_relu")
        if e == 0:
            act += ["second_exp"]
        if e >= 2:
            pe += both(f"e{e - 2}.weight")
    for e in (EXP - 2, EXP - 1):
        pe += both(f"e{e}.weight")
    for e in range(EXP):
        dve += both(f"e{e}.weighted")
    pe += both("final")
    act += both("final_copied")
    return {"pe": pe, "act": act, "dve": dve}


STEPS = tower_steps()
AT = {engine: {name: n + 1 for n, name in enumerate(names)} for engine, names in STEPS.items()}


class Signals:

    def __init__(self, engine, eng, sems, round_):
        self.engine, self.eng, self.sems, self.n, self.round = engine, eng, sems, 0, round_

    def mark(self, ins, name):
        assert STEPS[self.engine][self.n] == name, (STEPS[self.engine][self.n], name)
        ins.then_inc(self.sems[self.engine], 1)
        self.n += 1

    def skip(self, name):
        assert STEPS[self.engine][self.n] == name
        self.n += 1

    def wait(self, engine, name):
        self.eng.wait_ge(self.sems[engine], self.round * len(STEPS[engine]) + AT[engine][name])

    def close(self):
        assert self.n == len(STEPS[self.engine])


def program(nc, PAIRS, x, out, w):
    x_v = x.rearrange("b c h w -> (b c) (h w)")
    out_v = out.rearrange("(i m) (t p) c -> i p t m c", m=2, p=P)
    scr = [nc.dram_tensor(f"scratch{n}", (2 * (HW - 1) * HW, 2 * C), F32).ap() for n in range(2)]
    with ExitStack() as ctx:
        sb = lambda name, shape, dt=F32: ctx.enter_context(nc.sbuf_tensor(name, shape, dt))
        pb = lambda name, shape: ctx.enter_context(nc.psum_tensor(name, shape, F32))
        sem = lambda name: ctx.enter_context(nc.semaphore(name))

        ident = sb("ident", [P, P])
        ref = sb("ref", [P, 256])
        wy = sb("wy", [P, GRID])
        base = sb("base", [P, GROUPS * NH])
        WQO = sb("WQO", [P, 160])
        WKV = sb("WKV", [P, 2, P])
        WO2 = sb("WO2", [P, P])
        bo1s = sb("bo1s", [P, 2, OH])
        lngs = sb("lngs", [P, OH])
        lnbs = sb("lnbs", [P, OH])
        bo2s = sb("bo2s", [P, 2 * NH])
        center = sb("center", [P, P])
        mean = sb("mean", [P, P])
        hmask = sb("hmask", [P, P])
        rank = sb("rank", [P, EXP])
        eps = sb("eps", [P, 1])
        Wq = sb("Wq", [P, LAYERS, P])
        Wk = sb("Wk", [P, LAYERS, P])
        Wv = sb("Wv", [P, LAYERS, P])
        Wo = sb("Wo", [P, LAYERS, P])
        W1 = sb("W1", [P, LAYERS, 2, FF])
        W2 = sb("W2", [P, LAYERS, 2, C])
        cols = sb("cols", [P, 6, LAYERS])
        b1c = sb("b1c", [P, LAYERS, 2])
        Rw1 = sb("Rw1", [P, 2 * RH])
        rb1 = sb("rb1", [2 * RH, 1])
        Rw2 = sb("Rw2", [2 * RH, 2 * EXP])
        rb2 = sb("rb2", [P, EXP])
        E1w = sb("E1w", [P, EXP, P])
        E2w = sb("E2w", [P, EXP, P])
        E3w = sb("E3w", [P, EXP, P])
        eb1 = sb("eb1", [P, EXP])
        eb2 = sb("eb2", [P, EXP])
        eb3 = sb("eb3", [SPLIT, P])
        spread = sb("spread", [SPLIT, EXP, P], BF16)

        X = sb("X", [P, 2, CH, HW])
        T = sb("T", [P, 2, 2, CH + 1, C])
        V = sb("V", [P, GRID, HW])
        qf = sb("qf", [P, GRID, GRID])
        QO = sb("QO", [P, 2, TILES, 160])
        Z = sb("Z", [P, 256])
        Z2 = sb("Z2", [P, 256])
        Z3 = sb("Z3", [P, 256])
        st16 = sb("st16", [P, 2, GROUPS])
        rstd = sb("rstd", [P, GROUPS])
        HT = sb("HT", [P, 2, P])
        PI = sb("PI", [P, 256], I32)
        PF = sb("PF", [P, 256])
        FG = sb("FG", [P, 256, 2])
        W = sb("W", [P, 2, GROUPS * NH, 4])
        idx = sb("idx", [P, 2, GROUPS * NH], I32)
        idf = sb("idf", [P, GROUPS * NH])
        G = sb("G", [P, 3, NH, 4 * C])
        S = sb("S", [P, 2, NH * C])
        ST = sb("ST", [P, 4, P])
        PR = sb("PR", [P, NH * C])
        PV = sb("PV", [P, NH * C])
        sc = sb("sc", [P, 2, 64])
        ex = sb("ex", [P, 2, 64])
        mx = sb("mx", [P, NH])
        den = sb("den", [P, NH])
        rden = sb("rden", [P, NH])
        o8 = sb("o8", [P, C])
        HO = sb("HO", [P, GROUPS, C])
        HH = sb("HH", [P, NQ])
        XT = sb("XT", [P, NQ])
        SQ = sb("SQ", [P, NQ])
        R = SQ
        HN = sb("HN", [P, NQ])
        ARENA = sb("ARENA", [P, EXP, NQ])
        tok_major = lambda n: ARENA[:, n, :].rearrange("p (t n) -> p t n", n=P)
        QE, KE, QT, KT, VT = tok_major(0), ARENA[:, 1, :], ARENA[:, 2, :], tok_major(3), tok_major(4)
        BIG = ARENA
        OT = XT[:, :].rearrange("p (t n) -> p t n", n=P)
        CT = sb("CT", [P, P])
        MM = sb("MM", [P, P])
        kmax = sb("kmax", [P, 4])
        kden = sb("kden", [P, 4])
        qmax = sb("qmax", [P, P])
        LG = sb("LG", [P, GROUPS * EXP])
        L2 = sb("L2", [P, GROUPS * EXP])
        L3 = sb("L3", [P, GROUPS * EXP])
        S1 = sb("S1", [P, GROUPS * EXP])
        t16 = sb("t16", [P, 8, GROUPS])
        part16 = sb("part16", [P, 2, 2 * EXP * TILES], BF16)
        LS = sb("LS", [P, TILES, 3, 2 * EXP])
        WF = sb("WF", [SPLIT, NQ])
        WB = sb("WB", [SPLIT, NQ], BF16)
        spread32 = ARENA[0:SPLIT, 0, 0:EXP * P].rearrange("p (e n) -> p e n", n=P)

        rowp = pb("rowp", [P, 4, P])
        stp = pb("stp", [P, 4, P])
        offp = rowp[:, :, :].rearrange("p a b -> p (a b)")
        keyp = pb("keyp", [P, NH, C])
        valp = pb("valp", [P, NH, C])
        U = [pb(f"U{n}", [P, 2, HALF]) for n in range(2)]

        zeroed = sem("zeroed")
        w_loaded = sem("w_loaded")
        bias_projected = sem("bias_projected")
        folded = sem("folded")
        spread_ready = sem("spread_ready")
        x_loaded = [sem(f"x_loaded{n}") for n in range(2)]
        rows_interpolated = sem("rows_interpolated")
        rows_transposed = sem("rows_transposed")
        rows_copied = sem("rows_copied")
        scratch_stored = [sem(f"scratch_stored{n}") for n in range(2)]
        scratch_ready = sem("scratch_ready")
        qf_ready = sem("qf_ready")
        qo_projected = sem("qo_projected")
        qo_copied = sem("qo_copied")
        var_ready = sem("var_ready")
        small_act = sem("small_act")
        gelu_arg_ready = sem("gelu_arg_ready")
        hidden_ready = sem("hidden_ready")
        hidden_transposed = sem("hidden_transposed")
        hidden_copied = sem("hidden_copied")
        offsets_projected = sem("offsets_projected")
        offsets_taken = sem("offsets_taken")
        points_ready = sem("points_ready")
        patches_gathered = [sem(f"patches_gathered{n}") for n in range(3)]
        patches_weighed = sem("patches_weighed")
        patches_used = sem("patches_used")
        sampled_ready = sem("sampled_ready")
        sampled_transposed = sem("sampled_transposed")
        sampled_copied = sem("sampled_copied")
        keys_ready = sem("keys_ready")
        values_ready = sem("values_ready")
        keys_used = sem("keys_used")
        scores_ready = sem("scores_ready")
        probs_ready = sem("probs_ready")
        attended = sem("attended")
        out_stored = sem("out_stored")
        sp_turns = sem("sp_turns")
        pool_turns = sem("pool_turns")
        pe_turns = sem("pe_turns")
        pool_a = sem("pool_a")
        dve_a = sem("dve_a")
        dve_b = sem("dve_b")
        dve_t = sem("dve_t")
        rstd_log = sem("rstd_log")
        done = {e: sem(f"tower_{e}") for e in ("pe", "act", "dve")}
        SMALL_ACT = 5

        block = ctx.enter_context(nc.Block())
        half = lambda t, h: t[:, HALF * h:HALF * h + HALF]
        tiles = lambda t, h: t[:, 4 * h:4 * h + 4, :]
        flat = lambda t: t.rearrange("p a b -> p (a b)")

        def gathered(j, g):
            return (j * len(range(g % 3, GROUPS, 3)) + g // 3 + 1) * NH * 16

        def weigh(engine, b, g, part):
            n = NH // 2
            k0 = n * part
            patches = G[:, g % 3, k0:k0 + n, :].rearrange("p k (x c) -> p (k x) c", c=C)
            wgt = W[:, b, g * NH + k0:g * NH + k0 + n, :].rearrange("p k x -> p (k x)")
            return engine.tensor_tensor(patches, patches, wgt.unsqueeze(2).broadcast_to([P, 4 * n, C]), ALU.mult)

        def run(eng, body):
            body(0, 0, None, None)
            body(1, 1, 0, None)
            body(2, 0, 1, 0)
            with eng.Fori(1, PAIRS // 2 - 1) as s:
                body(s * 2 + 1, 1, s * 2, s * 2 - 1)
                body(s * 2 + 2, 0, s * 2 + 1, s * 2)
            body(PAIRS - 1, 1, PAIRS - 2, PAIRS - 3)
            body(None, 0, PAIRS - 1, PAIRS - 2)
            body(None, 1, None, PAIRS - 1)

        def slots(stages, tower):
            for g in range(SLOTS):
                for micro in range(4):
                    if stages is not None:
                        stages(g, micro, 0)
                    if tower is not None:
                        next(tower, None)
                    if stages is not None:
                        stages(g, micro, 1)

        @block.sync
        def _(sp):
            sp.wait_ge(zeroed, 15)
            n = 0

            def put(dst, src):
                nonlocal n
                sp.dma_start(dst, src).then_inc(w_loaded, 16)
                n += 1
            for m in range(2):
                r = slice(C * m, C * m + C)
                put(WQO[r, OH * m:OH * m + OH], w["L0_tok_W_o1"])
                put(WQO[r, 32 + C * m:32 + C * m + C], w["wqT"])
                put(WKV[r, 0, r], w["wkT"])
                put(WKV[r, 1, r], w["wvT"])
                put(bo1s[:, m, :], w["L0_tok_b_o1"].partition_broadcast(P))
            for g in range(P // OH):
                put(WO2[OH * g:OH * g + OH, OH * g:OH * g + OH], w["L0_tok_W_o2"])
            for dst, name in ((lngs, "ln_g"), (lnbs, "ln_b"), (bo2s, "b_o2")):
                put(dst[:, :], w[f"L0_tok_{name}"].partition_broadcast(P))
            for m in range(2):
                r = slice(C * m, C * m + C)
                for dst, src in ((Wq, w["L0_attn_Wq"]), (Wk, w["L0_attn_Wk"]), (Wv, w["L0_attn_Wv"]), (Wo, w["L0_attn_Wo"])):
                    put(dst[r, :, r], src.rearrange("l i o -> i l o"))
                put(W1[r, :, m, :], w["L0_attn_W1"].rearrange("l i o -> i l o"))
                put(cols[r, :, :], w["columns"])
                put(Rw1[r, RH * m:RH * m + RH], w["L0_ffn_router_w1"])
                put(Rw2[RH * m:RH * m + RH, EXP * m:EXP * m + EXP], w["L0_ffn_router_w2"])
                put(rb1[RH * m:RH * m + RH, :], w["L0_ffn_router_b1"].unsqueeze(1))
                for dst, src in ((E1w, w["L0_ffn_expert_w1"]), (E2w, w["L0_ffn_expert_w2"]), (E3w, w["L0_ffn_expert_w3"])):
                    put(dst[r, :, r], src.rearrange("l i o -> i l o"))
                put(eb1[r, :], w["eb1T"])
                put(eb2[r, :], w["eb2T"])
                for part in range(3):
                    first = EXP * (2 * part + m)
                    put(eb3[first:first + EXP, r], w["L0_ffn_expert_b3"])
            for f in range(2):
                put(W2[:, :, f, :], w["L0_attn_W2"][:, P * f:P * f + P, :].rearrange("l i o -> i l o"))
            put(b1c[:, :, :], w["b1T"])
            put(rb2[:, :], w["L0_ffn_router_b2"].partition_broadcast(P))
            for dst, name in ((ident, "c_ident"), (ref, "c_ref"), (wy, "c_wy"), (base, "c_base"), (center, "c_center"),
                              (mean, "c_mean"), (hmask, "c_hmask"), (rank, "c_rank")):
                put(dst[:, :], w[name])
            put(spread32, w["c_spread"])
            assert n == WEIGHT_LOADS, n

            def load(i, k):
                hold(sp, rows_transposed, (i * NCH + k - 1) * 4, sp_turns)
                hold(sp, rows_interpolated, i * NCH + k - 1, sp_turns)
                sp.dma_start(X[:, k % 2, :, :], x_v[bass.ts(i, P), CH * HW * k:CH * HW * (k + 1)]
                             .rearrange("p (h w) -> p h w", w=HW)).then_inc(x_loaded[k % 2], 16)

            def store(i, b, k):
                hold(sp, rows_copied, i * 4 * NCH + 4 * k + 4, sp_turns)
                first = 1 if k == 0 else 0
                n = CH - first
                for m in range(2):
                    src = T[:, k % 2, m, first:first + n, :]
                    src = bass.AP(src.tensor, src.offset, [src.ap[0], [C, n], [1, 2 * C]])
                    row = m * (HW - 1) + CH * k - 1 + first
                    sp.dma_start(scr[b][row * HW:(row + n) * HW, :].rearrange("(h w) c -> w h c", w=HW), src)\
                        .then_inc(scratch_stored[k % 2], 16)

            def store_out(t):
                for h in range(2):
                    hold(sp, done["act"], t * len(STEPS["act"]) + AT["act"][f"final_copied{h}"], sp_turns)
                for m in range(2):
                    dst = out_v[t, :, :, m, :] if isinstance(t, int) else \
                        out_v[bass.ds(t, 1), :, :, m, :].rearrange("a p t c -> (a p) t c")
                    sp.dma_start(dst, OT[:, :, C * m:C * m + C]).then_inc(out_stored, 16)

            def body(i, b, j, t):
                if i is not None:
                    hold(sp, patches_used, (i - 1) * GROUPS, sp_turns)
                    for k in range(NCH):
                        store(i, b, k)
                        if k < NCH - 2:
                            load(i, k + 2)
                        elif not (isinstance(i, int) and i == PAIRS - 1):
                            load(i + 1, k + 2 - NCH)
                    for n in range(2):
                        hold(sp, scratch_stored[n], (i + 1) * 2 * 16 * (NCH // 2), sp_turns)
                    sp.sem_inc(scratch_ready, 1)
                if t is not None:
                    store_out(t)
            load(0, 0)
            load(0, 1)
            run(sp, body)
            sp.wait_ge(out_stored, PAIRS * 32)

        @block.gpsimd
        def _(pool):
            for t in (W1, WQO, WKV, WO2, Wq, Wk, Wv, Wo, Rw1, Rw2, E1w, E2w, E3w, eb3):
                nc.gpsimd.memset(t[:], 0.0).then_inc(zeroed, 1)
            nc.gpsimd.memset(eps[:, :], LN_EPS).then_inc(zeroed, 1)

            g = nc.gpsimd
            pool.wait_ge(w_loaded, WEIGHT_LOADS * 16)

            def rows(c, i, k):
                hold(pool, x_loaded[k % 2], (i * (NCH // 2) + k // 2 + 1) * 16, pool_turns)
                runs = [r for r in ROWS if r[0] == k]
                for op in range(3):
                    for _, q0, cnt, r0 in runs:
                        upper = X[:, k % 2, r0:r0 + 4 * (cnt - 1) + 1:4, :]
                        lower = X[:, k % 2, r0 + 1:r0 + 4 * (cnt - 1) + 2:4, :]
                        o = V[:, q0:q0 + cnt, :]
                        if op == 0:
                            c.done(g.tensor_tensor(o, lower, upper, ALU.subtract))
                        if op == 1:
                            c.done(g.tensor_tensor(o, o, wy[:, q0:q0 + cnt].unsqueeze(2).broadcast_to([P, cnt, HW]), ALU.mult))
                        if op == 2:
                            c.done(g.tensor_tensor(o, o, upper, ALU.add))
                    c.wait()
                g.sem_inc(rows_interpolated, 1)

            def columns(c):
                for op in range(3):
                    for q0, cnt, p0 in RUNS:
                        left = V[:, :, p0:p0 + 4 * (cnt - 1) + 1:4]
                        right = V[:, :, p0 + 1:p0 + 4 * (cnt - 1) + 2:4]
                        o = qf[:, :, q0:q0 + cnt]
                        if op == 0:
                            c.done(g.tensor_tensor(o, right, left, ALU.subtract))
                        if op == 1:
                            c.done(g.tensor_tensor(o, o, wy[:, q0:q0 + cnt].unsqueeze(1).broadcast_to([P, GRID, cnt]), ALU.mult))
                        if op == 2:
                            c.done(g.tensor_tensor(o, o, left, ALU.add))
                    c.wait()
                g.sem_inc(qf_ready, 1)

            g16 = lambda t: t[:, :].rearrange("p (g k) -> p g k", k=OH)
            over_groups = lambda t: t[:, :].unsqueeze(1).broadcast_to([P, GROUPS, OH])

            def points(c, i, b):
                hold(pool, offsets_taken, i + 1, pool_turns)
                c.link(g.tensor_tensor(g16(Z), g16(Z3), over_groups(bo2s), ALU.add))
                c.link(g.tensor_scalar(Z[:, :], Z[:, :], 4.0, None, ALU.mult))
                c.link(g.tensor_tensor(Z[:, :], Z[:, :], ref[:, :], ALU.add))
                c.link(g.tensor_scalar(Z[:, :], Z[:, :], 0.0, float(HW - 1), ALU.max, ALU.min))
                c.link(g.tensor_copy(PI[:, :], Z[:, :]))
                c.link(g.tensor_copy(PF[:, :], PI[:, :]))
                c.link(g.tensor_tensor(Z2[:, :], PF[:, :], Z[:, :], ALU.subtract))
                c.link(g.tensor_scalar(Z2[:, :], Z2[:, :], 0.0, None, ALU.is_gt))
                c.link(g.tensor_tensor(PF[:, :], PF[:, :], Z2[:, :], ALU.subtract))
                c.link(g.tensor_scalar(PF[:, :], PF[:, :], float(HW - 2), None, ALU.min))
                pf = PF[:, :].rearrange("p (n a) -> p n a", a=2)
                c.done(g.tensor_scalar(idf[:, :], pf[:, :, 1], float(HW), None, ALU.mult))
                c.link(g.tensor_tensor(FG[:, :, 1], Z[:, :], PF[:, :], ALU.subtract))
                c.link(g.tensor_tensor(idf[:, :], idf[:, :], pf[:, :, 0], ALU.add))
                c.link(g.tensor_tensor(idf[:, :], idf[:, :], base[:, :], ALU.add))
                c.done(g.tensor_copy(idx[:, b, :], idf[:, :]))
                c.link(g.tensor_scalar(FG[:, :, 0], FG[:, :, 1], -1.0, 1.0, ALU.mult, ALU.add))
                fg = FG[:, :, :].rearrange("p (n a) w -> p n a w", a=2)
                c.link(g.tensor_tensor(W[:, b, :, :].rearrange("p n (x y) -> p n x y", x=2),
                                       fg[:, :, 0, :].unsqueeze(3).broadcast_to([P, GROUPS * NH, 2, 2]),
                                       fg[:, :, 1, :].unsqueeze(2).broadcast_to([P, GROUPS * NH, 2, 2]), ALU.mult))
                pool.sem_inc(points_ready, 1)

            def gather(j, b, n, points):
                if 0 in points:
                    hold(pool, patches_used, j * GROUPS + (n - 2 if n > 0 else 0), pool_turns)
                for p in points:
                    pool.indirect_dma_start(
                        G[:, n % 3, p, :], None, scr[1 - b],
                        bass.IndirectOffsetOnAxis(ap=idx[:, 1 - b, n * NH + p:n * NH + p + 1], axis=0),
                    ).then_inc(patches_gathered[n % 3], 16)

            def body(i, b, j, t):
                c = None if i is None else Steps(pool, pool_a, A_POOL, i, pool_turns)
                if j is not None:
                    hold(pool, points_ready, j + 1, pool_turns)
                    hold(pool, scratch_ready, j + 1, pool_turns)
                for n in range(GROUPS + 1):
                    if j is not None and n < GROUPS:
                        gather(j, b, n, range(0, FIRST_POINTS))
                    if j is not None and n >= 1:
                        hold(pool, patches_gathered[(n - 1) % 3], gathered(j, n - 1), pool_turns)
                        weigh(g, 1 - b, n - 1, 0).then_inc(patches_weighed, 1)
                    if j is not None and n < GROUPS:
                        gather(j, b, n, range(FIRST_POINTS, NH))
                    if i is not None and n < NCH:
                        rows(c, i, n)
                    if i is not None and n == NCH:
                        columns(c)
                if i is not None:
                    points(c, i, b)
                    c.close()
            run(pool, body)

        @block.scalar
        def _(act):
            sa = nc.scalar
            act.wait_ge(zeroed, 15)
            act.wait_ge(w_loaded, WEIGHT_LOADS * 16)

            def copy_rows(i, n):
                k, q = n // 4, n % 4
                b = k % 2
                if n == 0:
                    wait_if(act, scratch_stored[b], i * 2 * 16 * (NCH // 2))
                act.wait_ge(rows_transposed, i * 4 * NCH + n + 1)
                src = rowp[:, :, :].rearrange("p r (m c) -> p m r c", m=2)
                if q < 3 or k == NCH - 1:
                    sa.copy(T[:, b, :, 1 + 4 * q:5 + 4 * q, :], src).then_inc(rows_copied, 1)
                else:
                    sa.copy(T[:, b, :, 1 + 4 * q:5 + 4 * q, :], src)
                    wait_if(act, scratch_stored[1 - b], i * 2 * 16 * (NCH // 2) + 32 * ((k + 1) // 2))
                    sa.copy(T[:, 1 - b, :, 0, :], src[:, :, 3, :]).then_inc(rows_copied, 1)

            def offsets(i, part):
                if part == 0:
                    act.wait_ge(var_ready, i + 1)
                    sa.activation(rstd[:, :], st16[:, 1, :], ACT.Ln).then_inc(small_act, 1)
                    act.wait_ge(small_act, i * SMALL_ACT + 1)
                    sa.activation(rstd[:, :], rstd[:, :], ACT.Exp, scale=-0.5).then_inc(small_act, 1)
                if part == 1:
                    act.wait_ge(gelu_arg_ready, i + 1)
                    sa.activation(Z3[:, :], Z3[:, :], ACT.Exp).then_inc(small_act, 1)
                    act.wait_ge(small_act, i * SMALL_ACT + 3)
                    sa.activation(Z3[:, :], Z3[:, :], ACT.Ln, bias=1.0).then_inc(small_act, 1)
                    act.wait_ge(small_act, i * SMALL_ACT + 4)
                    sa.activation(Z3[:, :], Z3[:, :], ACT.Exp, scale=-1.0).then_inc(small_act, 1)
                if part == 3:
                    act.wait_ge(offsets_projected, i + 1)
                    sa.copy(Z3[:, :], offp[:, 0:256]).then_inc(offsets_taken, 1)
                if part == 2:
                    act.wait_ge(hidden_transposed, i + 1)
                    sa.copy(HT[:, :, :], offp[:, 0:256].rearrange("p (a b) -> p a b", a=2)).then_inc(hidden_copied, 1)

            def copy_qo(i, b, part):
                t0, n = 3 * part, min(3, TILES - 3 * part)
                act.wait_ge(qo_projected, i * 3 + part + 1)
                if part == 0:
                    wait_if(act, scores_ready, (i - 1) * GROUPS)
                sa.copy(QO[:, b, t0:t0 + n, :], offp[:, 0:160 * n].rearrange("p (t n) -> p t n", n=160)).then_inc(qo_copied, 1)

            def copy_sampled(j, g):
                act.wait_ge(sampled_transposed, j * GROUPS + g + 1)
                wait_if(act, values_ready, j * GROUPS + g)
                sa.copy(ST[:, :, :], stp[:, :, :]).then_inc(sampled_copied, 1)

            def probs(j, g):
                act.wait_ge(scores_ready, j * GROUPS + g + 1)
                sa.activation(ex[:, g % 2, :], sc[:, g % 2, :], ACT.Exp, scale=float(DH) ** -0.5).then_inc(probs_ready, 1)

            def tower(t):
                sg = Signals("act", act, done, t)
                logs = 0
                per = 2 * (2 * LAYERS + 2)

                def norm(tag):
                    nonlocal logs
                    for h in range(2):
                        sg.wait("pe", f"{tag}.center{h}")
                        sg.mark(sa.activation(half(SQ, h), U[0][:, h, :], ACT.Square), f"{tag}.square{h}")
                    yield
                    for h in range(2):
                        sg.wait("pe", f"{tag}.var{h}")
                        logs += 1
                        sa.activation(half(R, h), U[1][:, h, :], ACT.Ln, bias=eps[:, 0:1]).then_inc(rstd_log, 1)
                        act.wait_ge(rstd_log, t * per + logs)
                        sg.mark(sa.activation(half(R, h), half(R, h), ACT.Exp, scale=-0.5), f"{tag}.rstd{h}")
                    yield

                for h in range(2):
                    sg.wait("pe", f"h_transposed{h}")
                    sg.mark(sa.copy(half(HH, h), U[0][:, h, :]), f"h_copied{h}")
                yield
                yield from norm("in")
                for l in range(LAYERS):
                    yield from norm(f"a{l}")
                    sg.wait("dve", f"{l}.k_max")
                    for h in range(2):
                        sg.mark(sa.activation(half(KE, h), U[1][:, h, :], ACT.Exp, bias=kmax[:, 3:4], scale=QK_SCALE,
                                              accum_out=kden[:, h:h + 1]), f"{l}.k_exp{h}")
                    for h in range(2):
                        sg.wait("dve", f"{l}.q_shifted{h}")
                        sg.mark(sa.activation(tiles(QE, h), tiles(QE, h), ACT.Exp, scale=QK_SCALE), f"{l}.q_exp{h}")
                    yield
                    for what, dst, u in (("v", VT, 1), ("kT", KT, 0)):
                        for h in range(2):
                            sg.wait("pe", f"{l}.{what}{h}")
                            sg.mark(sa.copy(flat(tiles(dst, h)), U[u][:, h, :]), f"{l}.{what}_copied{h}")
                    yield
                    for h in range(2):
                        sg.wait("pe", f"{l}.qT{h}")
                        sg.mark(sa.copy(half(QT, h), U[1][:, h, :]), f"{l}.qT_copied{h}")
                    yield
                    yield
                    yield
                    yield from norm(f"f{l}")
                    for f in range(2):
                        for h in range(2):
                            for m in range(2):
                                c = 2 * f + m
                                sg.wait("pe", f"{l}.up{c}{h}")
                                sg.mark(sa.activation(half(BIG[:, c, :], h), U[m][:, h, :], ACT.Gelu, bias=b1c[:, l, f:f + 1]), f"{l}.gelu{c}{h}")
                        if f == 1:
                            act.preload_act_table_set("natural_log_exp_and_others")
                        yield
                    yield
                yield from norm("m")
                for h in range(2):
                    sg.wait("pe", f"router_hidden{h}")
                    sg.mark(sa.activation(QT[0:2 * RH, HALF * h:HALF * h + HALF], U[1][0:2 * RH, h, :], ACT.Relu, bias=rb1[:, 0:1]), f"router_relu{h}")
                yield
                sg.wait("dve", "logits_shifted")
                sg.mark(sa.activation(LG[:, :], LG[:, :], ACT.Exp), "expert_exp")
                yield
                for e in range(EXP):
                    for h in range(2):
                        sg.wait("pe", f"e{e}.first{h}")
                        sg.mark(sa.activation(half(SQ, h), U[0][:, h, :], ACT.Relu, bias=eb1[:, e:e + 1]), f"e{e}.first_relu{h}")
                    yield
                    if e == 2:
                        sg.wait("pe", "weights_transposed")
                        sg.mark(sa.copy(WB[:, :].rearrange("p (a b) -> p a b", a=2), U[0][0:SPLIT, :, :]), "weights_copied")
                        sg.mark(sa.copy(WF[:, :].rearrange("p (a b) -> p a b", a=2), U[0][0:SPLIT, :, :]), "weights_kept")
                        yield
                    for h in range(2):
                        sg.wait("pe", f"e{e}.second{h}")
                        sg.mark(sa.activation(half(BIG[:, e, :], h), U[1][:, h, :], ACT.Relu, bias=eb2[:, e:e + 1]), f"e{e}.second_relu{h}")
                    if e == 0:
                        sg.wait("dve", "top_ready")
                        sg.mark(sa.activation(t16[:, 4, :], t16[:, 3, :], ACT.Exp), "second_exp")
                    yield
                yield
                for h in range(2):
                    sg.wait("pe", f"final{h}")
                    sg.mark(sa.copy(flat(tiles(OT, h)), U[0][:, h, :]), f"final_copied{h}")
                    yield
                sg.close()
                assert logs == per
                yield

            def body(i, b, j, t):
                def stages(g, micro, after):
                    n = 4 * g + micro
                    if after:
                        return
                    if i is not None:
                        if n < 4 * NCH:
                            copy_rows(i, n)
                        if (g, micro) in QO_COPIES:
                            copy_qo(i, b, QO_COPIES.index((g, micro)))
                    if j is not None:
                        early = g == SLOTS - 1
                        if micro == (kind(g) in ("mix", "last")) and tile_of(g - 2) is not None:
                            probs(j, tile_of(g - 2))
                        if micro == (0 if early or kind(g) == "mix" else 1) and tile_of(g - 1) is not None:
                            copy_sampled(j, tile_of(g - 1))
                        if early and micro == 2:
                            probs(j, tile_of(g - 1))
                    if i is not None and (g, micro) in OFFSETS_ACT:
                        offsets(i, OFFSETS_ACT.index((g, micro)))
                slots(stages, None if t is None else tower(t))
            act.preload_act_table_set("natural_log_exp_and_others")
            act.wait_ge(folded, 2 * LAYERS)
            sa.copy(spread[:, :, :], spread32).then_inc(spread_ready, 1)
            act.wait_ge(spread_ready, 1)
            run(act, body)

        @block.tensor
        def _(pe):
            mmul = lambda o, a, b, start=True, stop=True: nc.tensor.matmul(o, a, b, start=start, stop=stop)
            pe.wait_ge(w_loaded, WEIGHT_LOADS * 16)
            for l in range(LAYERS):
                for f in range(2):
                    n = LAYERS * (2 * l + f)
                    ins = mmul(U[0][:, 0, n:n + LAYERS], W1[0:C, l, 0, P * f:P * f + P], cols[0:C, 4, :])
            ins.then_inc(bias_projected, 1)

            def transpose_rows(i, n):
                k, q = n // 4, n % 4
                if q == 0:
                    pe.wait_ge(x_loaded[k % 2], (i * (NCH // 2) + k // 2 + 1) * 16)
                if n == 0:
                    wait_if(pe, offsets_taken, i)
                wait_if(pe, rows_copied, i * 4 * NCH + n)
                for r in range(4):
                    ins = nc.tensor.transpose(rowp[:, r, :], X[:, k % 2, 4 * q + r, :], ident[:, :])
                ins.then_inc(rows_transposed, 1)

            def offsets(i, part):
                if part == 0:
                    pe.wait_ge(rows_copied, (i + 1) * 4 * NCH)
                    pe.wait_ge(qf_ready, i + 1)
                else:
                    pe.wait_ge(qo_copied, i * 3 + min(part, 3))
                if part < 3:
                    for t in range(3 * part, min(3 * part + 3, TILES)):
                        ins = mmul(offp[:, 160 * (t % 3):160 * (t % 3) + 160], flat(qf[:, 4 * t:4 * t + 4, :]), WQO[:, :])
                    ins.then_inc(qo_projected, 1)
                if part == 3:
                    pe.wait_ge(hidden_ready, i + 1)
                    for a in range(2):
                        ins = nc.tensor.transpose(offp[:, P * a:P * a + P], Z[:, P * a:P * a + P], ident[:, :])
                    ins.then_inc(hidden_transposed, 1)
                if part == 4:
                    pe.wait_ge(hidden_copied, i + 1)
                    for a in range(2):
                        ins = mmul(offp[:, P * a:P * a + P], HT[:, a, :], WO2[:, :])
                    ins.then_inc(offsets_projected, 1)

            def transpose_sampled(j, g):
                pe.wait_ge(sampled_ready, j * GROUPS + g + 1)
                wait_if(pe, sampled_copied, j * GROUPS + g)
                for a in range(4):
                    ins = nc.tensor.transpose(stp[:, a, :], S[:, g % 2, P * a:P * a + P], ident[:, :])
                ins.then_inc(sampled_transposed, 1)

            def project(j, g, which, bank, free, ready):
                pe.wait_ge(sampled_copied, j * GROUPS + g + 1)
                wait_if(pe, free, j * GROUPS + g)
                for a in range(4):
                    ins = mmul(bank[:, 2 * a:2 * a + 2, :].rearrange("p k c -> p (k c)"), ST[:, a, :], WKV[:, which, :])
                ins.then_inc(ready, 1)

            def tower(t):
                sg = Signals("pe", pe, done, t)

                def norm(tag, src, ready):
                    for h in range(2):
                        sg.wait(*ready(h))
                        sg.mark(mmul(U[0][:, h, :], center[:, :], half(src, h)), f"{tag}.center{h}")
                    yield
                    for h in range(2):
                        sg.wait("act", f"{tag}.square{h}")
                        sg.mark(mmul(U[1][:, h, :], mean[:, :], half(SQ, h)), f"{tag}.var{h}")
                    yield

                pe.wait_ge(attended, (t + 1) * GROUPS)
                wait_if(pe, done["act"], t * len(STEPS["act"]))
                for h in range(2):
                    for a in range(4):
                        n = 2 * (4 * h + a)
                        ins = nc.tensor.transpose(U[0][:, h, P * a:P * a + P], flat(HO[:, n:n + 2, :]), ident[:, :])
                    sg.mark(ins, f"h_transposed{h}")
                yield
                yield from norm("in", HH, lambda h: ("act", f"h_copied{h}"))
                for l in range(LAYERS):
                    yield from norm(f"a{l}", XT, lambda h: ("dve", f"in.norm{h}" if l == 0 else f"{l - 1}.ff_added{h}"))
                    for h in range(2):
                        sg.wait("dve", f"a{l}.shift{h}")
                        sg.mark(mmul(U[1][:, h, :], Wk[:, l, :], half(HN, h)), f"{l}.k{h}")
                    for h in range(2):
                        for a in range(4):
                            ins = mmul(U[0][:, h, P * a:P * a + P], HN[:, P * (4 * h + a):P * (4 * h + a) + P], Wq[:, l, :])
                        sg.mark(ins, f"{l}.q{h}")
                    yield
                    for h in range(2):
                        sg.wait("act", f"{l}.k_exp{h}")
                        for a in range(4):
                            ins = mmul(U[1][:, h, P * a:P * a + P], HN[:, P * (4 * h + a):P * (4 * h + a) + P], Wv[:, l, :])
                        sg.mark(ins, f"{l}.v{h}")
                    for h in range(2):
                        sg.wait("dve", f"{l}.q_shifted{h}")
                        for a in range(4):
                            ins = nc.tensor.transpose(U[0][:, h, P * a:P * a + P], KE[:, P * (4 * h + a):P * (4 * h + a) + P], ident[:, :])
                        sg.mark(ins, f"{l}.kT{h}")
                    yield
                    for a in range(TILES):
                        if a % 4 == 0:
                            sg.wait("act", f"{l}.kT_copied{a // 4}")
                        ins = mmul(U[0][:, 0, 0:P], VT[:, a, :], KT[:, a, :], start=a == 0, stop=a == TILES - 1)
                    sg.mark(ins, f"{l}.context")
                    for h in range(2):
                        sg.wait("dve", f"{l}.q_ready{h}")
                        for a in range(4):
                            ins = nc.tensor.transpose(U[1][:, h, P * a:P * a + P], QE[:, 4 * h + a, :], ident[:, :])
                        sg.mark(ins, f"{l}.qT{h}")
                    yield
                    sg.wait("dve", f"{l}.context_ready")
                    sg.mark(mmul(U[0][:, 1, 0:P], CT[:, :], Wo[:, l, :]), f"{l}.out_weights")
                    yield
                    sg.wait("dve", f"{l}.out_weights_ready")
                    for h in range(2):
                        sg.wait("act", f"{l}.qT_copied{h}")
                        sg.mark(mmul(U[1][:, h, :], MM[:, :], half(QT, h)), f"{l}.out{h}")
                    yield
                    yield from norm(f"f{l}", XT, lambda h: ("dve", f"{l}.added{h}"))
                    for f in range(2):
                        for h in range(2):
                            for m in range(2):
                                c = 2 * f + m
                                if f == 0:
                                    sg.wait("dve", f"f{l}.norm{h}")
                                else:
                                    sg.wait("act", f"{l}.gelu{m}{h}")
                                sg.mark(mmul(U[m][:, h, :], W1[:, l, m, P * f:P * f + P], half(HN, h)), f"{l}.up{c}{h}")
                        yield
                    for h in range(2):
                        sg.wait("act", f"{l}.gelu3{h}")
                        for f in range(2):
                            for m in range(2):
                                ins = mmul(U[0][C * m:C * m + C, h, :], W2[:, l, f, :], half(BIG[:, 2 * f + m, :], h), start=f == 0, stop=f == 1)
                        sg.mark(ins, f"{l}.down{h}")
                    yield
                yield from norm("m", HH, lambda h: ("dve", f"residual{h}"))
                for h in range(2):
                    sg.wait("dve", f"m.norm{h}")
                    sg.mark(mmul(U[1][0:2 * RH, h, :], Rw1[:, :], half(HN, h)), f"router_hidden{h}")
                yield
                sg.wait("act", "router_relu1")
                for a in range(TILES):
                    ins = mmul(U[0][:, 0, 2 * EXP * a:2 * EXP * a + 2 * EXP], QT[0:2 * RH, P * a:P * a + P], Rw2[:, :])
                sg.mark(ins, "logits")
                yield

                def weight(e, u):
                    for h in range(2):
                        sg.mark(mmul(U[u][:, h, :], spread[:, e, :], half(WB, h)), f"e{e}.weight{h}")

                for e in range(EXP):
                    for h in range(2):
                        if e == 0:
                            sg.wait("dve", "logits_shifted")
                        if e >= 3:
                            sg.wait("dve", f"e{e - 3}.weighted{h}")
                        sg.mark(mmul(U[0][:, h, :], E1w[:, e, :], half(HN, h)), f"e{e}.first{h}")
                    yield
                    if e == 2:
                        hold(pe, done["dve"], t * len(STEPS["dve"]) + AT["dve"]["weights_ready"], pe_turns)
                        hold(pe, done["act"], t * len(STEPS["act"]) + AT["act"]["e2.first_relu1"], pe_turns)
                        for a in range(TILES):
                            ins = nc.tensor.transpose(U[0][0:SPLIT, a // 4, P * (a % 4):P * (a % 4) + P], LS[:, a, :, :].rearrange("p k n -> p (k n)"), ident[:, :])
                        sg.mark(ins, "weights_transposed")
                        yield
                    for h in range(2):
                        sg.wait("act", f"e{e}.first_relu{h}")
                        sg.mark(mmul(U[1][:, h, :], E2w[:, e, :], half(SQ, h)), f"e{e}.second{h}")
                    if e == 2:
                        sg.wait("act", "weights_kept")
                    if e >= 2:
                        weight(e - 2, 0)
                    yield
                sg.wait("act", f"e{EXP - 1}.second_relu1")
                weight(EXP - 2, 1)
                sg.wait("dve", f"e{EXP - 3}.weighted1")
                weight(EXP - 1, 0)
                yield
                for h in range(2):
                    sg.wait("dve", f"e{EXP - 1}.weighted{h}")
                    for a in range(4):
                        tok = slice(P * (4 * h + a), P * (4 * h + a) + P)
                        o = U[0][:, h, P * a:P * a + P]
                        mmul(o, HH[:, tok], ident[:, :], True, False)
                        for e in range(EXP):
                            mmul(o, BIG[:, e, tok], E3w[:, e, :], False, False)
                        ins = mmul(o, WF[:, tok], eb3[:, :], False, True)
                    sg.mark(ins, f"final{h}")
                    yield
                sg.close()
                yield

            def body(i, b, j, t):
                def stages(g, micro, after):
                    if after:
                        return
                    if i is not None:
                        if 4 * g + micro < 4 * NCH:
                            transpose_rows(i, 4 * g + micro)
                        if (g, micro) in OFFSETS_PE:
                            offsets(i, OFFSETS_PE.index((g, micro)))
                    if j is not None:
                        n = tile_of(g - 1)
                        early = g == SLOTS - 1
                        if n is not None:
                            if micro == (0 if early or kind(g) == "mix" else 1):
                                transpose_sampled(j, n)
                            if micro == 2:
                                project(j, n, 0, keyp, keys_used, keys_ready)
                        lag = VALUES_PE.get((kind(g), micro))
                        if (g, micro) == (3 * LAYERS, 3):
                            lag = 1
                        n = None if lag is None else tile_of(g - lag)
                        if n is not None:
                            project(j, n, 1, valp, attended, values_ready)
                slots(stages, None if t is None else tower(t))
            pe.wait_ge(folded, 2 * LAYERS)
            pe.wait_ge(spread_ready, 1)
            run(pe, body)

        @block.vector
        def _(dve):
            v = nc.vector
            dve.wait_ge(w_loaded, WEIGHT_LOADS * 16)
            dve.wait_ge(bias_projected, 1)
            for l in range(LAYERS):
                own = U[0][:, 0, 2 * LAYERS * l:2 * LAYERS * l + 2 * LAYERS].rearrange("p (f n) -> p f n", n=LAYERS)[:, :, l]
                v.tensor_tensor(b1c[:, l, :], b1c[:, l, :], own, ALU.add).then_inc(folded, 1)
                v.tensor_scalar(W1[:, l, :, :], W1[:, l, :, :], cols[:, 3, l:l + 1], None, ALU.mult).then_inc(folded, 1)
            g16 = lambda t: t[:, :].rearrange("p (g k) -> p g k", k=OH)
            over_groups = lambda t: t[:, :].unsqueeze(1).broadcast_to([P, GROUPS, OH])

            def hidden_norm(c, i, b):
                wait_if(dve, points_ready, i)
                dve.wait_ge(qo_copied, i * 3 + 3)
                c.link(v.tensor_tensor(Z[:, :].rearrange("p (t n) -> p t n", n=32), QO[:, b, :, 0:32],
                                       flat(bo1s[:, :, :]).unsqueeze(1).broadcast_to([P, TILES, 32]), ALU.add))
                c.link(v.tensor_reduce(st16[:, 0, :], g16(Z), AX.X, ALU.add))
                c.link(v.scalar_tensor_tensor(g16(Z), st16[:, 0, :].unsqueeze(2).broadcast_to([P, GROUPS, OH]), -1.0 / OH,
                                              g16(Z), ALU.mult, ALU.add))
                c.link(v.tensor_tensor(Z2[:, :], Z[:, :], Z[:, :], ALU.mult))
                c.link(v.tensor_reduce(st16[:, 1, :], g16(Z2), AX.X, ALU.add))
                c.link(v.tensor_scalar(st16[:, 1, :], st16[:, 1, :], 1.0 / OH, LN_EPS, ALU.mult, ALU.add))
                v.sem_inc(var_ready, 1)

            def gelu_argument(c, i):
                dve.wait_ge(small_act, i * SMALL_ACT + 2)
                c.link(v.tensor_tensor(g16(Z), g16(Z), rstd[:, :].unsqueeze(2).broadcast_to([P, GROUPS, OH]), ALU.mult))
                c.link(v.tensor_tensor(g16(Z), g16(Z), over_groups(lngs), ALU.mult))
                c.link(v.tensor_tensor(g16(Z), g16(Z), over_groups(lnbs), ALU.add))
                c.link(v.tensor_tensor(Z2[:, :], Z[:, :], Z[:, :], ALU.mult))
                c.link(v.tensor_scalar(Z2[:, :], Z2[:, :], 0.044715 * GELU_2C, GELU_2C, ALU.mult, ALU.add))
                c.link(v.tensor_tensor(Z3[:, :], Z2[:, :], Z[:, :], ALU.mult))
                c.link(v.tensor_scalar(Z3[:, :], Z3[:, :], 40.0, None, ALU.min))
                v.sem_inc(gelu_arg_ready, 1)

            def gelu(c, i):
                dve.wait_ge(small_act, i * SMALL_ACT + 5)
                c.link(v.tensor_scalar(Z3[:, :], Z3[:, :], -1.0, 1.0, ALU.mult, ALU.add))
                c.link(v.tensor_tensor(Z[:, :], Z[:, :], Z3[:, :], ALU.mult))
                v.sem_inc(hidden_ready, 1)

            def weigh_half(c, j, b, g):
                if g == 0:
                    dve.wait_ge(points_ready, j + 1)
                dve.wait_ge(patches_gathered[g % 3], gathered(j, g))
                c.done(weigh(v, b, g, 1))

            def sample(c, j, g):
                n = g % 3
                c.wait()
                dve.wait_ge(patches_weighed, j * GROUPS + g + 1)
                c.link(v.tensor_tensor(G[:, n, :, 0:2 * C], G[:, n, :, 0:2 * C], G[:, n, :, 2 * C:4 * C], ALU.add))
                wait_if(dve, sampled_transposed, j * GROUPS + g - 1)
                c.link(v.tensor_tensor(S[:, g % 2, :].rearrange("p (k c) -> p k c", c=C), G[:, n, :, 0:C], G[:, n, :, C:2 * C], ALU.add))
                v.sem_inc(patches_used, 1)
                v.sem_inc(sampled_ready, 1)

            def scores(c, j, b, g):
                t, m, n = g // 2, g % 2, g % 2
                dve.wait_ge(keys_ready, j * GROUPS + g + 1)
                q = QO[:, b, t, 32 + C * m:32 + C * m + C].unsqueeze(1).broadcast_to([P, NH, C])
                c.link(v.tensor_tensor(PR[:, :].rearrange("p (k c) -> p k c", c=C), keyp[:, :, :], q, ALU.mult))
                v.sem_inc(keys_used, 1)
                c.link(v.tensor_reduce(sc[:, n, :], PR[:, :].rearrange("p (s d) -> p s d", d=DH), AX.X, ALU.add))
                c.link(v.tensor_reduce(mx[:, :], sc[:, n, :].rearrange("p (k h) -> p h k", h=NH), AX.X, ALU.max))
                s3 = sc[:, n, :].rearrange("p (k h) -> p k h", h=NH)
                c.link(v.tensor_tensor(s3, s3, mx[:, :].unsqueeze(1).broadcast_to([P, NH, NH]), ALU.subtract))
                v.sem_inc(scores_ready, 1)

            def attend(c, j, g):
                n = g % 2
                dve.wait_ge(probs_ready, j * GROUPS + g + 1)
                dve.wait_ge(values_ready, j * GROUPS + g + 1)
                e3 = ex[:, n, :].rearrange("p (k h) -> p k h", h=NH)
                c.done(v.tensor_reduce(den[:, :], e3.rearrange("p k h -> p h k"), AX.X, ALU.add))
                c.link(v.tensor_tensor(PV[:, :].rearrange("p (k h d) -> p k h d", h=NH, d=DH),
                                       valp[:, :, :].rearrange("p k (h d) -> p k h d", d=DH),
                                       e3.unsqueeze(3).broadcast_to([P, NH, NH, DH]), ALU.mult))
                c.done(v.reciprocal(rden[:, :], den[:, :]))
                c.link(v.tensor_reduce(o8[:, :], PV[:, :].rearrange("p (k c) -> p c k", c=C), AX.X, ALU.add))
                if g == 0:
                    wait_if(dve, done["pe"], (j - 1) * len(STEPS["pe"]) + 2 if not (isinstance(j, int) and j == 0) else 0)
                c.link(v.tensor_tensor(HO[:, g, :].rearrange("p (h d) -> p h d", d=DH), o8[:, :].rearrange("p (h d) -> p h d", d=DH),
                                       rden[:, :].unsqueeze(2).broadcast_to([P, NH, DH]), ALU.mult))
                v.sem_inc(attended, 1)

            def tower(t):
                sg = Signals("dve", dve, done, t)
                c = Steps(dve, dve_t, T_DVE, t)

                def norm(tag, dst, gain=None, bias=None):
                    yield
                    if tag == "in":
                        wait_if(dve, out_stored, t * 32)
                    for h in range(2):
                        sg.wait("act", f"{tag}.rstd{h}")
                        if gain is None:
                            ins = v.tensor_tensor(half(dst, h), U[0][:, h, :], half(R, h), ALU.mult)
                        else:
                            ins = v.scalar_tensor_tensor(half(dst, h), U[0][:, h, :], gain, half(R, h), ALU.mult, ALU.mult)
                        sg.mark(ins, f"{tag}.norm{h}")
                        if bias is not None:
                            sg.wait("dve", f"{tag}.norm{h}")
                            sg.mark(v.tensor_scalar(half(dst, h), half(dst, h), bias, None, ALU.add), f"{tag}.shift{h}")
                    yield

                yield
                yield from norm("in", XT)
                for l in range(LAYERS):
                    yield from norm(f"a{l}", HN, cols[:, 0, l:l + 1], cols[:, 1, l:l + 1])
                    for h in range(2):
                        sg.wait("pe", f"{l}.k{h}")
                        c.done(v.tensor_reduce(kmax[:, h:h + 1], U[1][:, h, :], AX.X, ALU.max))
                    c.wait()
                    c.link(v.tensor_reduce(kmax[:, 2:3], kmax[:, 0:2], AX.X, ALU.max))
                    sg.mark(v.tensor_scalar(kmax[:, 3:4], kmax[:, 2:3], -QK_SCALE, None, ALU.mult), f"{l}.k_max")
                    for h in range(2):
                        sg.wait("pe", f"{l}.q{h}")
                        qm = qmax[:, C * h:C * h + C]
                        u = U[0][:, h, :].rearrange("p (g d) -> p g d", d=DH)
                        c.link(v.tensor_reduce(qm, u, AX.X, ALU.max))
                        sg.mark(v.tensor_tensor(flat(tiles(QE, h)).rearrange("p (g d) -> p g d", d=DH), u,
                                                qm.unsqueeze(2).broadcast_to([P, C, DH]), ALU.subtract), f"{l}.q_shifted{h}")
                    yield
                    for h in range(2):
                        sg.wait("act", f"{l}.q_exp{h}")
                        qm = qmax[:, C * h:C * h + C]
                        q = flat(tiles(QE, h)).rearrange("p (g d) -> p g d", d=DH)
                        c.link(v.tensor_reduce(qm, q, AX.X, ALU.add))
                        c.link(v.reciprocal(qm, qm))
                        sg.mark(v.tensor_tensor(q, q, qm.unsqueeze(2).broadcast_to([P, C, DH]), ALU.mult), f"{l}.q_ready{h}")
                    yield
                    sg.wait("pe", f"{l}.context")
                    sg.mark(v.tensor_tensor(CT[:, :], U[0][:, 0, 0:P], hmask[:, :], ALU.mult), f"{l}.context_ready")
                    yield
                    c.link(v.tensor_tensor(kden[:, 2:3], kden[:, 0:1], kden[:, 1:2], ALU.add))
                    c.link(v.reciprocal(kden[:, 3:4], kden[:, 2:3]))
                    sg.wait("pe", f"{l}.out_weights")
                    sg.mark(v.tensor_scalar(MM[:, :], U[0][:, 1, 0:P], kden[:, 3:4], None, ALU.mult), f"{l}.out_weights_ready")
                    yield
                    for h in range(2):
                        sg.wait("pe", f"{l}.out{h}")
                        sg.mark(v.scalar_tensor_tensor(half(XT, h), U[1][:, h, :], cols[:, 2, l:l + 1], half(XT, h), ALU.add, ALU.add), f"{l}.added{h}")
                    yield
                    yield from norm(f"f{l}", HN)
                    if l == LAYERS - 1:
                        for h in range(2):
                            sg.mark(v.tensor_tensor(half(HH, h), half(HH, h), half(XT, h), ALU.add), f"skipped_over{h}")
                    yield
                    yield
                    for h in range(2):
                        sg.wait("pe", f"{l}.down{h}")
                        if l < LAYERS - 1:
                            sg.mark(v.scalar_tensor_tensor(half(XT, h), U[0][:, h, :], cols[:, 5, l:l + 1], half(XT, h), ALU.add, ALU.add), f"{l}.ff_added{h}")
                        else:
                            sg.wait("dve", f"skipped_over{h}")
                            sg.mark(v.scalar_tensor_tensor(half(HH, h), U[0][:, h, :], cols[:, 5, l:l + 1], half(HH, h), ALU.add, ALU.add), f"residual{h}")
                    yield
                yield from norm("m", HN)
                yield
                g6 = lambda t: t[:, :].rearrange("p (g e) -> p g e", e=EXP)
                bc = lambda t: t.unsqueeze(2).broadcast_to([P, GROUPS, EXP])
                row = lambda t: t[:, :].unsqueeze(1).broadcast_to([P, GROUPS, EXP])
                s16 = lambda n: t16[:, n, :]
                sg.wait("pe", "logits")
                c.link(v.tensor_tensor(g6(LG), U[0][:, 0, 0:GROUPS * EXP].rearrange("p (g e) -> p g e", e=EXP), row(rb2), ALU.add))
                c.link(v.tensor_reduce(s16(0), g6(LG), AX.X, ALU.max))
                sg.mark(v.tensor_tensor(g6(LG), g6(LG), bc(s16(0)), ALU.subtract), "logits_shifted")
                yield
                sg.wait("act", "expert_exp")
                c.link(v.tensor_reduce(s16(0), g6(LG), AX.X, ALU.add))
                c.link(v.reciprocal(s16(0), s16(0)))
                c.link(v.tensor_tensor(g6(LG), g6(LG), bc(s16(0)), ALU.mult))
                for k, (src, sel) in enumerate(((LG, S1), (L2, L3))):
                    if k == 1:
                        yield
                        c.link(v.scalar_tensor_tensor(L2[:, :], S1[:, :], -2.0, LG[:, :], ALU.mult, ALU.add))
                    c.link(v.tensor_reduce(s16(1 + k), g6(src), AX.X, ALU.max))
                    c.link(v.tensor_tensor(g6(sel), g6(src), bc(s16(1 + k)), ALU.is_equal))
                    c.link(v.tensor_tensor(g6(sel), g6(sel), row(rank), ALU.mult))
                    c.link(v.tensor_reduce(s16(5), g6(sel), AX.X, ALU.max))
                    c.link(v.tensor_tensor(g6(sel), g6(sel), bc(s16(5)), ALU.is_equal))
                sg.mark(v.tensor_tensor(s16(3), s16(2), s16(1), ALU.subtract), "top_ready")
                yield
                sg.wait("act", "second_exp")
                c.link(v.tensor_scalar(s16(6), s16(4), 1.0, None, ALU.add))
                c.link(v.reciprocal(s16(6), s16(6)))
                c.link(v.tensor_tensor(s16(7), s16(4), s16(6), ALU.mult))
                c.link(v.tensor_tensor(g6(S1), g6(S1), bc(s16(6)), ALU.mult))
                c.link(v.tensor_tensor(g6(L3), g6(L3), bc(s16(7)), ALU.mult))
                c.link(v.tensor_tensor(L3[:, :], L3[:, :], S1[:, :], ALU.add))
                tile12 = lambda t: t.rearrange("p (t n) -> p t n", n=2 * EXP)
                c.link(v.tensor_copy(part16[:, 0, :], L3[:, :]))
                c.done(v.tensor_copy(LS[:, :, 0, :], tile12(part16[:, 0, :])))
                c.link(v.tensor_tensor(L2[:, :], L3[:, :], part16[:, 0, :], ALU.subtract))
                c.link(v.tensor_copy(part16[:, 1, :], L2[:, :]))
                c.done(v.tensor_copy(LS[:, :, 1, :], tile12(part16[:, 1, :])))
                c.link(v.tensor_tensor(LS[:, :, 2, :], tile12(L2[:, :]), tile12(part16[:, 1, :]), ALU.subtract))
                v.sem_inc(done["dve"], 1)
                sg.skip("weights_ready")
                yield
                yield

                def weighted(e, u):
                    for h in range(2):
                        sg.wait("act", f"e{e}.second_relu{h}")
                        sg.wait("pe", f"e{e}.weight{h}")
                        o = half(BIG[:, e, :], h)
                        sg.mark(v.tensor_tensor(o, o, U[u][:, h, :], ALU.mult), f"e{e}.weighted{h}")

                yield
                for e in range(2, EXP):
                    yield
                    weighted(e - 2, 0)
                    yield
                weighted(EXP - 2, 1)
                weighted(EXP - 1, 0)
                yield
                sg.close()
                c.close()
                yield

            def body(i, b, j, t):
                ca = None if i is None else Steps(dve, dve_a, A_DVE, i)
                cb = None if j is None else Steps(dve, dve_b, B_DVE, j)

                def stages(g, micro, after):
                    for part in PARTS_DVE[kind(g)].get((micro, after), ()):
                        n = tile_of(g - int(part[-1]))
                        if j is None or n is None:
                            continue
                        if part == "weigh0":
                            weigh_half(cb, j, 1 - b, n)
                        elif part == "sample0":
                            sample(cb, j, n)
                        elif part[:-1] == "attend":
                            attend(cb, j, n)
                        else:
                            scores(cb, j, 1 - b, n)
                    if i is not None:
                        if (g, micro, after) == (11, 3, 1):
                            hidden_norm(ca, i, b)
                        if (g, micro, after) == (13, 0, 1):
                            gelu_argument(ca, i)
                        if (g, micro, after) == (13, 3, 1):
                            gelu(ca, i)
                slots(stages, None if t is None else tower(t))
                if ca:
                    ca.close()
                if cb:
                    cb.close()
            run(dve, body)


def kernel(**inputs):
    import numpy as _np
    import concourse.bacc as _bacc
    from concourse import mybir as _mybir
    from concourse.bass_utils import run_bass_kernel_spmd as _run

    nb = inputs["x"].shape[0]
    lin = _np.linspace(-1.0, 1.0, GRID, dtype=_np.float32)
    px = (lin + _np.float32(1)) * _np.float32(0.5) * _np.float32(HW - 1)
    tok = _np.arange(NQ)
    xy = _np.stack([px[tok % GRID], px[tok // GRID]], -1).reshape(TILES, P, 2).transpose(1, 0, 2)
    left = _np.minimum(_np.floor(px), HW - 2)
    same = lambda n: _np.equal.outer(_np.arange(P) // n, _np.arange(P) // n).astype(_np.float32)
    spread = _np.zeros((3, 2 * EXP, EXP, P), _np.float32)
    for m in range(2):
        for e in range(EXP):
            spread[:, EXP * m + e, e, C * m:C * m + C] = 1
    constants = {
        "c_ident": _np.eye(P, dtype=_np.float32),
        "c_ref": _np.broadcast_to(xy[:, :, None, None, :], (P, TILES, 2, NH, 2)).reshape(P, 256),
        "c_wy": _np.broadcast_to((px - left)[None], (P, GRID)),
        "c_base": _np.broadcast_to(_np.array([0, (HW - 1) * HW], _np.float32)[None, None, :, None], (P, TILES, 2, NH)).reshape(P, 128),
        "c_center": _np.eye(P, dtype=_np.float32) - same(C) / C,
        "c_mean": same(C) / C,
        "c_hmask": same(DH),
        "c_rank": _np.broadcast_to(_np.arange(8, 8 - EXP, -1, dtype=_np.float32)[None], (P, EXP)),
        "c_spread": spread.reshape(SPLIT, EXP, P),
    }
    skip = ["L0_tok_W_q", "L0_tok_W_k", "L0_tok_W_v", "L0_ffn_expert_b1", "L0_ffn_expert_b2", "L0_attn_b1"]
    skip += [f"L0_attn_{n}" for n in ("ln1_g", "ln1_b", "bo", "ln2_g", "ln2_b", "b2")]
    arrays = {k: _np.asarray(v) for k, v in inputs.items() if k not in skip}
    arrays |= {"wqT": _np.asarray(inputs["L0_tok_W_q"]).T, "wkT": _np.asarray(inputs["L0_tok_W_k"]).T, "wvT": _np.asarray(inputs["L0_tok_W_v"]).T}
    T = lambda name: _np.asarray(inputs[name]).T
    names = ("ln1_g", "ln1_b", "bo", "ln2_g", "ln2_b", "b2")
    arrays["columns"] = _np.stack([T(f"L0_attn_{n}") for n in names], 1)
    arrays |= {"eb1T": T("L0_ffn_expert_b1"), "eb2T": T("L0_ffn_expert_b2")}
    arrays["b1T"] = _np.asarray(inputs["L0_attn_b1"]).reshape(LAYERS, 2, P).transpose(2, 0, 1)
    arrays |= {k: v.astype(_np.float32) for k, v in constants.items()}
    arrays = {k: _np.ascontiguousarray(v) for k, v in arrays.items()}
    nc = _bacc.Bacc("TRN2", target_bir_lowering=False, num_devices=1)
    a = {k: nc.dram_tensor(f"in_{k}", v.shape, _mybir.dt.from_np(v.dtype), kind="ExternalInput").ap() for k, v in arrays.items()}
    out = nc.dram_tensor("out_0", (nb, NQ, C), F32, kind="ExternalOutput").ap()
    program(nc, nb // 2, a["x"], out, a)
    r = _run(nc, [{f"in_{k}": v for k, v in arrays.items()}], core_ids=[0])
    return r.results[0]["out_0"]
```
